# Optimizing a Trainium2 kernel written in Bass

```python
import numpy as np
import jax
import jax.numpy as jnp

def _softmax(x, axis=-1):
    return jax.nn.softmax(x, axis=axis)

def _gelu(x):
    return jax.nn.gelu(x, approximate=True)

def _silu(x):
    return jax.nn.silu(x)

def _sigmoid(x):
    return jax.nn.sigmoid(x)

def _layernorm(x, axis=-1, eps=1e-05):
    m = jnp.mean(x, axis=axis, keepdims=True)
    v = jnp.var(x, axis=axis, keepdims=True)
    return (x - m) / jnp.sqrt(v + eps)

def _scatter_add(tgt, idx, src, axis=0):
    return tgt.at[idx].add(src)

def _segment_sum(src, seg, n):
    return jax.ops.segment_sum(src, seg, n)
kernel_name = 'mk_gnn_preln_d2_gnn_r8_7c408c'

def setup_inputs(seed: int=0):
    np.random.seed(seed)
    _w = jnp.asarray

    def _rec_inputs():
        import jax
        import jax.numpy as jnp
        _gk = jax.random.key(seed)
        x = -0.0003713 + 1 * jax.random.normal(jax.random.fold_in(_gk, 1), (6250, 256), jnp.float32)
        src = jax.random.randint(jax.random.fold_in(_gk, 2), (200000,), 0, 6250, jnp.int32)
        dst = jnp.minimum((6250 * jax.random.uniform(jax.random.fold_in(_gk, 3), (200000,)) ** 2.0).astype(jnp.int32), 49999)
        _o = jnp.argsort(dst, stable=True)
        src = src[_o]
        dst = dst[_o]
        edge_attr_64 = -9.77346e-05 + 0.999888 * jax.random.normal(jax.random.fold_in(_gk, 12), (200000, 64), jnp.float32)
        edge_type_16 = jax.random.randint(jax.random.fold_in(_gk, 13), (200000,), 0, 16, jnp.int32)
        edge_weight1 = jax.random.uniform(jax.random.fold_in(_gk, 14), (200000, 1), jnp.float32, 0.0, 1)
        return (x, src, dst, edge_attr_64, edge_type_16, edge_weight1)
    x, src, dst, edge_attr_64, edge_type_16, edge_weight1 = _rec_inputs()

    def _L0_gnn_setup():
        import jax, jax.numpy as jnp
        import numpy as np
        N, E, D, H, FE = (6250, 100000, 256, 8, 64)
        HD = D // H
        key = jax.random.key(seed)
        ks = jax.random.split(key, 14)
        sD = 1.0 / np.sqrt(D)
        sF = 1.0 / np.sqrt(FE)
        return {'h': jax.random.normal(ks[0], (N, D), jnp.float32), 'efeat': jax.random.normal(ks[1], (E, FE), jnp.float32), 'src': jax.random.randint(ks[2], (E,), 0, N), 'dst': jax.random.randint(ks[3], (E,), 0, N), 'Wq': jax.random.normal(ks[4], (D, D), jnp.float32) * sD, 'Wk': jax.random.normal(ks[5], (D, D), jnp.float32) * sD, 'Wv': jax.random.normal(ks[6], (D, D), jnp.float32) * sD, 'W1': jax.random.normal(ks[7], (FE, D), jnp.float32) * sF, 'b1': jnp.zeros((D,), jnp.float32), 'W2': jax.random.normal(ks[8], (D, H), jnp.float32) * sD, 'b2': jnp.zeros((H,), jnp.float32), 'Wo': jax.random.normal(ks[9], (D, D), jnp.float32) * sD, 'bo': jnp.zeros((D,), jnp.float32)}
    _L0_gnn_all = _L0_gnn_setup()
    _L0_gnn_in = {k: v for k, v in _L0_gnn_all.items() if k in ('Wq', 'Wk', 'Wv', 'W1', 'b1', 'W2', 'b2', 'Wo', 'bo')}
    del _L0_gnn_all

    def _L1_gnn_setup():
        import jax, jax.numpy as jnp
        import numpy as np
        N_NODES = 6250
        N_EDGES = 100000
        NUM_RELS = 16
        FEAT = 256
        OUT = 256
        key = jax.random.key(seed)
        ks = jax.random.split(key, 7)
        h = jax.random.normal(ks[0], (N_NODES, FEAT), dtype=jnp.float32)
        norm = jax.random.uniform(ks[1], (N_EDGES, 1), dtype=jnp.float32)
        weight = jax.random.normal(ks[2], (NUM_RELS, FEAT, OUT), dtype=jnp.float32) * 0.05
        gate_weight = jax.random.normal(ks[3], (NUM_RELS, FEAT, 1), dtype=jnp.float32) * 0.05
        src = jax.random.randint(ks[4], (N_EDGES,), 0, N_NODES)
        dst = jax.random.randint(ks[5], (N_EDGES,), 0, N_NODES)
        rel_type = jax.random.randint(ks[6], (N_EDGES,), 0, NUM_RELS)
        return {'h': h, 'norm': norm, 'weight': weight, 'gate_weight': gate_weight, 'src': src, 'dst': dst, 'rel_type': rel_type}
    _L1_gnn_all = _L1_gnn_setup()
    _L1_gnn_in = {k: v for k, v in _L1_gnn_all.items() if k in ('weight', 'gate_weight')}
    del _L1_gnn_all
    return {'x': x, 'src': src, 'dst': dst, 'edge_attr_64': edge_attr_64, 'edge_type_16': edge_type_16, 'edge_weight1': edge_weight1, 'L0_gnn_Wq': _L0_gnn_in['Wq'], 'L0_gnn_Wk': _L0_gnn_in['Wk'], 'L0_gnn_Wv': _L0_gnn_in['Wv'], 'L0_gnn_W1': _L0_gnn_in['W1'], 'L0_gnn_b1': _L0_gnn_in['b1'], 'L0_gnn_W2': _L0_gnn_in['W2'], 'L0_gnn_b2': _L0_gnn_in['b2'], 'L0_gnn_Wo': _L0_gnn_in['Wo'], 'L0_gnn_bo': _L0_gnn_in['bo'], 'L1_gnn_weight': _L1_gnn_in['weight'], 'L1_gnn_gate_weight': _L1_gnn_in['gate_weight']}

def reference(x, src, dst, edge_attr_64, edge_type_16, edge_weight1, L0_gnn_Wq, L0_gnn_Wk, L0_gnn_Wv, L0_gnn_W1, L0_gnn_b1, L0_gnn_W2, L0_gnn_b2, L0_gnn_Wo, L0_gnn_bo, L1_gnn_weight, L1_gnn_gate_weight):
    import jax
    import jax.numpy as jnp

    def _L0_gnn_ref(h, efeat, src, dst, Wq, Wk, Wv, W1, b1, W2, b2, Wo, bo):
        import jax, jax.numpy as jnp
        import numpy as np
        N, E, D, H, FE = (6250, 100000, 256, 8, 64)
        HD = D // H
        n = h.shape[0]
        Q = (h @ Wq).reshape(n, H, HD)
        K = (h @ Wk).reshape(n, H, HD)
        V = (h @ Wv).reshape(n, H, HD)
        score = jnp.einsum('ehd,ehd->eh', Q[dst], K[src]) / np.sqrt(HD)
        score = score + jax.nn.relu(efeat @ W1 + b1) @ W2 + b2
        m = jax.ops.segment_max(score, dst, num_segments=n)
        ex = jnp.exp(score - m[dst])
        denom = jax.ops.segment_sum(ex, dst, num_segments=n)
        alpha = ex / denom[dst]
        out = jax.ops.segment_sum(alpha[:, :, None] * V[src], dst, num_segments=n)
        out = out.reshape(n, D)
        return out @ Wo + bo

    def _L1_gnn_ref(h, norm, weight, gate_weight, src, dst, rel_type):
        import jax, jax.numpy as jnp
        import numpy as np
        N_NODES = 6250
        N_EDGES = 100000
        NUM_RELS = 16
        FEAT = 256
        OUT = 256
        n_nodes = h.shape[0]
        all_msg = jnp.einsum('nf,rfo->rno', h, weight)
        msg = all_msg[rel_type, src] * norm
        all_gate = jnp.einsum('nf,rf->rn', h, gate_weight[..., 0])
        gate = jax.nn.sigmoid(all_gate[rel_type, src])[:, None]
        msg = msg * gate
        agg = jax.ops.segment_sum(msg, dst, num_segments=n_nodes)
        return jax.nn.relu(agg)
    h = jnp.maximum(_layernorm(x, axis=-1), 0.0)
    x = x + _L0_gnn_ref(h, edge_attr_64, src, dst, L0_gnn_Wq, L0_gnn_Wk, L0_gnn_Wv, L0_gnn_W1, L0_gnn_b1, L0_gnn_W2, L0_gnn_b2, L0_gnn_Wo, L0_gnn_bo)
    h = jnp.maximum(_layernorm(x, axis=-1), 0.0)
    x = x + _L1_gnn_ref(h, edge_weight1, L1_gnn_weight, L1_gnn_gate_weight, src, dst, edge_type_16)
    return x

_drawn_inputs = setup_inputs


def setup_inputs(seed=0):
    import zlib

    import numpy as np

    out = dict(_drawn_inputs(seed))
    spreads = {'L0_gnn_b1': (0.0, 0.8), 'L0_gnn_b2': (0.0, 0.8), 'L0_gnn_bo': (0.0, 0.1)}
    factors = {}
    for name, (base, spread) in spreads.items():
        noise = np.random.default_rng([zlib.crc32(name.encode()), seed]).standard_normal(out[name].shape)
        drawn = base * np.exp(spread * noise) if base else spread * noise
        out[name] = jnp.asarray(drawn.astype(out[name].dtype))
    for name, factor in factors.items():
        out[name] = (out[name] * factor).astype(out[name].dtype)
    return out
```

```python
from contextlib import ExitStack

import concourse.bass as bass
from concourse import mybir

F32 = mybir.dt.float32
BF16 = mybir.dt.bfloat16
I32 = mybir.dt.int32
ALU = mybir.AluOpType
ACT = mybir.ActivationFunctionType
AX = mybir.AxisListType

P = 128
N, E, D, H, FE, RELS = 6250, 200000, 256, 8, 64, 16
HD = D // H
HD1 = HD + 1
BLOCKS = -(-N // P)
NPAD = BLOCKS * P
LAST_ROWS = N - (BLOCKS - 1) * P
GE = 2 * P
ROWS = 16
ROW_GROUPS = 49
GROUPS = ROWS * ROW_GROUPS
FULL_GROUPS = E // GE
TAIL = E - FULL_GROUPS * GE
EPAD = GROUPS * GE
ROW_E = ROW_GROUPS * GE
COLS = 2 * GROUPS
U = 4
STEPS = GROUPS + BLOCKS - 1
ITERS = STEPS // U
CHUNKS = GROUPS // U
TCOLS = COLS + 2
TSTEPS = STEPS + U
PADNODE = NPAD - 1
BIG = 1.0e30
EPS = 1.0e-5
HB = P * 7

assert STEPS % U == 0 and GROUPS % U == 0 and PADNODE >= N


def wait(eng, sem, value):
    if isinstance(value, int) and value <= 0:
        return
    eng.wait_ge(sem, value)


def hold(eng, sem, value, passed):
    eng.wait_ge(sem, value)
    eng.sem_inc(passed, 1)


def build(nc, x, src, dst, edge_attr, edge_type, edge_weight, wq, wk, wv, w1, b1, w2, b2, wo, bo,
          rel_w, gate_w, out):
    newseg_d = nc.dram_tensor("newseg_d", [EPAD + 1], F32, kind="Internal").ap()
    k_d = nc.dram_tensor("k_d", [NPAD, D], F32, kind="Internal").ap()
    v_d = nc.dram_tensor("v_d", [NPAD, H * HD1], F32, kind="Internal").ap()
    msg_d = nc.dram_tensor("msg_d", [RELS * NPAD, D], F32, kind="Internal").ap()

    with ExitStack() as ctx:
        def sb(name, shape, dt=F32):
            return ctx.enter_context(nc.sbuf_tensor(name, shape, dt))

        t = {}
        t["dst"] = sb("t_dst", [P, TCOLS])
        t["src"] = sb("t_src", [P, TCOLS], I32)
        t["rel"] = sb("t_rel", [P, TCOLS], I32)
        t["norm"] = sb("t_norm", [P, TCOLS])
        t["nbase"] = sb("t_nbase", [P, TSTEPS])
        t["block"] = sb("t_block", [1, TSTEPS], I32)
        t["group"] = sb("t_group", [1, TSTEPS], I32)
        t["iota"] = sb("t_iota", [P, P])
        t["ident"] = sb("t_ident", [P, P])
        t["identb"] = sb("t_identb", [P, P], BF16)
        t["eps"] = sb("t_eps", [P, 1])
        t["chain"] = sb("t_chain", [1, 2, H, ROWS])
        edge_tables(nc, t, src, dst, edge_type, edge_weight, newseg_d)
        with ExitStack() as sums_ctx:
            with nc.sbuf_tensor("scores", [P, COLS, H], F32) as scores:
                with nc.sbuf_tensor("q3", [P, BLOCKS, 3, D], BF16) as q3:
                    node_projections(nc, t, q3, x, wq, wk, wv, k_d, v_d)
                    edge_scores(nc, t, q3, scores, edge_attr, w1, b1, w2, b2, k_d)
                softmax_numerators(nc, t, scores, newseg_d)
                att = sums_ctx.enter_context(nc.sbuf_tensor("att", [P, BLOCKS, H, HD1], F32, side="right"))
                weighted_sums(nc, t, scores, att, v_d)
            with nc.sbuf_tensor("x1", [P, BLOCKS, D], F32) as x1:
                messages(nc, t, att, x1, x, wo, bo, rel_w, gate_w, msg_d)
                message_sums(nc, t, x1, msg_d, out)


def phase(nc):
    ctx = ExitStack()
    sems = []

    def clear():
        nc.clear_and_free_semaphores(sems)
        nc.all_engine_barrier()

    ctx.callback(clear)

    def sb(name, shape, dt=F32):
        return ctx.enter_context(nc.sbuf_tensor(name, shape, dt))

    def ps(name, shape, dt=F32):
        return ctx.enter_context(nc.psum_tensor(name, shape, dt))

    def sem(name, n=None):
        if n is None:
            sems.append(nc.alloc_semaphore(name))
            return sems[-1]
        return [sem(f"{name}{i}") for i in range(n)]

    return ctx, sb, ps, sem


def edge_tables(nc, t, src, dst, edge_type, edge_weight, newseg_d):
    ctx, sb, ps, sem = phase(nc)
    J = -(-GROUPS // P)
    FULL_J = FULL_GROUPS // P
    REST = FULL_GROUPS - FULL_J * P
    PADROWS = GROUPS - FULL_J * P
    with ctx:
        dst_i = sb("dst_i", [P, J, GE], I32)
        src_i = sb("src_i", [P, J, GE], I32)
        typ_i = sb("typ_i", [P, J, GE], I32)
        nrm_f = sb("nrm_f", [P, J, GE])
        dst_f = sb("dst_f", [P, J, GE])
        src_f = sb("src_f", [P, J, GE])
        rel_f = sb("rel_f", [P, J, GE])
        before = sb("before", [P, J], I32)
        beforef = sb("beforef", [P, J])
        newseg = sb("newseg", [P, J, GE])
        last_blk = sb("last_blk", [P, J], I32)
        iota_g = sb("iota_g", [P, J], I32)
        iota_gf = sb("iota_gf", [P, J])
        key = sb("key", [P, J])
        iota_i = sb("iota_i", [P, TSTEPS], I32)
        iota_s = sb("iota_s", [P, TSTEPS])
        step128 = sb("step128", [P, TSTEPS])
        passed = sb("passed", [P, J, TSTEPS], BF16)
        ones = sb("ones", [P, P], BF16)
        ends = sb("ends", [1, 2, ROWS + 1], I32)
        endsf = sb("endsf", [1, 2, ROWS + 1])
        tail = sb("tail", [1, 1])
        blkf = sb("blkf", [1, TSTEPS])
        grpf = sb("grpf", [1, TSTEPS])
        HS = TSTEPS // 2
        turned = [ps(f"turned{i}", [P, 512]) for i in range(4)]
        count = [ps(f"count{i}", [P, 512]) for i in range(2)]
        pads_set = sem("pads_set")
        consts = sem("consts")
        loaded = sem("loaded")
        cast = sem("cast")
        link = sem("link")
        turned_ready = sem("turned_ready")
        turned_taken = sem("turned_taken")
        passed_ready = sem("passed_ready")
        count_ready = sem("count_ready")
        newseg_ready = sem("newseg_ready")
        stored = sem("stored")
        LOADS = 4 * 3 + 4 + 2 + 2
        block = ctx.enter_context(nc.Block())
        flat_w = edge_weight.rearrange("e a -> (e a)")

        @block.sync
        def _(sp):
            sp.wait_ge(pads_set, 6)
            for flat, to in ((dst, dst_i), (src, src_i), (edge_type, typ_i), (flat_w, nrm_f)):
                a, b = FULL_J * P * GE, FULL_GROUPS * GE
                sp.dma_start(to[:, 0:FULL_J, :], flat[0:a].rearrange("(j p e) -> p j e", p=P, e=GE)).then_inc(loaded, 16)
                sp.dma_start(to[0:REST, FULL_J, :], flat[a:b].rearrange("(p e) -> p e", e=GE)).then_inc(loaded, 16)
                sp.dma_start(to[REST:REST + 1, FULL_J, 0:TAIL], flat[b:E].rearrange("(a e) -> a e", a=1)).then_inc(loaded, 16)
            last = dst[0:FULL_GROUPS * GE].rearrange("(g e) -> g e", e=GE)[:, GE - 1:GE]
            with nc.allow_non_contiguous_dma(reason="one number of each group"):
                sp.dma_start(before[1:P, 0:1], last[0:P - 1, :]).then_inc(loaded, 16)
                sp.dma_start(before[:, 1:FULL_J], last[P - 1:P * FULL_J - 1, :].rearrange("(j p) a -> p (j a)", p=P)).then_inc(loaded, 16)
                sp.dma_start(before[0:REST + 1, FULL_J:J], last[P * FULL_J - 1:FULL_GROUPS, :]).then_inc(loaded, 16)
                n = E // ROW_E
                sp.dma_start(ends[:, 0, 0:n], dst[0:n * ROW_E].rearrange("(a q e) -> a q e", a=1, e=ROW_E)[:, :, ROW_E - 1]).then_inc(loaded, 16)
                sp.dma_start(ends[:, 1, 0:n], dst[0:n * ROW_E].rearrange("(a q e) -> a q e", a=1, e=ROW_E)[:, :, 0]).then_inc(loaded, 16)
                sp.dma_start(ends[:, 1, n:n + 1], dst[n * ROW_E:n * ROW_E + 1].rearrange("(a q) -> a q", a=1)).then_inc(loaded, 16)
            sp.wait_ge(newseg_ready, 1)
            a = FULL_J * P * GE
            sp.dma_start(newseg_d[0:a].rearrange("(j p e) -> p j e", p=P, e=GE), newseg[:, 0:FULL_J, :]).then_inc(stored, 16)
            sp.dma_start(newseg_d[a:EPAD].rearrange("(p e) -> p e", e=GE), newseg[0:PADROWS, FULL_J, :]).then_inc(stored, 16)
            sp.dma_start(newseg_d[EPAD:EPAD + 1].rearrange("(a e) -> a e", a=1), tail[:, :]).then_inc(stored, 16)
            sp.wait_ge(stored, 48)

        @block.gpsimd
        def _(pool):
            pool.memset(dst_i[:, FULL_J, :], PADNODE).then_inc(pads_set, 1)
            pool.memset(src_i[:, FULL_J, :], 0).then_inc(pads_set, 1)
            pool.memset(typ_i[:, FULL_J, :], 0).then_inc(pads_set, 1)
            pool.memset(nrm_f[:, FULL_J, :], 0.0).then_inc(pads_set, 1)
            pool.memset(before[:, :], PADNODE).then_inc(pads_set, 1)
            pool.memset(ends[:, :, :], PADNODE).then_inc(pads_set, 1)
            pool.memset(t["ident"][:, :], 0.0).then_inc(consts, 1)
            pool.memset(t["identb"][:, :], 0.0).then_inc(consts, 1)
            pool.memset(ones[:, :], 1.0).then_inc(consts, 1)
            pool.memset(t["eps"][:, :], EPS).then_inc(consts, 1)
            pool.memset(tail[:, :], -BIG).then_inc(consts, 1)
            pool.iota(iota_i[:, :], [[1, TSTEPS]], base=0, channel_multiplier=0).then_inc(consts, 1)
            pool.iota(iota_g[:, :], [[P, J]], base=0, channel_multiplier=1).then_inc(consts, 1)
            pool.memset(t["dst"][:, COLS:TCOLS], float(PADNODE)).then_inc(consts, 1)
            pool.memset(t["src"][:, COLS:TCOLS], 0).then_inc(consts, 1)
            pool.memset(t["rel"][:, COLS:TCOLS], 0).then_inc(consts, 1)
            pool.memset(t["norm"][:, COLS:TCOLS], 0.0).then_inc(consts, 1)
            pool.wait_ge(consts, 2)
            for m in (t["ident"], t["identb"]):
                pool.affine_select(out=m[:, :], in_=m[:, :], compare_op=ALU.not_equal, fill=1.0, base=0,
                                   pattern=[[-1, P]], channel_multiplier=1).then_inc(consts, 1)

        tables = ((dst_f, t["dst"]), (src_f, t["src"]), (rel_f, t["rel"]), (nrm_f, t["norm"]))
        jobs = [(f, to, j) for f, to in tables for j in range(J)]

        @block.tensor
        def _(pe):
            pe.wait_ge(consts, 13)
            pe.wait_ge(cast, 4)
            pe.wait_ge(loaded, 16 * (LOADS - 2))
            for n, (f, to, j) in enumerate(jobs):
                rows = P if j < FULL_J else PADROWS
                if n >= 4:
                    pe.wait_ge(turned_taken, n - 3)
                for k in range(2):
                    last = nc.tensor.transpose(turned[n % 4][:, k * P:k * P + rows], f[0:rows, j, k::2],
                                               t["ident"][0:rows, 0:rows])
                last.then_inc(turned_ready, 1)
            pe.wait_ge(passed_ready, J)
            for half in range(2):
                for j in range(J):
                    rows = P if j < FULL_J else PADROWS
                    last = nc.tensor.matmul(count[half][:, 0:HS], ones[0:rows, :], passed[0:rows, j, half * HS:half * HS + HS],
                                            start=(j == 0), stop=(j == J - 1))
            last.then_inc(count_ready, 1)

        @block.scalar
        def _(act):
            for n, (f, to, j) in enumerate(jobs):
                rows = P if j < FULL_J else PADROWS
                act.wait_ge(turned_ready, n + 1)
                view = to[:, 2 * P * j:2 * P * j + 2 * rows].rearrange("p (g k) -> p k g", k=2)
                nc.scalar.activation(view, turned[n % 4][:, 0:2 * P].rearrange("p (k g) -> p k g", k=2)[:, :, 0:rows],
                                     ACT.Copy).then_inc(turned_taken, 1)

        @block.vector
        def _(dve):
            n = [0]

            def done(ins):
                n[0] += 1
                ins.then_inc(link, 1)
                dve.wait_ge(link, n[0])

            dve.wait_ge(consts, 13)
            dve.wait_ge(loaded, 16 * (LOADS - 2))
            nc.vector.tensor_copy(t["iota"][:, :], iota_i[:, 0:P])
            nc.vector.tensor_copy(dst_f[:, :, :], dst_i[:, :, :]).then_inc(cast, 1)
            nc.vector.tensor_copy(src_f[:, :, :], src_i[:, :, :]).then_inc(cast, 1)
            nc.vector.tensor_copy(beforef[:, :], before[:, :])
            nc.vector.tensor_copy(iota_gf[:, :], iota_g[:, :])
            nc.vector.tensor_copy(endsf[:, :, :], ends[:, :, :])
            nc.vector.tensor_copy(iota_s[:, :], iota_i[:, :]).then_inc(cast, 1)
            done(nc.vector.tensor_scalar(last_blk[:, :], dst_i[:, :, GE - 1], 7, None, ALU.arith_shift_right))
            nc.vector.scalar_tensor_tensor(out=rel_f[:, :, :], in0=typ_i[:, :, :], scalar=float(NPAD), in1=src_f[:, :, :],
                                           op0=ALU.mult, op1=ALU.add).then_inc(cast, 1)
            done(nc.vector.tensor_tensor(key[:, :], last_blk[:, :], iota_gf[:, :], ALU.add))
            for j in range(J):
                rows = P if j < FULL_J else PADROWS
                nc.vector.tensor_scalar(passed[0:rows, j, :], iota_s[0:rows, :], key[0:rows, j:j + 1], None,
                                        ALU.is_gt).then_inc(passed_ready, 1)
            nc.vector.tensor_tensor(newseg[:, :, 1:GE], dst_f[:, :, 1:GE], dst_f[:, :, 0:GE - 1], ALU.is_equal)
            done(nc.vector.tensor_tensor(newseg[:, :, 0:1], dst_f[:, :, 0:1], beforef[:, :].unsqueeze(2), ALU.is_equal))
            nc.vector.tensor_scalar(newseg[:, :, :], newseg[:, :, :], -1.0, BIG, ALU.add, ALU.mult).then_inc(newseg_ready, 1)
            for way in range(2):
                c = t["chain"][:, way, 0, :]
                done(nc.vector.memset(c, 0.0))
                if way == 0:
                    done(nc.vector.tensor_tensor(c[:, 1:ROWS], endsf[:, 0, 1:ROWS], endsf[:, 0, 0:ROWS - 1], ALU.is_equal))
                else:
                    done(nc.vector.tensor_tensor(c[:, 0:ROWS - 1], endsf[:, 1, 0:ROWS - 1], endsf[:, 1, 1:ROWS], ALU.is_equal))
                done(nc.vector.tensor_scalar(c, c, -1.0, BIG, ALU.add, ALU.mult))
                for h in range(1, H):
                    nc.vector.tensor_copy(t["chain"][:, way, h, :], c)
            done(nc.vector.tensor_scalar(step128[:, :], iota_s[:, :], float(P), None, ALU.mult))
            dve.wait_ge(count_ready, 1)
            for half in range(2):
                a, b = half * HS, half * HS + HS
                nc.vector.tensor_copy(grpf[:, a:b], count[half][0:1, 0:HS])
                nc.vector.scalar_tensor_tensor(out=blkf[:, a:b], in0=count[half][0:1, 0:HS], scalar=-1.0, in1=iota_s[0:1, a:b],
                                               op0=ALU.mult, op1=ALU.add)
                done(nc.vector.scalar_tensor_tensor(out=t["nbase"][:, a:b], in0=count[half][:, 0:HS], scalar=-float(P),
                                                    in1=step128[:, a:b], op0=ALU.mult, op1=ALU.add))
            nc.vector.tensor_copy(t["block"][:, :], blkf[:, :])
            nc.vector.tensor_copy(t["group"][:, :], grpf[:, :])


def blocks_loop(eng, body, last=BLOCKS):
    body(0, 0, 0)
    pairs = (last - 1) // 2
    with eng.Fori(0, pairs) as i:
        body(2 * i + 1, 1, i)
        body(2 * i + 2, 0, i + 1)
    if last > 2 * pairs + 1:
        body(last - 1, 1, pairs)


def node_projections(nc, t, q3, x, wq, wk, wv, k_d, v_d):
    ctx, sb, ps, sem = phase(nc)
    with ctx:
        w = sb("w_qkv", [P, 2, 3 * D])
        xin = sb("xin", [P, 2, D])
        stats = sb("stats", [P, 2, 6])
        mv = sb("mv", [P, 2, 2])
        std = sb("std", [P, 2, 1])
        rstd = sb("rstd", [P, 2, 1])
        xn = sb("xn", [P, 2, D])
        hT = sb("hT", [P, 2, 2, P])
        qs = sb("qs", [P, 2, D])
        qr = sb("qr", [P, 2, D])
        ko = sb("ko", [P, 2, D])
        vo = sb("vo", [P, 2, H, HD1])
        turned = [ps(f"xT{i}", [P, 512]) for i in range(2)]
        qk = [ps(f"qk{i}", [P, 512]) for i in range(2)]
        vv = [ps(f"vv{i}", [P, 512]) for i in range(2)]
        dve_go = sem("dve_go")
        w_in = sem("w_in")
        ones_set = sem("ones_set")
        x_in = sem("x_in", 2)
        mv_ready = sem("mv_ready", 2)
        std_ready = sem("std_ready", 2)
        norm_link = sem("norm_link", 2)
        stat_link = sem("stat_link", 2)
        xn_ready = sem("xn_ready", 2)
        turned_ready = sem("xT_ready", 2)
        hT_ready = sem("hT_ready", 2)
        proj_ready = sem("proj_ready", 2)
        q_link = sem("q_link", 2)
        q_done = sem("q_done", 2)
        kv_ready = sem("kv_ready", 2)
        kv_stored = sem("kv_stored", 2)
        block = ctx.enter_context(nc.Block())

        @block.sync
        def _(sp):
            for i, m in enumerate((wq, wk, wv)):
                sp.dma_start(w[:, :, i * D:(i + 1) * D], m.rearrange("(c p) n -> p c n", p=P)).then_inc(w_in, 16)

            def load(b, s, n, rows=P):
                wait(sp, xn_ready[s], n)
                at = b * P
                sp.dma_start(xin[0:rows, s, :], x[bass.ds(at, rows), :]).then_inc(x_in[s], 16)

            blocks_loop(sp, load, BLOCKS - 1)
            load(BLOCKS - 1, 0, (BLOCKS - 1) // 2, LAST_ROWS)

        @block.gpsimd
        def _(pool):
            pool.memset(vo[:, :, :, HD:HD1], 1.0).then_inc(ones_set, 1)
            pool.wait_ge(ones_set, 1)

            def store(b, s, n):
                pool.wait_ge(kv_ready[s], n + 1)
                pool.dma_start(k_d[bass.ds(b * P, P), :], ko[:, s, :]).then_inc(kv_stored[s], 16)
                pool.dma_start(v_d[bass.ds(b * P, P), :], vo[:, s, :, :].rearrange("p h c -> p (h c)")).then_inc(kv_stored[s], 16)

            blocks_loop(pool, store)
            pool.wait_ge(kv_stored[0], 32 * (BLOCKS // 2 + 1))
            pool.wait_ge(kv_stored[1], 32 * (BLOCKS // 2))

        def skewed(eng, front, back):
            front(0, 0, 0)
            front(1, 1, 0)
            back(0, 0, 0)
            with eng.Fori(0, (BLOCKS - 3) // 2) as i:
                front(2 * i + 2, 0, i + 1)
                back(2 * i + 1, 1, i)
                front(2 * i + 3, 1, i + 1)
                back(2 * i + 2, 0, i + 1)
            n = (BLOCKS - 1) // 2
            front(BLOCKS - 1, 0, n)
            back(BLOCKS - 2, 1, n - 1)
            back(BLOCKS - 1, 0, n)

        @block.vector
        def _(dve):
            def front(b, s, n):
                hold(dve, x_in[s], 16 * (n + 1), dve_go)
                nc.vector.bn_stats(stats[:, s, :], xin[:, s, :]).then_inc(stat_link[s], 1)
                hold(dve, stat_link[s], n + 1, dve_go)
                nc.vector.bn_aggr(mv[:, s, :], stats[:, s, :]).then_inc(mv_ready[s], 1)
                dve.wait_ge(std_ready[s], n + 1)
                nc.vector.reciprocal(rstd[:, s, :], std[:, s, :]).then_inc(norm_link[s], 1)
                dve.wait_ge(norm_link[s], n + 1)
                nc.vector.tensor_scalar(xn[:, s, :], xin[:, s, :], mv[:, s, 0:1], rstd[:, s, :],
                                        ALU.subtract, ALU.mult).then_inc(xn_ready[s], 1)

            def back(b, s, n):
                dve.wait_ge(proj_ready[s], n + 1)
                q = qk[s][:, 0:D]
                scale = HD ** -0.5
                q0, q1, q2 = (q3[:, bass.ds(b, 1), i, :].rearrange("p a d -> p (a d)") for i in range(3))
                nc.vector.tensor_scalar(qs[:, s, :], q, scale, None, ALU.mult).then_inc(q_link[s], 1)
                dve.wait_ge(q_link[s], 5 * n + 1)
                nc.vector.tensor_copy(q0, qs[:, s, :]).then_inc(q_link[s], 1)
                dve.wait_ge(q_link[s], 5 * n + 2)
                nc.vector.tensor_tensor(qr[:, s, :], qs[:, s, :], q0, ALU.subtract).then_inc(q_link[s], 1)
                dve.wait_ge(q_link[s], 5 * n + 3)
                nc.vector.tensor_copy(q1, qr[:, s, :]).then_inc(q_link[s], 1)
                dve.wait_ge(q_link[s], 5 * n + 4)
                nc.vector.tensor_tensor(q2, qr[:, s, :], q1, ALU.subtract).then_inc(q_link[s], 1)

            skewed(dve, front, back)

        @block.scalar
        def _(act):
            def front(b, s, n):
                act.wait_ge(mv_ready[s], n + 1)
                nc.scalar.activation(std[:, s, :], mv[:, s, 1:2], ACT.Sqrt, bias=t["eps"][:, 0:1]).then_inc(std_ready[s], 1)
                act.wait_ge(turned_ready[s], n + 1)
                nc.scalar.activation(hT[:, s, :, :], turned[s][:, 0:2 * P].rearrange("p (c n) -> p c n", c=2),
                                     ACT.Relu).then_inc(hT_ready[s], 1)

            def back(b, s, n):
                act.wait_ge(proj_ready[s], n + 1)
                act.wait_ge(q_link[s], 5 * n + 1)
                wait(act, kv_stored[s], 32 * n)
                if isinstance(b, int) and b == 0:
                    act.wait_ge(ones_set, 1)
                nc.scalar.activation(ko[:, s, :], qk[s][:, D:2 * D], ACT.Copy)
                nc.scalar.activation(vo[:, s, :, 0:HD], vv[s][:, 0:D].rearrange("p (h c) -> p h c", h=H),
                                     ACT.Copy).then_inc(kv_ready[s], 1)

            skewed(act, front, back)

        @block.tensor
        def _(pe):
            pe.wait_ge(w_in, 48)

            def front(b, s, n):
                pe.wait_ge(xn_ready[s], n + 1)
                for c in range(2):
                    last = nc.tensor.transpose(turned[s][:, c * P:(c + 1) * P], xn[:, s, c * P:(c + 1) * P], t["ident"][:, :])
                last.then_inc(turned_ready[s], 1)

            def back(b, s, n):
                pe.wait_ge(hT_ready[s], n + 1)
                wait(pe, q_link[s], 5 * n)
                wait(pe, kv_ready[s], n)
                for c in range(2):
                    nc.tensor.matmul(qk[s][:, :], hT[:, s, c, :], w[:, c, 0:2 * D], start=(c == 0), stop=(c == 1))
                for c in range(2):
                    last = nc.tensor.matmul(vv[s][:, 0:D], hT[:, s, c, :], w[:, c, 2 * D:3 * D], start=(c == 0), stop=(c == 1))
                last.then_inc(proj_ready[s], 1)

            skewed(pe, front, back)


def block_of(eng, t, s):
    return eng.value_load(t["block"][0:1, bass.ds(s, 1)], min_val=0, max_val=BLOCKS - 1)


def group_of(eng, t, s, past=0):
    return eng.value_load(t["group"][0:1, bass.ds(s, 1)], min_val=0, max_val=GROUPS - 1 + past)


def edge_scores(nc, t, q3, scores, edge_attr, w1, b1, w2, b2, k_d):
    ctx, sb, ps, sem = phase(nc)
    with ctx:
        w1s = sb("w1s", [P, D])
        w2s = sb("w2s", [P, 2, H])
        b1s = sb("b1s", [P, 2])
        b2s = sb("b2s", [P, H])
        raw = sb("ef_raw", [P, U, P])
        efT = sb("efT", [P, U, P])
        hid = sb("hid", [P, 2, U, P])
        onehot = sb("onehot", [P, U, 2, P], BF16)
        ohT = sb("ohT", [P, U, 2, P], BF16)
        idx = sb("idx", [P, U, 2], I32)
        rows = sb("k_rows", [P, U, 2, D])
        prod = sb("prod", [P, 2, H, HD])
        red = sb("red", [P, 2, H])
        p_ef = ps("p_ef", [P, 512])
        p_hid = [ps(f"p_hid{i}", [P, 512]) for i in range(2)]
        p_mlp = ps("p_mlp", [P, 512])
        p_ohT = [ps(f"p_ohT{i}", [P, 1024], BF16) for i in range(2)]
        p_q = [ps(f"p_q{i}", [P, 512]) for i in range(2)]
        w_in = sem("w1_in")
        ef_in = sem("ef_in")
        ef_turned = sem("ef_turned")
        efT_ready = sem("efT_ready")
        hid_done = sem("hid_done", U)
        hid_ready = sem("hid_ready", U)
        mlp_done = sem("mlp_done")
        mlp_taken = sem("mlp_taken")
        onehot_ready = sem("onehot_ready", U)
        ohT_done = sem("ohT_done", U)
        ohT_ready = sem("ohT_ready", U)
        q_done = sem("q_rows_done", U)
        idx_ready = sem("idx_ready", U)
        gathered = sem("gathered", U)
        prod_done = sem("prod_done", U)
        red_done = sem("red_done", U)
        pool_go = sem("pool_go")
        block = ctx.enter_context(nc.Block())
        chunks = edge_attr[0:FULL_GROUPS * GE, :].rearrange("(g p k) f -> p g (k f)", p=P, k=2)

        @block.sync
        def _(sp):
            for k in range(2):
                sp.dma_start(w1s[k * FE:(k + 1) * FE, :], w1[:, :]).then_inc(w_in, 16)
            sp.dma_start(w2s[:, :, :], w2.rearrange("(c p) h -> p c h", p=P)).then_inc(w_in, 16)
            sp.dma_start(b2s[:, :], b2.rearrange("(a h) -> a h", a=1).to_broadcast([P, H])).then_inc(w_in, 16)
            with nc.allow_non_contiguous_dma(reason="256 numbers"):
                sp.dma_start(b1s[:, :], b1.rearrange("(c p) -> p c", p=P)).then_inc(w_in, 16)

            def load(c):
                wait(sp, ef_turned, c)
                sp.dma_start(raw[:, :, :], chunks[:, bass.ds(U * c, U), :]).then_inc(ef_in, 16)

            load(0)
            with sp.Fori(1, CHUNKS - 1) as c:
                load(c)
            sp.wait_ge(ef_turned, CHUNKS - 1)
            g = U * (CHUNKS - 1)
            sp.dma_start(raw[:, 0:FULL_GROUPS - g, :], chunks[:, g:FULL_GROUPS, :]).then_inc(ef_in, 16)
            sp.dma_start(raw[0:TAIL // 2, FULL_GROUPS - g, :],
                         edge_attr[FULL_GROUPS * GE:E, :].rearrange("(p k) f -> p (k f)", k=2)).then_inc(ef_in, 16)

        @block.gpsimd
        def _(pool):
            def gather(i, u):
                wait(pool, prod_done[u], i)
                hold(pool, idx_ready[u], i + 1, pool_go)
                for k in range(2):
                    pool.indirect_dma_start(rows[:, u, k, :], None, k_d[:, :],
                                            bass.IndirectOffsetOnAxis(idx[:, u, k:k + 1], 0)).then_inc(gathered[u], 16)

            for u in range(U):
                gather(0, u)
            with pool.Fori(1, ITERS) as i:
                for u in range(U):
                    gather(i, u)

        @block.scalar
        def _(act):
            def take_ef():
                nc.scalar.activation(efT[:, :, :], p_ef[:, :].rearrange("p (g e) -> p g e", g=U), ACT.Copy).then_inc(efT_ready, 1)

            def take_hidden(i, u, n):
                act.wait_ge(hid_done[u], n + 1)
                nc.scalar.activation(hid[:, u % 2, :, :], p_hid[u % 2][:, :].rearrange("p (g e) -> p g e", g=U), ACT.Relu,
                                     bias=b1s[:, u % 2:u % 2 + 1]).then_inc(hid_ready[u], 1)

            def next_idx(i, u, n):
                wait(act, gathered[u], 32 * n)
                s = U * i + u
                g = group_of(act, t, s, past=1)
                nc.scalar.activation(idx[:, u, :], t["src"][:, bass.ds(2 * g, 2)], ACT.Copy).then_inc(idx_ready[u], 1)

            def iteration(i, mlp):
                for u in range(U):
                    act.wait_ge(ohT_done[u], i + 1)
                    nc.scalar.activation(ohT[:, u, :, :], p_ohT[u % 2][:, 0:2 * P].rearrange("p (k n) -> p k n", k=2),
                                         ACT.Copy).then_inc(ohT_ready[u], 1)
                    if mlp:
                        take_hidden(i, u, i + 1)
                        if u == U - 1:
                            act.wait_ge(ef_turned, i + 3)
                            take_ef()
                    next_idx(i + 1, u, i + 1)

            for u in range(U):
                next_idx(0, u, 0)
            act.wait_ge(w_in, 80)
            act.wait_ge(ef_turned, 1)
            take_ef()
            for u in range(U):
                take_hidden(0, u, 0)
            act.wait_ge(ef_turned, 2)
            take_ef()
            iteration(0, True)
            with act.Fori(1, CHUNKS - 2) as i:
                iteration(i, True)
            i = CHUNKS - 2
            for u in range(U):
                act.wait_ge(ohT_done[u], i + 1)
                nc.scalar.activation(ohT[:, u, :, :], p_ohT[u % 2][:, 0:2 * P].rearrange("p (k n) -> p k n", k=2),
                                     ACT.Copy).then_inc(ohT_ready[u], 1)
                take_hidden(i, u, i + 1)
                next_idx(i + 1, u, i + 1)
            with act.Fori(CHUNKS - 1, ITERS) as i:
                iteration(i, False)

        @block.tensor
        def _(pe):
            def turn_ef(c):
                pe.wait_ge(ef_in, 16 * (c + 1) if not (isinstance(c, int) and c == CHUNKS - 1) else 16 * (CHUNKS + 1))
                for g in range(U):
                    last = nc.tensor.transpose(p_ef[:, g * P:(g + 1) * P], raw[:, g, :], t["ident"][:, :])
                last.then_inc(ef_turned, 1)

            def hidden(c, u):
                k, half = divmod(u, 2)
                if u == 0:
                    pe.wait_ge(efT_ready, c + 1)
                nc.tensor.matmul(p_hid[half][:, :], w1s[k * FE:(k + 1) * FE, half * P:(half + 1) * P],
                                 efT[k * FE:(k + 1) * FE, :, :], start=True, stop=True).then_inc(hid_done[u], 1)

            def mlp_out(c, u):
                k, half = divmod(u, 2)
                pe.wait_ge(hid_ready[u], c + 1)
                if u == 0:
                    wait(pe, mlp_taken, c)
                for g in range(U):
                    col = (2 * g + k) * H
                    last = nc.tensor.matmul(p_mlp[:, col:col + H], hid[:, half, g, :], w2s[:, half, :],
                                            start=(u == 0 and g == 0), stop=(half == 1), skip_group_check=True)
                if u == U - 1:
                    last.then_inc(mlp_done, 1)

            def iteration(i, mlp, turn=True):
                for u in range(U):
                    pe.wait_ge(onehot_ready[u], i + 1)
                    for k in range(2):
                        last = nc.tensor.transpose(p_ohT[u % 2][:, k * P:(k + 1) * P], onehot[:, u, k, :], t["identb"][:, :])
                    last.then_inc(ohT_done[u], 1)
                    if mlp:
                        hidden(i + 1, u)
                        if u == U - 1 and turn:
                            turn_ef(i + 2)
                    b = block_of(pe, t, U * i + u)
                    pe.wait_ge(ohT_ready[u], i + 1)
                    for k in range(2):
                        for part in range(3):
                            last = nc.tensor.matmul(p_q[u % 2][:, k * D:(k + 1) * D], ohT[:, u, k, :],
                                                    q3[:, bass.ds(b, 1), part, :], start=(part == 0), stop=(part == 2))
                    last.then_inc(q_done[u], 1)
                    if mlp:
                        mlp_out(i + 1, u)

            pe.wait_ge(w_in, 80)
            turn_ef(0)
            for u in range(U):
                hidden(0, u)
                mlp_out(0, u)
            turn_ef(1)
            iteration(0, True)
            with pe.Fori(1, CHUNKS - 3) as i:
                iteration(i, True)
            iteration(CHUNKS - 3, True)
            iteration(CHUNKS - 2, True, turn=False)
            with pe.Fori(CHUNKS - 1, ITERS) as i:
                iteration(i, False)

        @block.vector
        def _(dve):
            def make_onehot(s, u, load=True):
                g = group_of(dve, t, s, past=1)
                for k in range(2):
                    last = nc.vector.tensor_scalar(onehot[:, u, k, :], t["iota"][:, :], t["nbase"][:, bass.ds(s, 1)],
                                                   t["dst"][:, bass.ds(2 * g + k, 1)], ALU.add, ALU.is_equal)
                last.then_inc(onehot_ready[u], 1)

            def take_mlp(c):
                dve.wait_ge(mlp_done, c + 1)
                nc.vector.tensor_tensor(scores[:, bass.ds(2 * U * c, 2 * U), :],
                                        p_mlp[:, 0:2 * U * H].rearrange("p (c h) -> p c h", h=H),
                                        b2s[:, :].unsqueeze(1).to_broadcast([P, 2 * U, H]), ALU.add).then_inc(mlp_taken, 1)

            def iteration(i, mlp):
                for u in range(U):
                    s = U * i + u
                    make_onehot(s + 1, (u + 1) % U)
                    g = group_of(dve, t, s)
                    dve.wait_ge(q_done[u], i + 1)
                    dve.wait_ge(gathered[u], 32 * (i + 1))
                    nc.vector.tensor_tensor(prod[:, :, :, :].rearrange("p k h c -> p (k h c)"), p_q[u % 2][:, :],
                                            rows[:, u, :, :].rearrange("p k d -> p (k d)"), ALU.mult).then_inc(prod_done[u], 1)
                    dve.wait_ge(prod_done[u], i + 1)
                    nc.vector.tensor_reduce(red[:, :, :].rearrange("p k h -> p (k h)"),
                                            prod[:, :, :, :].rearrange("p k h c -> p (k h) c"), AX.X, ALU.add).then_inc(red_done[u], 1)
                    dve.wait_ge(red_done[u], i + 1)
                    if u == 0:
                        dve.wait_ge(mlp_taken, i + 1 if mlp is not None else CHUNKS)
                    to = scores[:, bass.ds(2 * g, 2), :]
                    nc.vector.tensor_tensor(to, to, red[:, :, :], ALU.add)
                if mlp:
                    take_mlp(i + 1)

            dve.wait_ge(w_in, 80)
            take_mlp(0)
            make_onehot(0, 0)
            iteration(0, True)
            with dve.Fori(1, CHUNKS - 1) as i:
                iteration(i, True)
            with dve.Fori(CHUNKS - 1, ITERS) as i:
                iteration(i, None)


def softmax_numerators(nc, t, scores, newseg_d):
    ctx, sb, ps, sem = phase(nc)
    PIECES = 7
    PL = ROW_E // PIECES
    with ctx:
        sT = sb("sT", [P, ROW_GROUPS, P, 2])
        mx = sb("mx", [P, ROW_E])
        pen = sb("pen", [P, 2, PL + 1])
        stage = sb("stage", [P, 2, 2, P])
        line = sb("line", [1, 4, P])
        carry = sb("carry", [P, 2])
        turned = [ps(f"sturn{i}", [P, 512]) for i in range(2)]
        small = ps("small", [P, 512])
        small2 = ps("small2", [P, 512])
        stage_ready = sem("stage_ready", 2)
        turned_ready = sem("sturned_ready", 2)
        turned_taken = sem("sturned_taken", 2)
        back_staged = sem("back_staged", 2)
        back_turned = sem("back_turned", 2)
        back_taken = sem("back_taken", 2)
        pen_in = sem("pen_in", 2)
        scanned = sem("scanned")
        line_ready = sem("line_ready")
        small_ready = sem("small_ready")
        link = sem("mlink")
        shifted = sem("shifted")
        block = ctx.enter_context(nc.Block())
        by_j = scores[:, :, :].rearrange("p (q j k) h -> p q j k h", q=ROWS, j=ROW_GROUPS)
        flat = sT[:, :, :, :].rearrange("r j p k -> r (j p k)")
        passes = [("f", range(PIECES)), ("f", range(PIECES)), ("b", range(PIECES - 1, -1, -1)), ("b", range(PIECES - 1, -1, -1))]
        plan = [(n, way, c) for n, (way, order) in enumerate(passes) for c in order]

        @block.sync
        def _(sp):
            for m, (n, way, c) in enumerate(plan):
                if m >= 2:
                    sp.wait_ge(scanned, m - 1)
                for q in range(ROWS):
                    a = q * ROW_E + c * PL
                    sp.dma_start(pen[q * H:(q + 1) * H, m % 2, :],
                                 newseg_d[a:a + PL + 1].rearrange("(a e) -> a e", a=1).to_broadcast([H, PL + 1])).then_inc(pen_in[m % 2], 16)

        @block.scalar
        def _(act):
            def stage_in(j, s, n):
                wait(act, turned_ready[s], n)
                nc.scalar.activation(stage[:, s, :, :].rearrange("p k (q h) -> p k q h", h=H),
                                     by_j[:, :, bass.ds(j, 1), :, :].rearrange("p q j k h -> p (j k) q h"),
                                     ACT.Copy).then_inc(stage_ready[s], 1)

            blocks_loop(act, stage_in)

            def stage_back(j, s, n):
                wait(act, back_turned[s], n)
                nc.scalar.activation(stage[:, s, :, :],
                                     sT[:, bass.ds(j, 1), :, :].rearrange("r j p k -> r (j k) p"),
                                     ACT.Exp).then_inc(back_staged[s], 1)

            act.wait_ge(shifted, 1)
            blocks_loop(act, stage_back)

        @block.tensor
        def _(pe):
            def turn(j, s, n):
                pe.wait_ge(stage_ready[s], n + 1)
                wait(pe, turned_taken[s], n)
                for k in range(2):
                    last = nc.tensor.transpose(turned[s][:, k * P:(k + 1) * P], stage[:, s, k, :], t["ident"][:, :])
                last.then_inc(turned_ready[s], 1)

            blocks_loop(pe, turn)
            for way in range(2):
                pe.wait_ge(line_ready, 3 * way + 1)
                nc.tensor.transpose(small[0:1, 0:P], carry[:, 0:1], t["ident"][:, :]).then_inc(small_ready, 1)
                pe.wait_ge(line_ready, 3 * way + 2)
                nc.tensor.transpose(small2[:, 0:1], line[:, 3, :], t["ident"][0:1, 0:1]).then_inc(small_ready, 1)

            def turn_back(j, s, n):
                pe.wait_ge(back_staged[s], n + 1)
                wait(pe, back_taken[s], n)
                for k in range(2):
                    last = nc.tensor.transpose(turned[s][:, k * P:(k + 1) * P], stage[:, s, k, :], t["ident"][:, :])
                last.then_inc(back_turned[s], 1)

            blocks_loop(pe, turn_back)

        @block.vector
        def _(dve):
            def take(j, s, n):
                dve.wait_ge(turned_ready[s], n + 1)
                nc.vector.tensor_copy(sT[:, bass.ds(j, 1), :, :].rearrange("r j p k -> r (j k) p"),
                                      turned[s][:, 0:2 * P].rearrange("r (k p) -> r k p", k=2)).then_inc(turned_taken[s], 1)

            blocks_loop(dve, take)
            dve.wait_ge(turned_taken[0], BLOCKS // 2 + 1)
            dve.wait_ge(turned_taken[1], BLOCKS // 2)
            cnt = [0]

            def done(ins):
                cnt[0] += 1
                ins.then_inc(link, 1)
                dve.wait_ge(link, cnt[0])

            for m, (n, way, c) in enumerate(plan):
                a, b = c * PL, (c + 1) * PL
                dve.wait_ge(pen_in[m % 2], 16 * ROWS * (m // 2 + 1))
                if m:
                    dve.wait_ge(scanned, m)
                first = c == (0 if way == "f" else PIECES - 1)
                if way == "f":
                    init = (-BIG if n == 0 else carry[:, 1:2]) if first else mx[:, a - 1:a]
                    nc.vector.tensor_tensor_scan(mx[:, a:b], pen[:, m % 2, 0:PL], flat[:, a:b] if n == 0 else mx[:, a:b], init,
                                                 ALU.add, ALU.max).then_inc(scanned, 1)
                else:
                    init = (-BIG if n == 2 else carry[:, 1:2]) if first else mx[:, b:b + 1]
                    nc.vector.tensor_tensor_scan(mx[:, a:b][:, ::-1], pen[:, m % 2, 1:PL + 1][:, ::-1], mx[:, a:b][:, ::-1], init,
                                                 ALU.add, ALU.max).then_inc(scanned, 1)
                if m % PIECES == PIECES - 1 and n in (0, 2):
                    w = 0 if n == 0 else 1
                    edge = mx[:, ROW_E - 1:ROW_E] if n == 0 else mx[:, 0:1]
                    dve.wait_ge(scanned, m + 1)
                    nc.vector.tensor_copy(carry[:, 0:1], edge).then_inc(line_ready, 1)
                    dve.wait_ge(small_ready, 2 * w + 1)
                    done(nc.vector.tensor_copy(line[:, 0, :].rearrange("a (h q) -> a h q", h=H),
                                               small[0:1, 0:P].rearrange("a (q h) -> a h q", h=H)))
                    pens = t["chain"][:, w, :, :].rearrange("a h q -> a (h q)")
                    step = 1 if n == 0 else -1
                    done(nc.vector.tensor_tensor_scan(line[:, 1, ::step], pens[:, ::step], line[:, 0, ::step], -BIG, ALU.add, ALU.max))
                    done(nc.vector.memset(line[:, 3, :], -BIG))
                    by_q = line[:, 3, :].rearrange("a (q h) -> a h q", h=H)
                    got = line[:, 1, :].rearrange("a (h q) -> a h q", h=H)
                    if n == 0:
                        nc.vector.tensor_copy(by_q[:, :, 1:ROWS], got[:, :, 0:ROWS - 1]).then_inc(line_ready, 1)
                    else:
                        nc.vector.tensor_copy(by_q[:, :, 0:ROWS - 1], got[:, :, 1:ROWS]).then_inc(line_ready, 1)
                    dve.wait_ge(small_ready, 2 * w + 2)
                    nc.vector.tensor_copy(carry[:, 1:2], small2[:, 0:1]).then_inc(line_ready, 1)
                    dve.wait_ge(line_ready, 3 * w + 3)
            dve.wait_ge(scanned, len(plan))
            nc.vector.tensor_tensor(flat, flat, mx[:, :], ALU.subtract).then_inc(shifted, 1)

            def take_back(j, s, n):
                dve.wait_ge(back_turned[s], n + 1)
                nc.vector.tensor_copy(by_j[:, :, bass.ds(j, 1), :, :].rearrange("p q j k h -> p (j k) q h"),
                                      turned[s][:, 0:2 * P].rearrange("p (k q h) -> p k q h", k=2, h=H)).then_inc(back_taken[s], 1)

            blocks_loop(dve, take_back)


def edge_sums(nc, t, name, table, width, index, acc, weigh, weigh_engine, extra=None):
    ctx, sb, ps, sem = phase(nc)
    with ctx:
        onehot = sb(name + "oh", [P, U, 2, P])
        idx = sb(name + "idx", [P, U, 2], I32)
        rows = sb(name + "rows", [P, U, 2, width])
        wrows = sb(name + "wrows", [P, U, 2, width])
        sums = [ps(f"{name}sums{i}", [P, 512]) for i in range(U)]
        onehot_ready = sem(name + "oh_ready", U)
        idx_ready = sem(name + "idx_ready", U)
        gathered = sem(name + "gathered", U)
        weighed = sem(name + "weighed", U)
        summed = sem(name + "summed", U)
        added = sem(name + "added", U)
        cleared = sem(name + "cleared")
        pool_go = sem(name + "pool_go")
        block = ctx.enter_context(nc.Block())

        def iterations(eng, body):
            body(0)
            with eng.Fori(1, ITERS) as i:
                body(i)

        @block.gpsimd
        def _(pool):
            def body(i):
                for u in range(U):
                    wait(pool, weighed[u], i)
                    hold(pool, idx_ready[u], i + 1, pool_go)
                    for k in range(2):
                        pool.indirect_dma_start(rows[:, u, k, :], None, table[:, :],
                                                bass.IndirectOffsetOnAxis(idx[:, u, k:k + 1], 0)).then_inc(gathered[u], 16)

            iterations(pool, body)

        def do_weigh(eng, i, u, g):
            eng.wait_ge(gathered[u], 32 * (i + 1))
            wait(eng, summed[u], i)
            weigh(wrows[:, u, :, :], rows[:, u, :, :], g).then_inc(weighed[u], 1)

        @block.scalar
        def _(act):
            def next_idx(i, u, n):
                wait(act, gathered[u], 32 * n)
                s = U * i + u
                g = group_of(act, t, s, past=1)
                nc.scalar.activation(idx[:, u, :], index[:, bass.ds(2 * g, 2)], ACT.Copy).then_inc(idx_ready[u], 1)

            def body(i):
                for u in range(U):
                    if weigh_engine == "scalar":
                        s = U * i + u
                        g = group_of(act, t, s)
                        do_weigh(act, i, u, g)
                    next_idx(i + 1, u, i + 1)

            for u in range(U):
                next_idx(0, u, 0)
            iterations(act, body)

        @block.tensor
        def _(pe):
            def body(i):
                for u in range(U):
                    pe.wait_ge(onehot_ready[u], i + 1)
                    pe.wait_ge(weighed[u], i + 1)
                    wait(pe, added[u], i)
                    for k in range(2):
                        last = nc.tensor.matmul(sums[u][:, 0:width], onehot[:, u, k, :], wrows[:, u, k, :],
                                                start=(k == 0), stop=(k == 1))
                    last.then_inc(summed[u], 1)

            iterations(pe, body)

        @block.vector
        def _(dve):
            def prepare(s, u, i):
                g = group_of(dve, t, s)
                wait(dve, summed[u], i)
                for k in range(2):
                    last = nc.vector.tensor_scalar(onehot[:, u, k, :], t["iota"][:, :], t["nbase"][:, bass.ds(s, 1)],
                                                   t["dst"][:, bass.ds(2 * g + k, 1)], ALU.add, ALU.is_equal)
                last.then_inc(onehot_ready[u], 1)
                if weigh_engine == "vector":
                    do_weigh(dve, i, u, g)

            def add(s, u, i):
                b = block_of(dve, t, s)
                dve.wait_ge(summed[u], i + 1)
                if u > 0:
                    dve.wait_ge(added[u - 1], i + 1)
                else:
                    wait(dve, added[U - 1], i)
                to = acc[:, bass.ds(b, 1), :]
                nc.vector.tensor_tensor(to, to, sums[u][:, 0:width].unsqueeze(1), ALU.add).then_inc(added[u], 1)

            nc.vector.memset(acc[:, :, :], 0.0).then_inc(cleared, 1)
            dve.wait_ge(cleared, 1)
            for u in range(U):
                prepare(u, u, 0)
                if u:
                    add(u - 1, u - 1, 0)
            with dve.Fori(1, ITERS) as i:
                for u in range(U):
                    prepare(U * i + u, u, i)
                    if u:
                        add(U * i + u - 1, u - 1, i)
                    else:
                        add(U * i - 1, U - 1, i - 1)
            add(STEPS - 1, U - 1, ITERS - 1)
            dve.wait_ge(added[U - 1], ITERS)


def weighted_sums(nc, t, scores, att, v_d):
    def weigh(out, rows, g):
        return nc.vector.tensor_tensor(
            out.rearrange("p k (h c) -> p (k h) c", h=H), rows.rearrange("p k (h c) -> p (k h) c", h=H),
            scores[:, bass.ds(2 * g, 2), :].rearrange("p k h -> p (k h)").unsqueeze(2).to_broadcast([P, 2 * H, HD1]), ALU.mult)

    edge_sums(nc, t, "v_", v_d, H * HD1, t["src"], att[:, :, :, :].rearrange("p b h c -> p b (h c)"), weigh, "vector")


def messages(nc, t, att, x1, x, wo, bo, rel_w, gate_w, msg_d):
    ctx, sb, ps, sem = phase(nc)
    QUARTERS = 4
    with ctx:
        wos = sb("wos", [P, 2, D])
        bos = sb("bos", [P, D])
        wr = sb("wr", [P, 2, RELS, D])
        gw = sb("gw", [P, 2, RELS])
        xin = sb("x_res", [P, 2, D])
        den = sb("den", [P, H, 1])
        rden = sb("rden", [P, H, 1])
        o = sb("o", [P, H, HD])
        oT = sb("oT", [P, 2, P])
        stats = sb("stats1", [P, 6])
        mv = sb("mv1", [P, 2])
        std = sb("std1", [P, 1])
        rstd = sb("rstd1", [P, 1])
        xn = sb("xn1", [P, D])
        hT = sb("h1T", [P, 2, 2, P])
        gate = sb("gate", [P, 2, RELS])
        msg = sb("msg", [P, RELS, D])
        p_oT = ps("p_oT", [P, 512])
        p_o = ps("p_o", [P, 512])
        p_xT = ps("p_xT", [P, 512])
        p_g = ps("p_g", [P, 512])
        p_m = [ps(f"p_m{i}", [P, 512]) for i in range(4)]
        dve_go = sem("dve_go1")
        w_in = sem("wr_in")
        x_in = sem("xr_in", 2)
        xb_ready = sem("xb_ready", 2)
        den_link = sem("den_link")
        o_ready = sem("o_ready")
        oT_done = sem("oT_done")
        oT_ready = sem("oT_ready")
        wo_done = sem("wo_done")
        x1_ready = sem("x1_ready")
        ln_link = sem("ln_link")
        std_ready = sem("std1_ready")
        xn_ready = sem("xn1_ready")
        xT_done = sem("xT_done")
        hT_ready = sem("h1T_ready")
        gate_done = sem("gate_done")
        gate_ready = sem("gate_ready")
        msg_done = sem("msg_done", 4)
        msg_taken = sem("msg_taken", 4)
        msg_stored = sem("msg_stored", QUARTERS)
        block = ctx.enter_context(nc.Block())
        table = msg_d.rearrange("(r n) d -> n r d", r=RELS)

        def all_blocks(eng, front, back, ends=None):
            front(0, 0, 0)
            back(0, 0, 0, True)
            with eng.Fori(0, (BLOCKS - 3) // 2) as i:
                back(2 * i + 1, 1, i, True)
                back(2 * i + 2, 0, i + 1, True)
            back(BLOCKS - 2, 1, (BLOCKS - 3) // 2, True)
            back(BLOCKS - 1, 0, (BLOCKS - 1) // 2, False)

        @block.sync
        def _(sp):
            sp.dma_start(wos[:, :, :], wo.rearrange("(c p) n -> p c n", p=P)).then_inc(w_in, 16)
            sp.dma_start(bos[:, :], bo.rearrange("(a n) -> a n", a=1).to_broadcast([P, D])).then_inc(w_in, 16)
            for c in range(2):
                sp.dma_start(wr[:, c, :, :], rel_w[:, c * P:(c + 1) * P, :].rearrange("r p n -> p r n")).then_inc(w_in, 16)
            with nc.allow_non_contiguous_dma(reason="4096 numbers"):
                for c in range(2):
                    sp.dma_start(gw[:, c, :], gate_w[:, c * P:(c + 1) * P, :].rearrange("r p a -> p (r a)")).then_inc(w_in, 16)

            def load(b, s, n, rows=P):
                wait(sp, x1_ready, b - 1)
                sp.dma_start(xin[0:rows, s, :], x[bass.ds(b * P, rows), :]).then_inc(x_in[s], 16)

            def store(b):
                for q in range(QUARTERS):
                    use = 2 * b + q // 2
                    sp.wait_ge(msg_taken[2 * (q % 2)], use + 1)
                    sp.wait_ge(msg_taken[2 * (q % 2) + 1], use + 1)
                    sp.dma_start(table[bass.ds(b * P, P), 4 * q:4 * q + 4, :], msg[:, 4 * q:4 * q + 4, :]).then_inc(msg_stored[q], 16)

            load(0, 0, 0)
            load(1, 1, 0)
            store(0)
            with sp.Fori(0, (BLOCKS - 3) // 2) as i:
                load(2 * i + 2, 0, i + 1)
                store(2 * i + 1)
                load(2 * i + 3, 1, i + 1)
                store(2 * i + 2)
            load(BLOCKS - 1, 0, BLOCKS // 2, LAST_ROWS)
            store(BLOCKS - 2)
            store(BLOCKS - 1)
            for q in range(QUARTERS):
                sp.wait_ge(msg_stored[q], 16 * BLOCKS)

        @block.gpsimd
        def _(pool):
            pool.wait_ge(w_in, 96)

            def add_bias(b, s, n):
                pool.wait_ge(x_in[s], 16 * (n + 1))
                nc.gpsimd.tensor_tensor(xin[:, s, :], xin[:, s, :], bos[:, :], ALU.add).then_inc(xb_ready[s], 1)

            blocks_loop(pool, add_bias)

        def front_of(pieces):
            def front(b, s, n):
                for piece in pieces:
                    piece(b, s, n)
            return front

        def next_of(b, s, n):
            return (b + 1, 1 - s, n if s == 0 else n + 1)

        @block.vector
        def _(dve):
            def normalise(b, s, n):
                a = att[:, bass.ds(b, 1), :, :].rearrange("p b h c -> p (b h) c")
                nc.vector.tensor_scalar(den[:, :, :], a[:, :, HD:HD1], 1.0e-30, None, ALU.max).then_inc(den_link, 1)
                dve.wait_ge(den_link, 2 * b + 1)
                nc.vector.reciprocal(rden[:, :, :], den[:, :, :]).then_inc(den_link, 1)
                dve.wait_ge(den_link, 2 * b + 2)
                nc.vector.tensor_tensor(o[:, :, :], a[:, :, 0:HD], rden[:, :, :].to_broadcast([P, H, HD]), ALU.mult).then_inc(o_ready, 1)

            def residual(b, s, n):
                to = x1[:, bass.ds(b, 1), :].rearrange("p b d -> p (b d)")
                dve.wait_ge(wo_done, b + 1)
                dve.wait_ge(xb_ready[s], n + 1)
                nc.vector.tensor_tensor(to, p_o[:, 0:D], xin[:, s, :], ALU.add).then_inc(x1_ready, 1)
                hold(dve, x1_ready, b + 1, dve_go)
                nc.vector.bn_stats(stats[:, :], to).then_inc(ln_link, 1)
                hold(dve, ln_link, 3 * b + 1, dve_go)
                nc.vector.bn_aggr(mv[:, :], stats[:, :]).then_inc(ln_link, 1)

            def layer_norm(b, s, n):
                to = x1[:, bass.ds(b, 1), :].rearrange("p b d -> p (b d)")
                dve.wait_ge(std_ready, b + 1)
                nc.vector.reciprocal(rstd[:, :], std[:, :]).then_inc(ln_link, 1)
                dve.wait_ge(ln_link, 3 * b + 3)
                nc.vector.tensor_scalar(xn[:, :], to, mv[:, 0:1], rstd[:, :], ALU.subtract, ALU.mult).then_inc(xn_ready, 1)

            def take(b, s, c):
                use = 2 * b + c // 4
                dve.wait_ge(msg_done[c % 4], use + 1)
                wait(dve, msg_stored[c // 2], 16 * b)
                for r in range(2):
                    last = nc.vector.tensor_scalar(msg[:, 2 * c + r, :], p_m[c % 4][:, r * D:(r + 1) * D],
                                                   gate[:, s, 2 * c + r:2 * c + r + 1], None, ALU.mult)
                last.then_inc(msg_taken[c % 4], 1)

            def back(b, s, n, more):
                if more:
                    normalise(*next_of(b, s, n))
                dve.wait_ge(gate_ready, b + 1)
                take(b, s, 1)
                if more:
                    residual(*next_of(b, s, n))
                take(b, s, 3)
                if more:
                    layer_norm(*next_of(b, s, n))
                take(b, s, 5)
                take(b, s, 7)

            all_blocks(dve, front_of([normalise, residual, layer_norm]), back)

        @block.scalar
        def _(act):
            def take_oT(b, s, n):
                act.wait_ge(oT_done, b + 1)
                nc.scalar.activation(oT[:, :, :], p_oT[:, 0:2 * P].rearrange("p (c n) -> p c n", c=2), ACT.Copy).then_inc(oT_ready, 1)

            def root(b, s, n):
                act.wait_ge(ln_link, 3 * b + 2)
                nc.scalar.activation(std[:, :], mv[:, 1:2], ACT.Sqrt, bias=t["eps"][:, 0:1]).then_inc(std_ready, 1)

            def take_hT(b, s, n):
                act.wait_ge(xT_done, b + 1)
                nc.scalar.activation(hT[:, s, :, :], p_xT[:, 0:2 * P].rearrange("p (c n) -> p c n", c=2), ACT.Relu).then_inc(hT_ready, 1)

            def gates(b, s, n):
                act.wait_ge(gate_done, b + 1)
                nc.scalar.activation(gate[:, s, :], p_g[:, 0:RELS], ACT.Sigmoid).then_inc(gate_ready, 1)

            def take(b, s, c):
                use = 2 * b + c // 4
                act.wait_ge(msg_done[c % 4], use + 1)
                wait(act, msg_stored[c // 2], 16 * b)
                for r in range(2):
                    last = nc.scalar.activation(msg[:, 2 * c + r, :], p_m[c % 4][:, r * D:(r + 1) * D], ACT.Copy,
                                                scale=gate[:, s, 2 * c + r:2 * c + r + 1])
                last.then_inc(msg_taken[c % 4], 1)

            def back(b, s, n, more):
                act.wait_ge(gate_ready, b + 1)
                if more:
                    take_oT(*next_of(b, s, n))
                take(b, s, 0)
                take(b, s, 2)
                if more:
                    root(*next_of(b, s, n))
                take(b, s, 4)
                if more:
                    take_hT(*next_of(b, s, n))
                take(b, s, 6)
                if more:
                    gates(*next_of(b, s, n))

            all_blocks(act, front_of([take_oT, root, take_hT, gates]), back)

        @block.tensor
        def _(pe):
            pe.wait_ge(w_in, 96)

            def turn_o(b, s, n):
                pe.wait_ge(o_ready, b + 1)
                flat = o[:, :, :].rearrange("p h c -> p (h c)")
                for c in range(2):
                    last = nc.tensor.transpose(p_oT[:, c * P:(c + 1) * P], flat[:, c * P:(c + 1) * P], t["ident"][:, :])
                last.then_inc(oT_done, 1)

            def project(b, s, n):
                pe.wait_ge(oT_ready, b + 1)
                for c in range(2):
                    last = nc.tensor.matmul(p_o[:, 0:D], oT[:, c, :], wos[:, c, :], start=(c == 0), stop=(c == 1))
                last.then_inc(wo_done, 1)

            def turn_x(b, s, n):
                pe.wait_ge(xn_ready, b + 1)
                for c in range(2):
                    last = nc.tensor.transpose(p_xT[:, c * P:(c + 1) * P], xn[:, c * P:(c + 1) * P], t["ident"][:, :])
                last.then_inc(xT_done, 1)

            def gates(b, s, n):
                pe.wait_ge(hT_ready, b + 1)
                for c in range(2):
                    last = nc.tensor.matmul(p_g[:, 0:RELS], hT[:, s, c, :], gw[:, c, :], start=(c == 0), stop=(c == 1))
                last.then_inc(gate_done, 1)

            def relations(b, s, c):
                use = 2 * b + c // 4
                wait(pe, msg_taken[c % 4], use)
                for half in range(2):
                    last = nc.tensor.matmul(p_m[c % 4][:, :], hT[:, s, half, :], wr[:, half, 2 * c:2 * c + 2, :],
                                            start=(half == 0), stop=(half == 1))
                last.then_inc(msg_done[c % 4], 1)

            def back(b, s, n, more):
                relations(b, s, 0)
                if more:
                    turn_o(*next_of(b, s, n))
                relations(b, s, 1)
                if more:
                    project(*next_of(b, s, n))
                relations(b, s, 2)
                relations(b, s, 3)
                relations(b, s, 4)
                if more:
                    turn_x(*next_of(b, s, n))
                relations(b, s, 5)
                relations(b, s, 6)
                if more:
                    gates(*next_of(b, s, n))
                relations(b, s, 7)

            all_blocks(pe, front_of([turn_o, project, turn_x, gates]), back)


def message_sums(nc, t, x1, msg_d, out):
    with nc.sbuf_tensor("agg", [P, BLOCKS, D], F32) as agg:
        def weigh(o, rows, g):
            for k in range(2):
                last = nc.scalar.activation(o[:, k, :], rows[:, k, :], ACT.Copy, scale=t["norm"][:, bass.ds(2 * g + k, 1)])
            return last

        edge_sums(nc, t, "m_", msg_d, D, t["rel"], agg[:, :, :], weigh, "scalar")

        ctx, sb, ps, sem = phase(nc)
        PARTS = 7
        W = BLOCKS // PARTS
        with ctx:
            out_ready = sem("out_ready")
            out_stored = sem("out_stored")
            block = ctx.enter_context(nc.Block())

            @block.vector
            def _(dve):
                for c in range(PARTS):
                    a = slice(c * W, (c + 1) * W)
                    nc.vector.scalar_tensor_tensor(out=agg[:, a, :], in0=agg[:, a, :], scalar=0.0, in1=x1[:, a, :],
                                                   op0=ALU.max, op1=ALU.add).then_inc(out_ready, 1)

            @block.sync
            def _(sp):
                whole = out[0:(BLOCKS - 1) * P, :].rearrange("(b p) d -> p b d", p=P)
                for c in range(PARTS):
                    a, b = c * W, min((c + 1) * W, BLOCKS - 1)
                    sp.wait_ge(out_ready, c + 1)
                    sp.dma_start(whole[:, a:b, :], agg[:, a:b, :]).then_inc(out_stored, 16)
                sp.dma_start(out[(BLOCKS - 1) * P:N, :], agg[0:LAST_ROWS, BLOCKS - 1, :]).then_inc(out_stored, 16)
                sp.wait_ge(out_stored, 16 * (PARTS + 1))


_INS = ['x', 'src', 'dst', 'edge_attr_64', 'edge_type_16', 'edge_weight1', 'L0_gnn_Wq', 'L0_gnn_Wk', 'L0_gnn_Wv',
        'L0_gnn_W1', 'L0_gnn_b1', 'L0_gnn_W2', 'L0_gnn_b2', 'L0_gnn_Wo', 'L0_gnn_bo', 'L1_gnn_weight', 'L1_gnn_gate_weight']


def kernel(**inputs):
    import numpy as _np
    import concourse.bacc as _bacc
    from concourse import mybir as _mybir
    from concourse.bass_utils import run_bass_kernel_spmd as _run

    nc = _bacc.Bacc("TRN2", target_bir_lowering=False, num_devices=1)
    arrays, args = {}, []
    for name in _INS:
        a = _np.ascontiguousarray(inputs[name])
        arrays[f"in_{name}_dram"] = a
        args.append(nc.dram_tensor(f"in_{name}_dram", a.shape, _mybir.dt.from_np(a.dtype), kind="ExternalInput").ap())
    args.append(nc.dram_tensor("out_0_dram", (N, D), F32, kind="ExternalOutput").ap())
    build(nc, *args)
    r = _run(nc, [arrays], core_ids=[0])
    return r.results[0]["out_0_dram"]
```

```python
from contextlib import ExitStack

import concourse.bass as bass
from concourse import mybir

F32 = mybir.dt.float32
BF16 = mybir.dt.bfloat16
I32 = mybir.dt.int32
ALU = mybir.AluOpType
ACT = mybir.ActivationFunctionType
AX = mybir.AxisListType

P = 128
N, E, D, H, FE, RELS = 6250, 200000, 256, 8, 64, 16
HD = D // H
HD1 = HD + 1
BLOCKS = -(-N // P)
NPAD = BLOCKS * P
LAST_ROWS = N - (BLOCKS - 1) * P
GE = 2 * P
ROWS = 16
ROW_GROUPS = 49
GROUPS = ROWS * ROW_GROUPS
FULL_GROUPS = E // GE
TAIL = E - FULL_GROUPS * GE
EPAD = GROUPS * GE
ROW_E = ROW_GROUPS * GE
COLS = 2 * GROUPS
U = 4
STEPS = GROUPS + BLOCKS - 1
ITERS = STEPS // U
CHUNKS = GROUPS // U
TSTEPS = STEPS + U
TCOLS = 2 * TSTEPS
PADNODE = NPAD - 1
BIG = 1.0e30
EPS = 1.0e-5
MW0 = (U - 1) * H
MW = (2 * U - 1) * H
WIN = 16 * (2 + 1 + 1 + U)

assert STEPS % U == 0 and GROUPS % U == 0 and PADNODE >= N


def wait(eng, sem, value):
    if isinstance(value, int) and value <= 0:
        return
    eng.wait_ge(sem, value)


def hold(eng, sem, value, passed):
    eng.wait_ge(sem, value)
    eng.sem_inc(passed, 1)


def build(nc, x, src, dst, edge_attr, edge_type, edge_weight, wq, wk, wv, w1, b1, w2, b2, wo, bo,
          rel_w, gate_w, out):
    newseg_d = nc.dram_tensor("newseg_d", [EPAD + 1], F32, kind="Internal").ap()
    k_d = nc.dram_tensor("k_d", [NPAD, D], F32, kind="Internal").ap()
    v_d = nc.dram_tensor("v_d", [NPAD, H * HD1], F32, kind="Internal").ap()
    mlp_d = nc.dram_tensor("mlp_d", [GROUPS * H, GE], F32, kind="Internal").ap()
    msg_d = nc.dram_tensor("msg_d", [RELS * NPAD, D], F32, kind="Internal").ap()

    with ExitStack() as ctx:
        def sb(name, shape, dt=F32):
            return ctx.enter_context(nc.sbuf_tensor(name, shape, dt))

        t = {}
        t["dst"] = sb("t_dst", [P, TCOLS])
        t["src"] = sb("t_src", [P, TCOLS], I32)
        t["rel"] = sb("t_rel", [P, TCOLS], I32)
        t["norm"] = sb("t_norm", [P, TCOLS])
        t["block"] = sb("t_block", [1, TSTEPS], I32)
        t["group"] = sb("t_group", [1, TSTEPS], I32)
        t["iota"] = sb("t_iota", [P, P])
        t["iotab"] = sb("t_iotab", [P, P], BF16)
        t["ident"] = sb("t_ident", [P, P])
        t["identb"] = sb("t_identb", [P, P], BF16)
        t["eps"] = sb("t_eps", [P, 1])
        t["chain"] = sb("t_chain", [1, 2, H, ROWS])
        edge_tables(nc, t, src, dst, edge_type, edge_weight, newseg_d)
        with ExitStack() as sums_ctx:
            with nc.sbuf_tensor("scores", [P, COLS, H], F32) as scores:
                with nc.sbuf_tensor("q3", [P, BLOCKS, 3, D], BF16) as q3:
                    node_projections(nc, t, q3, scores, x, wq, wk, wv, k_d, v_d)
                    edge_scores(nc, t, q3, scores, edge_attr, w1, b1, w2, b2, k_d, mlp_d)
                softmax_numerators(nc, t, scores, newseg_d, mlp_d)
                att = sums_ctx.enter_context(nc.sbuf_tensor("att", [P, BLOCKS, H, HD1], F32, side="right"))
                weighted_sums(nc, t, scores, att, v_d)
            with nc.sbuf_tensor("x1", [P, BLOCKS, D], F32) as x1:
                messages(nc, t, att, x1, x, wo, bo, rel_w, gate_w, msg_d)
                message_sums(nc, t, x1, msg_d, out)


def phase(nc):
    ctx = ExitStack()
    sems = []

    def clear():
        nc.clear_and_free_semaphores(sems)
        nc.all_engine_barrier()

    ctx.callback(clear)

    def sb(name, shape, dt=F32):
        return ctx.enter_context(nc.sbuf_tensor(name, shape, dt))

    def ps(name, shape, dt=F32):
        return ctx.enter_context(nc.psum_tensor(name, shape, dt))

    def sem(name, n=None):
        if n is None:
            sems.append(nc.alloc_semaphore(name))
            return sems[-1]
        return [sem(f"{name}{i}") for i in range(n)]

    return ctx, sb, ps, sem


def edge_tables(nc, t, src, dst, edge_type, edge_weight, newseg_d):
    ctx, sb, ps, sem = phase(nc)
    J = -(-GROUPS // P)
    FULL_J = FULL_GROUPS // P
    REST = FULL_GROUPS - FULL_J * P
    PADROWS = GROUPS - FULL_J * P
    with ctx:
        dst_i = sb("dst_i", [P, J, GE], I32)
        src_i = sb("src_i", [P, J, GE], I32)
        typ_i = sb("typ_i", [P, J, GE], I32)
        nrm_f = sb("nrm_f", [P, J, GE])
        dst_f = sb("dst_f", [P, J, GE])
        src_f = sb("src_f", [P, J, GE])
        rel_f = sb("rel_f", [P, J, GE])
        before = sb("before", [P, J], I32)
        beforef = sb("beforef", [P, J])
        newseg = sb("newseg", [P, J, GE])
        last_blk = sb("last_blk", [P, J], I32)
        iota_g = sb("iota_g", [P, J], I32)
        iota_gf = sb("iota_gf", [P, J])
        key = sb("key", [P, J])
        iota_i = sb("iota_i", [P, TSTEPS], I32)
        iota_s = sb("iota_s", [P, TSTEPS])
        step128 = sb("step128", [P, TSTEPS])
        passed = sb("passed", [P, J, TSTEPS], BF16)
        ones = sb("ones", [P, P], BF16)
        pick = sb("pick", [P, J, TSTEPS])
        nbase = sb("nbase", [P, TSTEPS])
        ends = sb("ends", [1, 2, ROWS + 1], I32)
        endsf = sb("endsf", [1, 2, ROWS + 1])
        tail = sb("tail", [1, 1])
        blkf = sb("blkf", [1, TSTEPS])
        grpf = sb("grpf", [1, TSTEPS])
        HS = TSTEPS // 2
        turned = [ps(f"turned{i}", [P, 512]) for i in range(4)]
        count = [ps(f"count{i}", [P, 512]) for i in range(2)]
        pads_set = sem("pads_set")
        consts = sem("consts")
        loaded = sem("loaded")
        cast = sem("cast")
        link = sem("link")
        turned_ready = sem("turned_ready")
        turned_taken = sem("turned_taken")
        passed_ready = sem("passed_ready")
        pick_ready = sem("pick_ready")
        dst_taken = sem("dst_taken")
        count_ready = sem("count_ready")
        newseg_ready = sem("newseg_ready")
        stored = sem("stored")
        LOADS = 4 * 3 + 4 + 2 + 2
        block = ctx.enter_context(nc.Block())
        flat_w = edge_weight.rearrange("e a -> (e a)")

        @block.sync
        def _(sp):
            sp.wait_ge(pads_set, 6)
            for flat, to in ((dst, dst_i), (src, src_i), (edge_type, typ_i), (flat_w, nrm_f)):
                a, b = FULL_J * P * GE, FULL_GROUPS * GE
                sp.dma_start(to[:, 0:FULL_J, :], flat[0:a].rearrange("(j p e) -> p j e", p=P, e=GE)).then_inc(loaded, 16)
                sp.dma_start(to[0:REST, FULL_J, :], flat[a:b].rearrange("(p e) -> p e", e=GE)).then_inc(loaded, 16)
                sp.dma_start(to[REST:REST + 1, FULL_J, 0:TAIL], flat[b:E].rearrange("(a e) -> a e", a=1)).then_inc(loaded, 16)
            last = dst[0:FULL_GROUPS * GE].rearrange("(g e) -> g e", e=GE)[:, GE - 1:GE]
            with nc.allow_non_contiguous_dma(reason="one number of each group"):
                sp.dma_start(before[1:P, 0:1], last[0:P - 1, :]).then_inc(loaded, 16)
                sp.dma_start(before[:, 1:FULL_J], last[P - 1:P * FULL_J - 1, :].rearrange("(j p) a -> p (j a)", p=P)).then_inc(loaded, 16)
                sp.dma_start(before[0:REST + 1, FULL_J:J], last[P * FULL_J - 1:FULL_GROUPS, :]).then_inc(loaded, 16)
                n = E // ROW_E
                sp.dma_start(ends[:, 0, 0:n], dst[0:n * ROW_E].rearrange("(a q e) -> a q e", a=1, e=ROW_E)[:, :, ROW_E - 1]).then_inc(loaded, 16)
                sp.dma_start(ends[:, 1, 0:n], dst[0:n * ROW_E].rearrange("(a q e) -> a q e", a=1, e=ROW_E)[:, :, 0]).then_inc(loaded, 16)
                sp.dma_start(ends[:, 1, n:n + 1], dst[n * ROW_E:n * ROW_E + 1].rearrange("(a q) -> a q", a=1)).then_inc(loaded, 16)
            sp.wait_ge(newseg_ready, 1)
            a = FULL_J * P * GE
            sp.dma_start(newseg_d[0:a].rearrange("(j p e) -> p j e", p=P, e=GE), newseg[:, 0:FULL_J, :]).then_inc(stored, 16)
            sp.dma_start(newseg_d[a:EPAD].rearrange("(p e) -> p e", e=GE), newseg[0:PADROWS, FULL_J, :]).then_inc(stored, 16)
            sp.dma_start(newseg_d[EPAD:EPAD + 1].rearrange("(a e) -> a e", a=1), tail[:, :]).then_inc(stored, 16)
            sp.wait_ge(stored, 48)

        @block.gpsimd
        def _(pool):
            pool.memset(dst_i[:, FULL_J, :], PADNODE).then_inc(pads_set, 1)
            pool.memset(src_i[:, FULL_J, :], 0).then_inc(pads_set, 1)
            pool.memset(typ_i[:, FULL_J, :], 0).then_inc(pads_set, 1)
            pool.memset(nrm_f[:, FULL_J, :], 0.0).then_inc(pads_set, 1)
            pool.memset(before[:, :], PADNODE).then_inc(pads_set, 1)
            pool.memset(ends[:, :, :], PADNODE).then_inc(pads_set, 1)
            pool.memset(t["ident"][:, :], 0.0).then_inc(consts, 1)
            pool.memset(t["identb"][:, :], 0.0).then_inc(consts, 1)
            pool.memset(ones[:, :], 1.0).then_inc(consts, 1)
            pool.memset(t["eps"][:, :], EPS).then_inc(consts, 1)
            pool.memset(tail[:, :], -BIG).then_inc(consts, 1)
            pool.iota(iota_i[:, :], [[1, TSTEPS]], base=0, channel_multiplier=0).then_inc(consts, 1)
            pool.iota(iota_g[:, :], [[P, J]], base=0, channel_multiplier=1).then_inc(consts, 1)
            pool.wait_ge(consts, 2)
            for m in (t["ident"], t["identb"]):
                pool.affine_select(out=m[:, :], in_=m[:, :], compare_op=ALU.not_equal, fill=1.0, base=0,
                                   pattern=[[-1, P]], channel_multiplier=1).then_inc(consts, 1)

        tables = ((dst_f, t["dst"]), (src_f, t["src"]), (rel_f, t["rel"]), (nrm_f, t["norm"]))
        jobs = [(f, to, half, k) for f, to in tables for half in range(2) for k in range(2)]
        spans = [range(max(0, half * HS - BLOCKS + 1) // P, min(J - 1, (half * HS + HS - 1) // P) + 1) for half in range(2)]

        @block.tensor
        def _(pe):
            pe.wait_ge(consts, 9)
            pe.wait_ge(cast, 4)
            pe.wait_ge(loaded, 16 * (LOADS - 2))
            pe.wait_ge(passed_ready, J)
            for half in range(2):
                for j in range(J):
                    rows = P if j < FULL_J else PADROWS
                    last = nc.tensor.matmul(count[half][:, 0:HS], ones[0:rows, :], passed[0:rows, j, half * HS:half * HS + HS],
                                            start=(j == 0), stop=(j == J - 1))
            last.then_inc(count_ready, 1)
            pe.wait_ge(pick_ready, 1)
            for n, (f, to, half, k) in enumerate(jobs):
                if n >= 4:
                    pe.wait_ge(turned_taken if n >= 8 else dst_taken, n - 7 if n >= 8 else n - 3)
                for j in spans[half]:
                    rows = P if j < FULL_J else PADROWS
                    last = nc.tensor.matmul(turned[n % 4][:, 0:HS], f[0:rows, j, k::2], pick[0:rows, j, half * HS:half * HS + HS],
                                            start=(j == spans[half][0]), stop=(j == spans[half][-1]))
                last.then_inc(turned_ready, 1)

        @block.scalar
        def _(act):
            for n, (f, to, half, k) in enumerate(jobs):
                if n < 4:
                    continue
                act.wait_ge(turned_ready, n + 1)
                view = to[:, :].rearrange("p (s k) -> p k s", k=2)[:, k, half * HS:half * HS + HS]
                nc.scalar.activation(view, turned[n % 4][:, 0:HS], ACT.Copy).then_inc(turned_taken, 1)

        @block.vector
        def _(dve):
            n = [0]

            def done(ins):
                n[0] += 1
                ins.then_inc(link, 1)
                dve.wait_ge(link, n[0])

            dve.wait_ge(consts, 9)
            dve.wait_ge(loaded, 16 * (LOADS - 2))
            nc.vector.tensor_copy(t["iota"][:, :], iota_i[:, 0:P])
            nc.vector.tensor_copy(t["iotab"][:, :], iota_i[:, 0:P])
            nc.vector.tensor_copy(dst_f[:, :, :], dst_i[:, :, :]).then_inc(cast, 1)
            nc.vector.tensor_copy(src_f[:, :, :], src_i[:, :, :]).then_inc(cast, 1)
            nc.vector.tensor_copy(beforef[:, :], before[:, :])
            nc.vector.tensor_copy(iota_gf[:, :], iota_g[:, :])
            nc.vector.tensor_copy(endsf[:, :, :], ends[:, :, :])
            nc.vector.tensor_copy(iota_s[:, :], iota_i[:, :]).then_inc(cast, 1)
            done(nc.vector.tensor_scalar(last_blk[:, :], dst_i[:, :, GE - 1], 7, None, ALU.arith_shift_right))
            nc.vector.scalar_tensor_tensor(out=rel_f[:, :, :], in0=typ_i[:, :, :], scalar=float(NPAD), in1=src_f[:, :, :],
                                           op0=ALU.mult, op1=ALU.add).then_inc(cast, 1)
            done(nc.vector.tensor_tensor(key[:, :], last_blk[:, :], iota_gf[:, :], ALU.add))
            for j in range(J):
                rows = P if j < FULL_J else PADROWS
                nc.vector.tensor_scalar(passed[0:rows, j, :], iota_s[0:rows, :], key[0:rows, j:j + 1], None,
                                        ALU.is_gt).then_inc(passed_ready, 1)
            done(nc.vector.tensor_scalar(step128[:, :], iota_s[:, :], float(P), None, ALU.mult))
            dve.wait_ge(count_ready, 1)
            for half in range(2):
                a, b = half * HS, half * HS + HS
                for j in spans[half]:
                    last = nc.vector.tensor_scalar(pick[:, j, a:b], count[half][:, 0:HS], iota_gf[:, j:j + 1], None, ALU.is_equal)
            last.then_inc(pick_ready, 1)
            for half in range(2):
                a, b = half * HS, half * HS + HS
                nc.vector.tensor_copy(grpf[:, a:b], count[half][0:1, 0:HS])
                nc.vector.scalar_tensor_tensor(out=blkf[:, a:b], in0=count[half][0:1, 0:HS], scalar=-1.0, in1=iota_s[0:1, a:b],
                                               op0=ALU.mult, op1=ALU.add)
                done(nc.vector.scalar_tensor_tensor(out=nbase[:, a:b], in0=count[half][:, 0:HS], scalar=-float(P),
                                                    in1=step128[:, a:b], op0=ALU.mult, op1=ALU.add))
            nc.vector.tensor_copy(t["block"][:, :], blkf[:, :])
            nc.vector.tensor_copy(t["group"][:, :], grpf[:, :])
            for m, (f, to, half, k) in enumerate(jobs[0:4]):
                dve.wait_ge(turned_ready, m + 1)
                a, b = half * HS, half * HS + HS
                view = to[:, :].rearrange("p (s k) -> p k s", k=2)[:, k, a:b]
                nc.vector.tensor_tensor(view, turned[m][:, 0:HS], nbase[:, a:b], ALU.subtract).then_inc(dst_taken, 1)
            nc.vector.tensor_tensor(newseg[:, :, 1:GE], dst_f[:, :, 1:GE], dst_f[:, :, 0:GE - 1], ALU.is_equal)
            done(nc.vector.tensor_tensor(newseg[:, :, 0:1], dst_f[:, :, 0:1], beforef[:, :].unsqueeze(2), ALU.is_equal))
            nc.vector.tensor_scalar(newseg[:, :, :], newseg[:, :, :], -1.0, BIG, ALU.add, ALU.mult).then_inc(newseg_ready, 1)
            for way in range(2):
                c = t["chain"][:, way, 0, :]
                done(nc.vector.memset(c, 0.0))
                if way == 0:
                    done(nc.vector.tensor_tensor(c[:, 1:ROWS], endsf[:, 0, 1:ROWS], endsf[:, 0, 0:ROWS - 1], ALU.is_equal))
                else:
                    done(nc.vector.tensor_tensor(c[:, 0:ROWS - 1], endsf[:, 1, 0:ROWS - 1], endsf[:, 1, 1:ROWS], ALU.is_equal))
                done(nc.vector.tensor_scalar(c, c, -1.0, BIG, ALU.add, ALU.mult))
                for h in range(1, H):
                    nc.vector.tensor_copy(t["chain"][:, way, h, :], c)


def blocks_loop(eng, body, last=BLOCKS):
    body(0, 0, 0)
    pairs = (last - 1) // 2
    with eng.Fori(0, pairs) as i:
        body(2 * i + 1, 1, i)
        body(2 * i + 2, 0, i + 1)
    if last > 2 * pairs + 1:
        body(last - 1, 1, pairs)


def node_projections(nc, t, q3, scores, x, wq, wk, wv, k_d, v_d):
    ctx, sb, ps, sem = phase(nc)
    with ctx:
        w = sb("w_qkv", [P, 2, 3 * D])
        xin = sb("xin", [P, 2, D])
        stats = sb("stats", [P, 2, 6])
        mv = sb("mv", [P, 2, 2])
        std = sb("std", [P, 2, 1])
        rstd = sb("rstd", [P, 2, 1])
        xn = sb("xn", [P, 2, D])
        hT = sb("hT", [P, 2, 2, P])
        qs = sb("qs", [P, 2, D])
        qr = sb("qr", [P, 2, D])
        ko = sb("ko", [P, 2, D])
        vo = sb("vo", [P, 2, H, HD1])
        turned = [ps(f"xT{i}", [P, 512]) for i in range(2)]
        qk = [ps(f"qk{i}", [P, 512]) for i in range(2)]
        vv = [ps(f"vv{i}", [P, 512]) for i in range(2)]
        dve_go = sem("dve_go")
        w_in = sem("w_in")
        ones_set = sem("ones_set")
        x_in = sem("x_in", 2)
        mv_ready = sem("mv_ready", 2)
        std_ready = sem("std_ready", 2)
        norm_link = sem("norm_link", 2)
        stat_link = sem("stat_link", 2)
        xn_ready = sem("xn_ready", 2)
        turned_ready = sem("xT_ready", 2)
        hT_ready = sem("hT_ready", 2)
        proj_ready = sem("proj_ready", 2)
        q_link = sem("q_link", 2)
        q_done = sem("q_done", 2)
        kv_ready = sem("kv_ready", 2)
        kv_stored = sem("kv_stored", 2)
        block = ctx.enter_context(nc.Block())

        @block.sync
        def _(sp):
            for i, m in enumerate((wq, wk, wv)):
                sp.dma_start(w[:, :, i * D:(i + 1) * D], m.rearrange("(c p) n -> p c n", p=P)).then_inc(w_in, 16)

            def load(b, s, n, rows=P):
                wait(sp, xn_ready[s], n)
                at = b * P
                sp.dma_start(xin[0:rows, s, :], x[bass.ds(at, rows), :]).then_inc(x_in[s], 16)

            blocks_loop(sp, load, BLOCKS - 1)
            load(BLOCKS - 1, 0, (BLOCKS - 1) // 2, LAST_ROWS)

        @block.gpsimd
        def _(pool):
            pool.memset(vo[:, :, :, HD:HD1], 1.0).then_inc(ones_set, 1)
            pool.wait_ge(ones_set, 1)

            def store(b, s, n):
                pool.wait_ge(kv_ready[s], n + 1)
                pool.dma_start(k_d[bass.ds(b * P, P), :], ko[:, s, :]).then_inc(kv_stored[s], 16)
                pool.dma_start(v_d[bass.ds(b * P, P), :], vo[:, s, :, :].rearrange("p h c -> p (h c)")).then_inc(kv_stored[s], 16)

            blocks_loop(pool, store)
            pool.memset(scores[:, :, :], 0.0)
            pool.wait_ge(kv_stored[0], 32 * (BLOCKS // 2 + 1))
            pool.wait_ge(kv_stored[1], 32 * (BLOCKS // 2))

        def skewed(eng, front, back):
            front(0, 0, 0)
            front(1, 1, 0)
            back(0, 0, 0)
            with eng.Fori(0, (BLOCKS - 3) // 2) as i:
                front(2 * i + 2, 0, i + 1)
                back(2 * i + 1, 1, i)
                front(2 * i + 3, 1, i + 1)
                back(2 * i + 2, 0, i + 1)
            n = (BLOCKS - 1) // 2
            front(BLOCKS - 1, 0, n)
            back(BLOCKS - 2, 1, n - 1)
            back(BLOCKS - 1, 0, n)

        @block.vector
        def _(dve):
            def front(b, s, n):
                hold(dve, x_in[s], 16 * (n + 1), dve_go)
                nc.vector.bn_stats(stats[:, s, :], xin[:, s, :]).then_inc(stat_link[s], 1)
                hold(dve, stat_link[s], n + 1, dve_go)
                nc.vector.bn_aggr(mv[:, s, :], stats[:, s, :]).then_inc(mv_ready[s], 1)
                dve.wait_ge(std_ready[s], n + 1)
                nc.vector.reciprocal(rstd[:, s, :], std[:, s, :]).then_inc(norm_link[s], 1)
                dve.wait_ge(norm_link[s], n + 1)
                nc.vector.tensor_scalar(xn[:, s, :], xin[:, s, :], mv[:, s, 0:1], rstd[:, s, :],
                                        ALU.subtract, ALU.mult).then_inc(xn_ready[s], 1)

            def back(b, s, n):
                dve.wait_ge(proj_ready[s], n + 1)
                q = qk[s][:, 0:D]
                scale = HD ** -0.5
                q0, q1, q2 = (q3[:, bass.ds(b, 1), i, :].rearrange("p a d -> p (a d)") for i in range(3))
                nc.vector.tensor_scalar(qs[:, s, :], q, scale, None, ALU.mult).then_inc(q_link[s], 1)
                dve.wait_ge(q_link[s], 5 * n + 1)
                nc.vector.tensor_copy(q0, qs[:, s, :]).then_inc(q_link[s], 1)
                dve.wait_ge(q_link[s], 5 * n + 2)
                nc.vector.tensor_tensor(qr[:, s, :], qs[:, s, :], q0, ALU.subtract).then_inc(q_link[s], 1)
                dve.wait_ge(q_link[s], 5 * n + 3)
                nc.vector.tensor_copy(q1, qr[:, s, :]).then_inc(q_link[s], 1)
                dve.wait_ge(q_link[s], 5 * n + 4)
                nc.vector.tensor_tensor(q2, qr[:, s, :], q1, ALU.subtract).then_inc(q_link[s], 1)

            skewed(dve, front, back)

        @block.scalar
        def _(act):
            def front(b, s, n):
                act.wait_ge(mv_ready[s], n + 1)
                nc.scalar.activation(std[:, s, :], mv[:, s, 1:2], ACT.Sqrt, bias=t["eps"][:, 0:1]).then_inc(std_ready[s], 1)
                act.wait_ge(turned_ready[s], n + 1)
                nc.scalar.activation(hT[:, s, :, :], turned[s][:, 0:2 * P].rearrange("p (c n) -> p c n", c=2),
                                     ACT.Relu).then_inc(hT_ready[s], 1)

            def back(b, s, n):
                act.wait_ge(proj_ready[s], n + 1)
                act.wait_ge(q_link[s], 5 * n + 1)
                wait(act, kv_stored[s], 32 * n)
                if isinstance(b, int) and b == 0:
                    act.wait_ge(ones_set, 1)
                nc.scalar.activation(ko[:, s, :], qk[s][:, D:2 * D], ACT.Copy)
                nc.scalar.activation(vo[:, s, :, 0:HD], vv[s][:, 0:D].rearrange("p (h c) -> p h c", h=H),
                                     ACT.Copy).then_inc(kv_ready[s], 1)

            skewed(act, front, back)

        @block.tensor
        def _(pe):
            pe.wait_ge(w_in, 48)

            def front(b, s, n):
                pe.wait_ge(xn_ready[s], n + 1)
                for c in range(2):
                    last = nc.tensor.transpose(turned[s][:, c * P:(c + 1) * P], xn[:, s, c * P:(c + 1) * P], t["ident"][:, :])
                last.then_inc(turned_ready[s], 1)

            def back(b, s, n):
                pe.wait_ge(hT_ready[s], n + 1)
                wait(pe, q_link[s], 5 * n)
                wait(pe, kv_ready[s], n)
                for c in range(2):
                    nc.tensor.matmul(qk[s][:, :], hT[:, s, c, :], w[:, c, 0:2 * D], start=(c == 0), stop=(c == 1))
                for c in range(2):
                    last = nc.tensor.matmul(vv[s][:, 0:D], hT[:, s, c, :], w[:, c, 2 * D:3 * D], start=(c == 0), stop=(c == 1))
                last.then_inc(proj_ready[s], 1)

            skewed(pe, front, back)


IN_RANGE = "the chip counts these tables' blocks and groups up to the last and no further"


def block_of(nc, eng, t, s):
    return nc.values_load(t["block"][0:1, bass.ds(s, 1)], engines=(eng.engine,), min_val=0, max_val=BLOCKS - 1,
                          skip_runtime_bounds_check_because=IN_RANGE)


def group_of(nc, eng, t, s, past=0):
    return nc.values_load(t["group"][0:1, bass.ds(s, 1)], engines=(eng.engine,), min_val=0, max_val=GROUPS - 1 + past,
                          skip_runtime_bounds_check_because=IN_RANGE)


def edge_scores(nc, t, q3, scores, edge_attr, w1, b1, w2, b2, k_d, mlp_d):
    ctx, sb, ps, sem = phase(nc)
    with ctx:
        w1s = sb("w1s", [P, D])
        w2s = sb("w2s", [P, 2, MW])
        b1s = sb("b1s", [P, 2])
        b2s = sb("b2s", [U * H, 1])
        raw = sb("ef_raw", [P, U, P])
        efT = sb("efT", [P, U, P])
        hid = sb("hid", [P, 2, U, P])
        onehot = sb("onehot", [P, U, 2, P], BF16)
        ohT = sb("ohT", [P, U, 2, P], BF16)
        idx = sb("idx", [P, U, 2], I32)
        rows = sb("k_rows", [P, U, 2, D])
        prod = sb("prod", [P, 2, H, HD])
        red = sb("red", [P, 2, H])
        mlp = sb("mlp", [U * H, P, 2])
        p_ef = ps("p_ef", [P, 512])
        p_hid = [ps(f"p_hid{i}", [P, 512]) for i in range(2)]
        p_mlp = ps("p_mlp", [P, 512])
        p_ohT = [ps(f"p_ohT{i}", [P, 1024], BF16) for i in range(2)]
        p_q = [ps(f"p_q{i}", [P, 512]) for i in range(2)]
        w_in = sem("w1_in")
        ef_in = sem("ef_in")
        ef_turned = sem("ef_turned")
        efT_ready = sem("efT_ready")
        hid_done = sem("hid_done", U)
        hid_ready = sem("hid_ready", U)
        mlp_done = sem("mlp_done")
        mlp_taken = sem("mlp_taken")
        mlp_stored = sem("mlp_stored")
        w2_cleared = sem("w2_cleared")
        onehot_ready = sem("onehot_ready", U)
        ohT_done = sem("ohT_done", U)
        ohT_ready = sem("ohT_ready", U)
        q_done = sem("q_rows_done", U)
        idx_ready = sem("idx_ready", U)
        gathered = sem("gathered", U)
        prod_done = sem("prod_done", U)
        red_done = sem("red_done", U)
        pool_go = sem("pool_go")
        block = ctx.enter_context(nc.Block())
        chunks = edge_attr[0:FULL_GROUPS * GE, :].rearrange("(g p k) f -> p g (k f)", p=P, k=2)

        @block.sync
        def _(sp):
            for k in range(2):
                sp.dma_start(w1s[k * FE:(k + 1) * FE, :], w1[:, :]).then_inc(w_in, 16)
            sp.wait_ge(w2_cleared, 1)
            sp.dma_start(w2s[:, :, MW0:MW0 + H], w2.rearrange("(c p) h -> p c h", p=P)).then_inc(w_in, 16)
            with nc.allow_non_contiguous_dma(reason="256 numbers"):
                sp.dma_start(b1s[:, :], b1.rearrange("(c p) -> p c", p=P)).then_inc(w_in, 16)
                for g in range(U):
                    sp.dma_start(b2s[g * H:(g + 1) * H, :], b2.rearrange("(h a) -> h a", a=1)).then_inc(w_in, 16)

            def load(c):
                wait(sp, ef_turned, c)
                sp.dma_start(raw[:, :, :], chunks[:, bass.ds(U * c, U), :]).then_inc(ef_in, 16)

            def store(c):
                sp.wait_ge(mlp_taken, c + 1)
                sp.dma_start(mlp_d[bass.ds(U * H * c, U * H), :], mlp[:, :, :].rearrange("r p k -> r (p k)")).then_inc(mlp_stored, 16)

            for c in range(3):
                load(c)
            with sp.Fori(0, CHUNKS - 4) as c:
                store(c)
                load(c + 3)
            store(CHUNKS - 4)
            sp.wait_ge(ef_turned, CHUNKS - 1)
            g = U * (CHUNKS - 1)
            sp.dma_start(raw[:, 0:FULL_GROUPS - g, :], chunks[:, g:FULL_GROUPS, :]).then_inc(ef_in, 16)
            sp.dma_start(raw[0:TAIL // 2, FULL_GROUPS - g, :],
                         edge_attr[FULL_GROUPS * GE:E, :].rearrange("(p k) f -> p (k f)", k=2)).then_inc(ef_in, 16)
            for c in range(CHUNKS - 3, CHUNKS):
                store(c)
            sp.wait_ge(mlp_stored, 16 * CHUNKS)

        @block.gpsimd
        def _(pool):
            pool.memset(w2s[:, :, :], 0.0).then_inc(w2_cleared, 1)

            def gather(i, u):
                wait(pool, prod_done[u], i)
                hold(pool, idx_ready[u], i + 1, pool_go)
                for k in range(2):
                    pool.indirect_dma_start(rows[:, u, k, :], None, k_d[:, :],
                                            bass.IndirectOffsetOnAxis(idx[:, u, k:k + 1], 0)).then_inc(gathered[u], 16)

            for u in range(U):
                gather(0, u)
            with pool.Fori(1, ITERS) as i:
                for u in range(U):
                    gather(i, u)

        @block.scalar
        def _(act):
            def take_ef():
                nc.scalar.activation(efT[:, :, :], p_ef[:, :].rearrange("p (g e) -> p g e", g=U), ACT.Copy).then_inc(efT_ready, 1)

            def take_hidden(i, u, n):
                act.wait_ge(hid_done[u], n + 1)
                nc.scalar.activation(hid[:, u % 2, :, :], p_hid[u % 2][:, :].rearrange("p (g e) -> p g e", g=U), ACT.Relu,
                                     bias=b1s[:, u % 2:u % 2 + 1]).then_inc(hid_ready[u], 1)

            def next_idx(i, u, n):
                wait(act, gathered[u], 32 * n)
                s = U * i + u
                nc.scalar.activation(idx[:, u, :], t["src"][:, bass.ds(2 * s, 2)], ACT.Copy).then_inc(idx_ready[u], 1)

            def take_onehot(u, n):
                act.wait_ge(ohT_done[u], n + 1)
                nc.scalar.activation(ohT[:, u, :, :], p_ohT[u % 2][:, 0:2 * P].rearrange("p (k n) -> p k n", k=2),
                                     ACT.Copy).then_inc(ohT_ready[u], 1)

            def take_mlp(c):
                act.wait_ge(mlp_done, c + 1)
                wait(act, mlp_stored, 16 * c)
                nc.scalar.activation(mlp[:, :, :].rearrange("r p k -> r k p"),
                                     p_mlp[0:U * H, 0:2 * P].rearrange("r (k p) -> r k p", k=2),
                                     ACT.Identity, bias=b2s[:, :]).then_inc(mlp_taken, 1)

            def iteration(i, hidden, mlp=True, features=True):
                for u in range(U):
                    take_onehot((u + 1) % U, i + (u + 1) // U)
                    if mlp and u == 0:
                        take_mlp(i)
                    if hidden:
                        take_hidden(i, u, i + 1)
                        if u == U - 1 and features:
                            act.wait_ge(ef_turned, i + 3)
                            take_ef()
                    next_idx(i + 1, u, i + 1)

            for u in range(U):
                next_idx(0, u, 0)
            act.wait_ge(w_in, WIN)
            act.wait_ge(ef_turned, 1)
            take_ef()
            for u in range(U):
                take_hidden(0, u, 0)
            act.wait_ge(ef_turned, 2)
            take_ef()
            take_onehot(0, 0)
            iteration(0, True)
            with act.Fori(1, CHUNKS - 2) as i:
                iteration(i, True)
            iteration(CHUNKS - 2, True, features=False)
            iteration(CHUNKS - 1, False)
            with act.Fori(CHUNKS, ITERS) as i:
                iteration(i, False, mlp=False)

        @block.tensor
        def _(pe):
            def turn_ef(c):
                pe.wait_ge(ef_in, 16 * (c + 1) if not (isinstance(c, int) and c == CHUNKS - 1) else 16 * (CHUNKS + 1))
                for g in range(U):
                    last = nc.tensor.transpose(p_ef[:, g * P:(g + 1) * P], raw[:, g, :], t["ident"][:, :])
                last.then_inc(ef_turned, 1)

            def hidden(c, u):
                k, half = divmod(u, 2)
                if u == 0:
                    pe.wait_ge(efT_ready, c + 1)
                nc.tensor.matmul(p_hid[half][:, :], w1s[k * FE:(k + 1) * FE, half * P:(half + 1) * P],
                                 efT[k * FE:(k + 1) * FE, :, :], start=True, stop=True).then_inc(hid_done[u], 1)

            def mlp_out(c, u):
                k, half = divmod(u, 2)
                pe.wait_ge(hid_ready[u], c + 1)
                if u == 0:
                    wait(pe, mlp_taken, c)
                for g in range(U):
                    last = nc.tensor.matmul(p_mlp[0:U * H, k * P:(k + 1) * P], w2s[:, half, MW0 - g * H:MW0 + (U - g) * H],
                                            hid[:, half, g, :], start=(half == 0 and g == 0), stop=(half == 1 and g == U - 1))
                if u == U - 1:
                    last.then_inc(mlp_done, 1)

            def turn_onehot(u, n):
                pe.wait_ge(onehot_ready[u], n + 1)
                for k in range(2):
                    last = nc.tensor.transpose(p_ohT[u % 2][:, k * P:(k + 1) * P], onehot[:, u, k, :], t["identb"][:, :])
                last.then_inc(ohT_done[u], 1)

            def iteration(i, next_chunk, turn=True, drain=True):
                for u in range(U):
                    turn_onehot((u + 1) % U, i + (u + 1) // U)
                    if u == 0 and drain:
                        mlp_out(i, U - 1)
                    if next_chunk:
                        if u:
                            mlp_out(i + 1, u - 1)
                        hidden(i + 1, u)
                        if u == U - 1 and turn:
                            turn_ef(i + 2)
                    b = block_of(nc, pe, t, U * i + u)
                    pe.wait_ge(ohT_ready[u], i + 1)
                    for k in range(2):
                        for part in range(3):
                            last = nc.tensor.matmul(p_q[u % 2][:, k * D:(k + 1) * D], ohT[:, u, k, :],
                                                    q3[:, bass.ds(b, 1), part, :], start=(part == 0), stop=(part == 2))
                    last.then_inc(q_done[u], 1)

            pe.wait_ge(w_in, WIN)
            turn_ef(0)
            for u in range(U):
                hidden(0, u)
                if u:
                    mlp_out(0, u - 1)
            turn_ef(1)
            turn_onehot(0, 0)
            iteration(0, True)
            with pe.Fori(1, CHUNKS - 3) as i:
                iteration(i, True)
            iteration(CHUNKS - 3, True)
            iteration(CHUNKS - 2, True, turn=False)
            iteration(CHUNKS - 1, False)
            with pe.Fori(CHUNKS, ITERS) as i:
                iteration(i, False, drain=False)

        @block.vector
        def _(dve):
            def make_onehot(s, u, k):
                return nc.vector.tensor_scalar(onehot[:, u, k, :], t["iotab"][:, :], t["dst"][:, bass.ds(2 * s + k, 1)], None,
                                               ALU.is_equal)

            def iteration(i):
                for u in range(U):
                    s = U * i + u
                    g = group_of(nc, dve, t, s)
                    ahead, v = s + 3, (u + 3) % U
                    dve.wait_ge(q_done[u], i + 1)
                    dve.wait_ge(gathered[u], 32 * (i + 1))
                    nc.vector.tensor_tensor(prod[:, :, :, :].rearrange("p k h c -> p (k h c)"), p_q[u % 2][:, :],
                                            rows[:, u, :, :].rearrange("p k d -> p (k d)"), ALU.mult).then_inc(prod_done[u], 1)
                    make_onehot(ahead, v, 0)
                    dve.wait_ge(prod_done[u], i + 1)
                    nc.vector.tensor_reduce(red[:, :, :].rearrange("p k h -> p (k h)"),
                                            prod[:, :, :, :].rearrange("p k h c -> p (k h) c"), AX.X, ALU.add).then_inc(red_done[u], 1)
                    make_onehot(ahead, v, 1).then_inc(onehot_ready[v], 1)
                    dve.wait_ge(red_done[u], i + 1)
                    to = scores[:, bass.ds(2 * g, 2), :]
                    nc.vector.tensor_tensor(to, to, red[:, :, :], ALU.add)

            for s in range(3):
                make_onehot(s, s, 0)
                make_onehot(s, s, 1).then_inc(onehot_ready[s], 1)
            iteration(0)
            with dve.Fori(1, ITERS) as i:
                iteration(i)


def softmax_numerators(nc, t, scores, newseg_d, mlp_d):
    ctx, sb, ps, sem = phase(nc)
    PIECES = 7
    PL = ROW_E // PIECES
    MLP_PIECES = [(0, ROW_GROUPS)]
    with ctx:
        sT = sb("sT", [P, ROW_GROUPS, P, 2])
        mx = sb("mx", [P, ROW_E])
        pen = sb("pen", [P, 2, PL + 1])
        stage = sb("stage", [P, 2, 2, P])
        line = sb("line", [1, 4, P])
        carry = sb("carry", [P, 2])
        turned = [ps(f"sturn{i}", [P, 512]) for i in range(2)]
        small = ps("small", [P, 512])
        small2 = ps("small2", [P, 512])
        stage_ready = sem("stage_ready", 2)
        turned_ready = sem("sturned_ready", 2)
        turned_taken = sem("sturned_taken", 2)
        back_staged = sem("back_staged", 2)
        back_turned = sem("back_turned", 2)
        back_taken = sem("back_taken", 2)
        pen_in = sem("pen_in", 2)
        mlp_in = sem("mlp_in", 1)
        scanned = sem("scanned")
        line_ready = sem("line_ready")
        small_ready = sem("small_ready")
        link = sem("mlink")
        shifted = sem("shifted")
        block = ctx.enter_context(nc.Block())
        by_j = scores[:, :, :].rearrange("p (q j k) h -> p q j k h", q=ROWS, j=ROW_GROUPS)
        flat = sT[:, :, :, :].rearrange("r j p k -> r (j p k)")
        passes = [("f", range(PIECES)), ("f", range(PIECES)), ("b", range(PIECES - 1, -1, -1)), ("b", range(PIECES - 1, -1, -1))]
        plan = [(n, way, c) for n, (way, order) in enumerate(passes) for c in order]

        @block.sync
        def _(sp):
            by_row = mlp_d.rearrange("(q j h) e -> q h j e", q=ROWS, h=H)
            for i, (a, b) in enumerate(MLP_PIECES):
                for q in range(ROWS):
                    sp.dma_start(sT[q * H:(q + 1) * H, a:b, :, :].rearrange("r j p k -> r j (p k)"),
                                 by_row[q:q + 1, :, a:b, :].rearrange("q h j e -> (q h) j e")).then_inc(mlp_in[i], 16)
            for m, (n, way, c) in enumerate(plan):
                if m >= 2:
                    sp.wait_ge(scanned, m - 1)
                for q in range(ROWS):
                    a = q * ROW_E + c * PL
                    sp.dma_start(pen[q * H:(q + 1) * H, m % 2, :],
                                 newseg_d[a:a + PL + 1].rearrange("(a e) -> a e", a=1).to_broadcast([H, PL + 1])).then_inc(pen_in[m % 2], 16)

        @block.scalar
        def _(act):
            def stage_in(j, s, n):
                wait(act, turned_ready[s], n)
                nc.scalar.activation(stage[:, s, :, :].rearrange("p k (q h) -> p k q h", h=H),
                                     by_j[:, :, bass.ds(j, 1), :, :].rearrange("p q j k h -> p (j k) q h"),
                                     ACT.Copy).then_inc(stage_ready[s], 1)

            blocks_loop(act, stage_in)

            def stage_back(j, s, n):
                wait(act, back_turned[s], n)
                nc.scalar.activation(stage[:, s, :, :],
                                     sT[:, bass.ds(j, 1), :, :].rearrange("r j p k -> r (j k) p"),
                                     ACT.Exp).then_inc(back_staged[s], 1)

            act.wait_ge(shifted, 1)
            blocks_loop(act, stage_back)

        @block.tensor
        def _(pe):
            def turn(j, s, n):
                pe.wait_ge(stage_ready[s], n + 1)
                wait(pe, turned_taken[s], n)
                for k in range(2):
                    last = nc.tensor.transpose(turned[s][:, k * P:(k + 1) * P], stage[:, s, k, :], t["ident"][:, :])
                last.then_inc(turned_ready[s], 1)

            blocks_loop(pe, turn)
            for way in range(2):
                pe.wait_ge(line_ready, 3 * way + 1)
                nc.tensor.transpose(small[0:1, 0:P], carry[:, 0:1], t["ident"][:, :]).then_inc(small_ready, 1)
                pe.wait_ge(line_ready, 3 * way + 2)
                nc.tensor.transpose(small2[:, 0:1], line[:, 3, :], t["ident"][0:1, 0:1]).then_inc(small_ready, 1)

            def turn_back(j, s, n):
                pe.wait_ge(back_staged[s], n + 1)
                wait(pe, back_taken[s], n)
                for k in range(2):
                    last = nc.tensor.transpose(turned[s][:, k * P:(k + 1) * P], stage[:, s, k, :], t["ident"][:, :])
                last.then_inc(back_turned[s], 1)

            blocks_loop(pe, turn_back)

        @block.vector
        def _(dve):
            def take(j, s, n):
                dve.wait_ge(turned_ready[s], n + 1)
                to = sT[:, bass.ds(j, 1), :, :].rearrange("r j p k -> r (j k) p")
                nc.vector.tensor_tensor(to, to, turned[s][:, 0:2 * P].rearrange("r (k p) -> r k p", k=2),
                                        ALU.add).then_inc(turned_taken[s], 1)

            dve.wait_ge(mlp_in[0], 16 * ROWS)
            blocks_loop(dve, take)
            dve.wait_ge(turned_taken[0], BLOCKS // 2 + 1)
            dve.wait_ge(turned_taken[1], BLOCKS // 2)
            cnt = [0]

            def done(ins):
                cnt[0] += 1
                ins.then_inc(link, 1)
                dve.wait_ge(link, cnt[0])

            for m, (n, way, c) in enumerate(plan):
                a, b = c * PL, (c + 1) * PL
                dve.wait_ge(pen_in[m % 2], 16 * ROWS * (m // 2 + 1))
                if m:
                    dve.wait_ge(scanned, m)
                first = c == (0 if way == "f" else PIECES - 1)
                if way == "f":
                    init = (-BIG if n == 0 else carry[:, 1:2]) if first else mx[:, a - 1:a]
                    nc.vector.tensor_tensor_scan(mx[:, a:b], pen[:, m % 2, 0:PL], flat[:, a:b] if n == 0 else mx[:, a:b], init,
                                                 ALU.add, ALU.max).then_inc(scanned, 1)
                else:
                    init = (-BIG if n == 2 else carry[:, 1:2]) if first else mx[:, b:b + 1]
                    nc.vector.tensor_tensor_scan(mx[:, a:b][:, ::-1], pen[:, m % 2, 1:PL + 1][:, ::-1], mx[:, a:b][:, ::-1], init,
                                                 ALU.add, ALU.max).then_inc(scanned, 1)
                if m % PIECES == PIECES - 1 and n in (0, 2):
                    w = 0 if n == 0 else 1
                    edge = mx[:, ROW_E - 1:ROW_E] if n == 0 else mx[:, 0:1]
                    dve.wait_ge(scanned, m + 1)
                    nc.vector.tensor_copy(carry[:, 0:1], edge).then_inc(line_ready, 1)
                    dve.wait_ge(small_ready, 2 * w + 1)
                    done(nc.vector.tensor_copy(line[:, 0, :].rearrange("a (h q) -> a h q", h=H),
                                               small[0:1, 0:P].rearrange("a (q h) -> a h q", h=H)))
                    pens = t["chain"][:, w, :, :].rearrange("a h q -> a (h q)")
                    step = 1 if n == 0 else -1
                    done(nc.vector.tensor_tensor_scan(line[:, 1, ::step], pens[:, ::step], line[:, 0, ::step], -BIG, ALU.add, ALU.max))
                    done(nc.vector.memset(line[:, 3, :], -BIG))
                    by_q = line[:, 3, :].rearrange("a (q h) -> a h q", h=H)
                    got = line[:, 1, :].rearrange("a (h q) -> a h q", h=H)
                    if n == 0:
                        nc.vector.tensor_copy(by_q[:, :, 1:ROWS], got[:, :, 0:ROWS - 1]).then_inc(line_ready, 1)
                    else:
                        nc.vector.tensor_copy(by_q[:, :, 0:ROWS - 1], got[:, :, 1:ROWS]).then_inc(line_ready, 1)
                    dve.wait_ge(small_ready, 2 * w + 2)
                    nc.vector.tensor_copy(carry[:, 1:2], small2[:, 0:1]).then_inc(line_ready, 1)
                    dve.wait_ge(line_ready, 3 * w + 3)
            dve.wait_ge(scanned, len(plan))
            nc.vector.tensor_tensor(flat, flat, mx[:, :], ALU.subtract).then_inc(shifted, 1)

            def take_back(j, s, n):
                dve.wait_ge(back_turned[s], n + 1)
                nc.vector.tensor_copy(by_j[:, :, bass.ds(j, 1), :, :].rearrange("p q j k h -> p (j k) q h"),
                                      turned[s][:, 0:2 * P].rearrange("p (k q h) -> p k q h", k=2, h=H)).then_inc(back_taken[s], 1)

            blocks_loop(dve, take_back)


def edge_sums(nc, t, name, table, width, index, acc, weigh, weigh_engine, extra=None):
    ctx, sb, ps, sem = phase(nc)
    with ctx:
        onehot = sb(name + "oh", [P, U, 2, P])
        idx = sb(name + "idx", [P, U, 2], I32)
        rows = sb(name + "rows", [P, U, 2, width])
        wrows = sb(name + "wrows", [P, U, 2, width])
        sums = [ps(f"{name}sums{i}", [P, 512]) for i in range(U)]
        onehot_ready = sem(name + "oh_ready", U)
        idx_ready = sem(name + "idx_ready", U)
        gathered = sem(name + "gathered", U)
        weighed = sem(name + "weighed", U)
        summed = sem(name + "summed", U)
        added = sem(name + "added", U)
        cleared = sem(name + "cleared")
        pool_go = sem(name + "pool_go")
        block = ctx.enter_context(nc.Block())

        def iterations(eng, body):
            body(0)
            with eng.Fori(1, ITERS) as i:
                body(i)

        @block.gpsimd
        def _(pool):
            def body(i):
                for u in range(U):
                    wait(pool, weighed[u], i)
                    hold(pool, idx_ready[u], i + 1, pool_go)
                    for k in range(2):
                        pool.indirect_dma_start(rows[:, u, k, :], None, table[:, :],
                                                bass.IndirectOffsetOnAxis(idx[:, u, k:k + 1], 0)).then_inc(gathered[u], 16)

            iterations(pool, body)

        def do_weigh(eng, i, u, s):
            eng.wait_ge(gathered[u], 32 * (i + 1))
            wait(eng, summed[u], i)
            weigh(wrows[:, u, :, :], rows[:, u, :, :], s).then_inc(weighed[u], 1)

        @block.scalar
        def _(act):
            def next_idx(i, u, n):
                wait(act, gathered[u], 32 * n)
                s = U * i + u
                nc.scalar.activation(idx[:, u, :], index[:, bass.ds(2 * s, 2)], ACT.Copy).then_inc(idx_ready[u], 1)

            def body(i):
                for u in range(U):
                    if weigh_engine == "scalar":
                        do_weigh(act, i, u, U * i + u)
                    next_idx(i + 1, u, i + 1)

            for u in range(U):
                next_idx(0, u, 0)
            iterations(act, body)

        @block.tensor
        def _(pe):
            def body(i):
                for u in range(U):
                    pe.wait_ge(onehot_ready[u], i + 1)
                    pe.wait_ge(weighed[u], i + 1)
                    wait(pe, added[u], i)
                    for k in range(2):
                        last = nc.tensor.matmul(sums[u][:, 0:width], onehot[:, u, k, :], wrows[:, u, k, :],
                                                start=(k == 0), stop=(k == 1))
                    last.then_inc(summed[u], 1)

            iterations(pe, body)

        @block.vector
        def _(dve):
            def prepare(s, u, i):
                wait(dve, summed[u], i)
                for k in range(2):
                    last = nc.vector.tensor_scalar(onehot[:, u, k, :], t["iota"][:, :], t["dst"][:, bass.ds(2 * s + k, 1)],
                                                   None, ALU.is_equal)
                last.then_inc(onehot_ready[u], 1)
                if weigh_engine == "vector":
                    do_weigh(dve, i, u, s)

            def add(s, u, i):
                b = block_of(nc, dve, t, s)
                dve.wait_ge(summed[u], i + 1)
                if u > 0:
                    dve.wait_ge(added[u - 1], i + 1)
                else:
                    wait(dve, added[U - 1], i)
                to = acc[:, bass.ds(b, 1), :]
                nc.vector.tensor_tensor(to, to, sums[u][:, 0:width].unsqueeze(1), ALU.add).then_inc(added[u], 1)

            nc.vector.memset(acc[:, :, :], 0.0).then_inc(cleared, 1)
            dve.wait_ge(cleared, 1)
            for u in range(U):
                prepare(u, u, 0)
                if u:
                    add(u - 1, u - 1, 0)
            with dve.Fori(1, ITERS) as i:
                for u in range(U):
                    prepare(U * i + u, u, i)
                    if u:
                        add(U * i + u - 1, u - 1, i)
                    else:
                        add(U * i - 1, U - 1, i - 1)
            add(STEPS - 1, U - 1, ITERS - 1)
            dve.wait_ge(added[U - 1], ITERS)


def weighted_sums(nc, t, scores, att, v_d):
    def weigh(out, rows, s):
        g = group_of(nc, nc.vector, t, s)
        return nc.vector.tensor_tensor(
            out.rearrange("p k (h c) -> p (k h) c", h=H), rows.rearrange("p k (h c) -> p (k h) c", h=H),
            scores[:, bass.ds(2 * g, 2), :].rearrange("p k h -> p (k h)").unsqueeze(2).to_broadcast([P, 2 * H, HD1]), ALU.mult)

    edge_sums(nc, t, "v_", v_d, H * HD1, t["src"], att[:, :, :, :].rearrange("p b h c -> p b (h c)"), weigh, "vector")


def messages(nc, t, att, x1, x, wo, bo, rel_w, gate_w, msg_d):
    ctx, sb, ps, sem = phase(nc)
    QUARTERS = 4
    with ctx:
        wos = sb("wos", [P, 2, D])
        bos = sb("bos", [P, D])
        wr = sb("wr", [P, 2, RELS, D])
        gw = sb("gw", [P, 2, RELS])
        xin = sb("x_res", [P, 2, D])
        den = sb("den", [P, H, 1])
        rden = sb("rden", [P, H, 1])
        o = sb("o", [P, H, HD])
        oT = sb("oT", [P, 2, P])
        stats = sb("stats1", [P, 6])
        mv = sb("mv1", [P, 2])
        std = sb("std1", [P, 1])
        rstd = sb("rstd1", [P, 1])
        xn = sb("xn1", [P, D])
        hT = sb("h1T", [P, 2, 2, P])
        gate = sb("gate", [P, 2, RELS])
        msg = sb("msg", [P, RELS, D])
        p_oT = ps("p_oT", [P, 512])
        p_o = ps("p_o", [P, 512])
        p_xT = ps("p_xT", [P, 512])
        p_g = ps("p_g", [P, 512])
        p_m = [ps(f"p_m{i}", [P, 512]) for i in range(4)]
        dve_go = sem("dve_go1")
        w_in = sem("wr_in")
        x_in = sem("xr_in", 2)
        xb_ready = sem("xb_ready", 2)
        den_link = sem("den_link")
        o_ready = sem("o_ready")
        oT_done = sem("oT_done")
        oT_ready = sem("oT_ready")
        wo_done = sem("wo_done")
        x1_ready = sem("x1_ready")
        ln_link = sem("ln_link")
        std_ready = sem("std1_ready")
        xn_ready = sem("xn1_ready")
        xT_done = sem("xT_done")
        hT_ready = sem("h1T_ready")
        gate_done = sem("gate_done")
        gate_ready = sem("gate_ready")
        msg_done = sem("msg_done", 4)
        msg_taken = sem("msg_taken", 4)
        msg_stored = sem("msg_stored", QUARTERS)
        block = ctx.enter_context(nc.Block())
        table = msg_d.rearrange("(r n) d -> n r d", r=RELS)

        def all_blocks(eng, front, back, ends=None):
            front(0, 0, 0)
            back(0, 0, 0, True)
            with eng.Fori(0, (BLOCKS - 3) // 2) as i:
                back(2 * i + 1, 1, i, True)
                back(2 * i + 2, 0, i + 1, True)
            back(BLOCKS - 2, 1, (BLOCKS - 3) // 2, True)
            back(BLOCKS - 1, 0, (BLOCKS - 1) // 2, False)

        @block.sync
        def _(sp):
            sp.dma_start(wos[:, :, :], wo.rearrange("(c p) n -> p c n", p=P)).then_inc(w_in, 16)
            sp.dma_start(bos[:, :], bo.rearrange("(a n) -> a n", a=1).to_broadcast([P, D])).then_inc(w_in, 16)
            for c in range(2):
                sp.dma_start(wr[:, c, :, :], rel_w[:, c * P:(c + 1) * P, :].rearrange("r p n -> p r n")).then_inc(w_in, 16)
            with nc.allow_non_contiguous_dma(reason="4096 numbers"):
                for c in range(2):
                    sp.dma_start(gw[:, c, :], gate_w[:, c * P:(c + 1) * P, :].rearrange("r p a -> p (r a)")).then_inc(w_in, 16)

            def load(b, s, n, rows=P):
                wait(sp, x1_ready, b - 1)
                sp.dma_start(xin[0:rows, s, :], x[bass.ds(b * P, rows), :]).then_inc(x_in[s], 16)

            def store(b):
                for q in range(QUARTERS):
                    use = 2 * b + q // 2
                    sp.wait_ge(msg_taken[2 * (q % 2)], use + 1)
                    sp.wait_ge(msg_taken[2 * (q % 2) + 1], use + 1)
                    sp.dma_start(table[bass.ds(b * P, P), 4 * q:4 * q + 4, :], msg[:, 4 * q:4 * q + 4, :]).then_inc(msg_stored[q], 16)

            load(0, 0, 0)
            load(1, 1, 0)
            store(0)
            with sp.Fori(0, (BLOCKS - 3) // 2) as i:
                load(2 * i + 2, 0, i + 1)
                store(2 * i + 1)
                load(2 * i + 3, 1, i + 1)
                store(2 * i + 2)
            load(BLOCKS - 1, 0, BLOCKS // 2, LAST_ROWS)
            store(BLOCKS - 2)
            store(BLOCKS - 1)
            for q in range(QUARTERS):
                sp.wait_ge(msg_stored[q], 16 * BLOCKS)

        @block.gpsimd
        def _(pool):
            pool.wait_ge(w_in, 96)

            def add_bias(b, s, n):
                pool.wait_ge(x_in[s], 16 * (n + 1))
                nc.gpsimd.tensor_tensor(xin[:, s, :], xin[:, s, :], bos[:, :], ALU.add).then_inc(xb_ready[s], 1)

            blocks_loop(pool, add_bias)

        def front_of(pieces):
            def front(b, s, n):
                for piece in pieces:
                    piece(b, s, n)
            return front

        def next_of(b, s, n):
            return (b + 1, 1 - s, n if s == 0 else n + 1)

        @block.vector
        def _(dve):
            def normalise(b, s, n):
                a = att[:, bass.ds(b, 1), :, :].rearrange("p b h c -> p (b h) c")
                nc.vector.tensor_scalar(den[:, :, :], a[:, :, HD:HD1], 1.0e-30, None, ALU.max).then_inc(den_link, 1)
                dve.wait_ge(den_link, 2 * b + 1)
                nc.vector.reciprocal(rden[:, :, :], den[:, :, :]).then_inc(den_link, 1)
                dve.wait_ge(den_link, 2 * b + 2)
                nc.vector.tensor_tensor(o[:, :, :], a[:, :, 0:HD], rden[:, :, :].to_broadcast([P, H, HD]), ALU.mult).then_inc(o_ready, 1)

            def residual(b, s, n):
                to = x1[:, bass.ds(b, 1), :].rearrange("p b d -> p (b d)")
                dve.wait_ge(wo_done, b + 1)
                dve.wait_ge(xb_ready[s], n + 1)
                nc.vector.tensor_tensor(to, p_o[:, 0:D], xin[:, s, :], ALU.add).then_inc(x1_ready, 1)
                hold(dve, x1_ready, b + 1, dve_go)
                nc.vector.bn_stats(stats[:, :], to).then_inc(ln_link, 1)
                hold(dve, ln_link, 3 * b + 1, dve_go)
                nc.vector.bn_aggr(mv[:, :], stats[:, :]).then_inc(ln_link, 1)

            def layer_norm(b, s, n):
                to = x1[:, bass.ds(b, 1), :].rearrange("p b d -> p (b d)")
                dve.wait_ge(std_ready, b + 1)
                nc.vector.reciprocal(rstd[:, :], std[:, :]).then_inc(ln_link, 1)
                dve.wait_ge(ln_link, 3 * b + 3)
                nc.vector.tensor_scalar(xn[:, :], to, mv[:, 0:1], rstd[:, :], ALU.subtract, ALU.mult).then_inc(xn_ready, 1)

            def take(b, s, c):
                use = 2 * b + c // 4
                dve.wait_ge(msg_done[c % 4], use + 1)
                wait(dve, msg_stored[c // 2], 16 * b)
                for r in range(2):
                    last = nc.vector.tensor_scalar(msg[:, 2 * c + r, :], p_m[c % 4][:, r * D:(r + 1) * D],
                                                   gate[:, s, 2 * c + r:2 * c + r + 1], None, ALU.mult)
                last.then_inc(msg_taken[c % 4], 1)

            def back(b, s, n, more):
                if more:
                    normalise(*next_of(b, s, n))
                dve.wait_ge(gate_ready, b + 1)
                take(b, s, 1)
                if more:
                    residual(*next_of(b, s, n))
                take(b, s, 3)
                if more:
                    layer_norm(*next_of(b, s, n))
                take(b, s, 5)
                take(b, s, 7)

            all_blocks(dve, front_of([normalise, residual, layer_norm]), back)

        @block.scalar
        def _(act):
            def take_oT(b, s, n):
                act.wait_ge(oT_done, b + 1)
                nc.scalar.activation(oT[:, :, :], p_oT[:, 0:2 * P].rearrange("p (c n) -> p c n", c=2), ACT.Copy).then_inc(oT_ready, 1)

            def root(b, s, n):
                act.wait_ge(ln_link, 3 * b + 2)
                nc.scalar.activation(std[:, :], mv[:, 1:2], ACT.Sqrt, bias=t["eps"][:, 0:1]).then_inc(std_ready, 1)

            def take_hT(b, s, n):
                act.wait_ge(xT_done, b + 1)
                nc.scalar.activation(hT[:, s, :, :], p_xT[:, 0:2 * P].rearrange("p (c n) -> p c n", c=2), ACT.Relu).then_inc(hT_ready, 1)

            def gates(b, s, n):
                act.wait_ge(gate_done, b + 1)
                nc.scalar.activation(gate[:, s, :], p_g[:, 0:RELS], ACT.Sigmoid).then_inc(gate_ready, 1)

            def take(b, s, c):
                use = 2 * b + c // 4
                act.wait_ge(msg_done[c % 4], use + 1)
                wait(act, msg_stored[c // 2], 16 * b)
                for r in range(2):
                    last = nc.scalar.activation(msg[:, 2 * c + r, :], p_m[c % 4][:, r * D:(r + 1) * D], ACT.Copy,
                                                scale=gate[:, s, 2 * c + r:2 * c + r + 1])
                last.then_inc(msg_taken[c % 4], 1)

            def back(b, s, n, more):
                act.wait_ge(gate_ready, b + 1)
                if more:
                    take_oT(*next_of(b, s, n))
                take(b, s, 0)
                take(b, s, 2)
                if more:
                    root(*next_of(b, s, n))
                take(b, s, 4)
                if more:
                    take_hT(*next_of(b, s, n))
                take(b, s, 6)
                if more:
                    gates(*next_of(b, s, n))

            all_blocks(act, front_of([take_oT, root, take_hT, gates]), back)

        @block.tensor
        def _(pe):
            pe.wait_ge(w_in, 96)

            def turn_o(b, s, n):
                pe.wait_ge(o_ready, b + 1)
                flat = o[:, :, :].rearrange("p h c -> p (h c)")
                for c in range(2):
                    last = nc.tensor.transpose(p_oT[:, c * P:(c + 1) * P], flat[:, c * P:(c + 1) * P], t["ident"][:, :])
                last.then_inc(oT_done, 1)

            def project(b, s, n):
                pe.wait_ge(oT_ready, b + 1)
                for c in range(2):
                    last = nc.tensor.matmul(p_o[:, 0:D], oT[:, c, :], wos[:, c, :], start=(c == 0), stop=(c == 1))
                last.then_inc(wo_done, 1)

            def turn_x(b, s, n):
                pe.wait_ge(xn_ready, b + 1)
                for c in range(2):
                    last = nc.tensor.transpose(p_xT[:, c * P:(c + 1) * P], xn[:, c * P:(c + 1) * P], t["ident"][:, :])
                last.then_inc(xT_done, 1)

            def gates(b, s, n):
                pe.wait_ge(hT_ready, b + 1)
                for c in range(2):
                    last = nc.tensor.matmul(p_g[:, 0:RELS], hT[:, s, c, :], gw[:, c, :], start=(c == 0), stop=(c == 1))
                last.then_inc(gate_done, 1)

            def relations(b, s, c):
                use = 2 * b + c // 4
                wait(pe, msg_taken[c % 4], use)
                for half in range(2):
                    last = nc.tensor.matmul(p_m[c % 4][:, :], hT[:, s, half, :], wr[:, half, 2 * c:2 * c + 2, :],
                                            start=(half == 0), stop=(half == 1))
                last.then_inc(msg_done[c % 4], 1)

            def back(b, s, n, more):
                relations(b, s, 0)
                if more:
                    turn_o(*next_of(b, s, n))
                relations(b, s, 1)
                if more:
                    project(*next_of(b, s, n))
                relations(b, s, 2)
                relations(b, s, 3)
                relations(b, s, 4)
                if more:
                    turn_x(*next_of(b, s, n))
                relations(b, s, 5)
                relations(b, s, 6)
                if more:
                    gates(*next_of(b, s, n))
                relations(b, s, 7)

            all_blocks(pe, front_of([turn_o, project, turn_x, gates]), back)


def message_sums(nc, t, x1, msg_d, out):
    with nc.sbuf_tensor("agg", [P, BLOCKS, D], F32) as agg:
        def weigh(o, rows, s):
            for k in range(2):
                last = nc.scalar.activation(o[:, k, :], rows[:, k, :], ACT.Copy, scale=t["norm"][:, bass.ds(2 * s + k, 1)])
            return last

        edge_sums(nc, t, "m_", msg_d, D, t["rel"], agg[:, :, :], weigh, "scalar")

        ctx, sb, ps, sem = phase(nc)
        PARTS = 7
        W = BLOCKS // PARTS
        with ctx:
            out_ready = sem("out_ready")
            out_stored = sem("out_stored")
            block = ctx.enter_context(nc.Block())

            @block.vector
            def _(dve):
                for c in range(PARTS):
                    a = slice(c * W, (c + 1) * W)
                    nc.vector.scalar_tensor_tensor(out=agg[:, a, :], in0=agg[:, a, :], scalar=0.0, in1=x1[:, a, :],
                                                   op0=ALU.max, op1=ALU.add).then_inc(out_ready, 1)

            @block.sync
            def _(sp):
                whole = out[0:(BLOCKS - 1) * P, :].rearrange("(b p) d -> p b d", p=P)
                for c in range(PARTS):
                    a, b = c * W, min((c + 1) * W, BLOCKS - 1)
                    sp.wait_ge(out_ready, c + 1)
                    sp.dma_start(whole[:, a:b, :], agg[:, a:b, :]).then_inc(out_stored, 16)
                sp.dma_start(out[(BLOCKS - 1) * P:N, :], agg[0:LAST_ROWS, BLOCKS - 1, :]).then_inc(out_stored, 16)
                sp.wait_ge(out_stored, 16 * (PARTS + 1))


_INS = ['x', 'src', 'dst', 'edge_attr_64', 'edge_type_16', 'edge_weight1', 'L0_gnn_Wq', 'L0_gnn_Wk', 'L0_gnn_Wv',
        'L0_gnn_W1', 'L0_gnn_b1', 'L0_gnn_W2', 'L0_gnn_b2', 'L0_gnn_Wo', 'L0_gnn_bo', 'L1_gnn_weight', 'L1_gnn_gate_weight']


def kernel(**inputs):
    import numpy as _np
    import concourse.bacc as _bacc
    from concourse import mybir as _mybir
    from concourse.bass_utils import run_bass_kernel_spmd as _run

    nc = _bacc.Bacc("TRN2", target_bir_lowering=False, num_devices=1)
    arrays, args = {}, []
    for name in _INS:
        a = _np.ascontiguousarray(inputs[name])
        arrays[f"in_{name}_dram"] = a
        args.append(nc.dram_tensor(f"in_{name}_dram", a.shape, _mybir.dt.from_np(a.dtype), kind="ExternalInput").ap())
    args.append(nc.dram_tensor("out_0_dram", (N, D), F32, kind="ExternalOutput").ap())
    build(nc, *args)
    r = _run(nc, [arrays], core_ids=[0])
    return r.results[0]["out_0_dram"]
```

```python
from contextlib import ExitStack

import concourse.bass as bass
from concourse import mybir

F32 = mybir.dt.float32
BF16 = mybir.dt.bfloat16
I32 = mybir.dt.int32
ALU = mybir.AluOpType
ACT = mybir.ActivationFunctionType
AX = mybir.AxisListType

P = 128
N, E, D, H, FE, RELS = 6250, 200000, 256, 8, 64, 16
HD = D // H
HD1 = HD + 1
BLOCKS = -(-N // P)
NPAD = BLOCKS * P
LAST_ROWS = N - (BLOCKS - 1) * P
GE = 2 * P
ROWS = 16
ROW_GROUPS = 49
GROUPS = ROWS * ROW_GROUPS
FULL_GROUPS = E // GE
TAIL = E - FULL_GROUPS * GE
EPAD = GROUPS * GE
ROW_E = ROW_GROUPS * GE
COLS = 2 * GROUPS
U = 4
STEPS = GROUPS + BLOCKS - 1
ITERS = STEPS // U
CHUNKS = GROUPS // U
TSTEPS = STEPS + U
TCOLS = 2 * TSTEPS
PADNODE = NPAD - 1
BIG = 1.0e30
EPS = 1.0e-5
MW0 = (U - 1) * H
MW = (2 * U - 1) * H
WIN = 16 * (2 + 1 + 1 + U)

assert STEPS % U == 0 and GROUPS % U == 0 and PADNODE >= N


def wait(eng, sem, value):
    if isinstance(value, int) and value <= 0:
        return
    eng.wait_ge(sem, value)


def hold(eng, sem, value, passed):
    eng.wait_ge(sem, value)
    eng.sem_inc(passed, 1)


def build(nc, x, src, dst, edge_attr, edge_type, edge_weight, wq, wk, wv, w1, b1, w2, b2, wo, bo,
          rel_w, gate_w, out):
    newseg_d = nc.dram_tensor("newseg_d", [EPAD + 1], BF16, kind="Internal").ap()
    k_d = nc.dram_tensor("k_d", [NPAD, D], F32, kind="Internal").ap()
    v_d = nc.dram_tensor("v_d", [NPAD, H * HD1], F32, kind="Internal").ap()
    dstrow_d = nc.dram_tensor("dstrow_d", [TSTEPS, 2 * P], BF16, kind="Internal").ap()
    mlp_d = nc.dram_tensor("mlp_d", [GROUPS * H, GE], F32, kind="Internal").ap()
    msg_d = nc.dram_tensor("msg_d", [RELS * NPAD, D], F32, kind="Internal").ap()

    with ExitStack() as ctx:
        def sb(name, shape, dt=F32):
            return ctx.enter_context(nc.sbuf_tensor(name, shape, dt))

        t = {}
        t["dst"] = sb("t_dst", [P, TCOLS])
        t["src"] = sb("t_src", [P, TCOLS], I32)
        t["rel"] = sb("t_rel", [P, TCOLS], I32)
        t["norm"] = sb("t_norm", [P, TCOLS])
        t["block"] = sb("t_block", [1, TSTEPS], I32)
        t["group"] = sb("t_group", [1, TSTEPS], I32)
        t["iota"] = sb("t_iota", [P, P])
        t["node"] = sb("t_node", [P, 1])
        t["ident"] = sb("t_ident", [P, P])
        t["eps"] = sb("t_eps", [P, 1])
        t["chain"] = sb("t_chain", [1, 2, H, ROWS])
        edge_tables(nc, t, src, dst, edge_type, edge_weight, newseg_d, dstrow_d)
        with ExitStack() as sums_ctx:
            with nc.sbuf_tensor("scores", [P, COLS, H], F32) as scores:
                with nc.sbuf_tensor("q3", [P, BLOCKS, 3, D], BF16) as q3:
                    node_projections(nc, t, q3, scores, x, wq, wk, wv, k_d, v_d)
                    edge_scores(nc, t, q3, scores, edge_attr, w1, b1, w2, b2, k_d, mlp_d, dstrow_d)
                softmax_numerators(nc, t, scores, newseg_d, mlp_d)
                att = sums_ctx.enter_context(nc.sbuf_tensor("att", [P, BLOCKS, H, HD1], F32, side="right"))
                weighted_sums(nc, t, scores, att, v_d)
            with nc.sbuf_tensor("x1", [P, BLOCKS, D], F32) as x1:
                messages(nc, t, att, x1, x, wo, bo, rel_w, gate_w, msg_d)
                message_sums(nc, t, x1, msg_d, out)


def phase(nc):
    ctx = ExitStack()
    sems = []

    def clear():
        nc.clear_and_free_semaphores(sems)
        nc.all_engine_barrier()

    ctx.callback(clear)

    def sb(name, shape, dt=F32):
        return ctx.enter_context(nc.sbuf_tensor(name, shape, dt))

    def ps(name, shape, dt=F32):
        return ctx.enter_context(nc.psum_tensor(name, shape, dt))

    def sem(name, n=None):
        if n is None:
            sems.append(nc.alloc_semaphore(name))
            return sems[-1]
        return [sem(f"{name}{i}") for i in range(n)]

    return ctx, sb, ps, sem


def edge_tables(nc, t, src, dst, edge_type, edge_weight, newseg_d, dstrow_d):
    ctx, sb, ps, sem = phase(nc)
    J = -(-GROUPS // P)
    FULL_J = FULL_GROUPS // P
    REST = FULL_GROUPS - FULL_J * P
    PADROWS = GROUPS - FULL_J * P
    with ctx:
        dst_i = sb("dst_i", [P, J, GE], I32)
        src_i = sb("src_i", [P, J, GE], I32)
        typ_i = sb("typ_i", [P, J, GE], I32)
        nrm_f = sb("nrm_f", [P, J, GE])
        dst_f = sb("dst_f", [P, J, GE])
        src_f = sb("src_f", [P, J, GE])
        rel_f = sb("rel_f", [P, J, GE])
        before = sb("before", [P, J], I32)
        beforef = sb("beforef", [P, J])
        same = sb("same", [P, J, GE])
        newseg = sb("newseg", [P, J, GE], BF16)
        last_blk = sb("last_blk", [P, J], I32)
        iota_g = sb("iota_g", [P, J], I32)
        iota_gf = sb("iota_gf", [P, J])
        key = sb("key", [P, J])
        iota_i = sb("iota_i", [P, TSTEPS], I32)
        iota_s = sb("iota_s", [P, TSTEPS])
        step128 = sb("step128", [P, TSTEPS])
        passed = sb("passed", [P, J, TSTEPS], BF16)
        ones = sb("ones", [P, P], BF16)
        pick = sb("pick", [P, J, TSTEPS])
        nbase = sb("nbase", [P, TSTEPS])
        minus = sb("minus", [1, GE])
        ST = -(-TSTEPS // P)
        dstrow = sb("dstrow", [P, ST, 2, P], BF16)
        ends = sb("ends", [1, 2, ROWS + 1], I32)
        endsf = sb("endsf", [1, 2, ROWS + 1])
        tail = sb("tail", [1, 1], BF16)
        blkf = sb("blkf", [1, TSTEPS])
        grpf = sb("grpf", [1, TSTEPS])
        HS = TSTEPS // 2
        turned = [ps(f"turned{i}", [P, 512]) for i in range(4)]
        count = [ps(f"count{i}", [P, 512]) for i in range(2)]
        pads_set = sem("pads_set")
        consts = sem("consts")
        loaded = sem("loaded")
        cast = sem("cast")
        link = sem("link")
        turned_ready = sem("turned_ready")
        turned_taken = sem("turned_taken")
        passed_ready = sem("passed_ready")
        pick_ready = sem("pick_ready")
        dst_taken = sem("dst_taken")
        base_ready = sem("base_ready")
        count_ready = sem("count_ready")
        newseg_ready = sem("newseg_ready")
        stored = sem("stored")
        LOADS = 4 * 3 + 4 + 2 + 2
        block = ctx.enter_context(nc.Block())
        flat_w = edge_weight.rearrange("e a -> (e a)")

        tables = ((dst_f, t["dst"]), (src_f, t["src"]), (rel_f, t["rel"]), (nrm_f, t["norm"]))
        jobs = [(f, to, half, k) for f, to in tables for half in range(2) for k in range(2)]

        def spans(half, past):
            out = []
            for j in range(J):
                a, b = max(half * HS, j * P), min(half * HS + HS, j * P + P + past)
                if a < b:
                    out.append((j, a, b))
            return out


        @block.sync
        def _(sp):
            sp.wait_ge(pads_set, 6)
            for flat, to in ((dst, dst_i), (src, src_i), (edge_type, typ_i), (flat_w, nrm_f)):
                a, b = FULL_J * P * GE, FULL_GROUPS * GE
                sp.dma_start(to[:, 0:FULL_J, :], flat[0:a].rearrange("(j p e) -> p j e", p=P, e=GE)).then_inc(loaded, 16)
                sp.dma_start(to[0:REST, FULL_J, :], flat[a:b].rearrange("(p e) -> p e", e=GE)).then_inc(loaded, 16)
                sp.dma_start(to[REST:REST + 1, FULL_J, 0:TAIL], flat[b:E].rearrange("(a e) -> a e", a=1)).then_inc(loaded, 16)
            last = dst[0:FULL_GROUPS * GE].rearrange("(g e) -> g e", e=GE)[:, GE - 1:GE]
            with nc.allow_non_contiguous_dma(reason="one number of each group"):
                sp.dma_start(before[1:P, 0:1], last[0:P - 1, :]).then_inc(loaded, 16)
                sp.dma_start(before[:, 1:FULL_J], last[P - 1:P * FULL_J - 1, :].rearrange("(j p) a -> p (j a)", p=P)).then_inc(loaded, 16)
                sp.dma_start(before[0:REST + 1, FULL_J:J], last[P * FULL_J - 1:FULL_GROUPS, :]).then_inc(loaded, 16)
                n = E // ROW_E
                sp.dma_start(ends[:, 0, 0:n], dst[0:n * ROW_E].rearrange("(a q e) -> a q e", a=1, e=ROW_E)[:, :, ROW_E - 1]).then_inc(loaded, 16)
                sp.dma_start(ends[:, 1, 0:n], dst[0:n * ROW_E].rearrange("(a q e) -> a q e", a=1, e=ROW_E)[:, :, 0]).then_inc(loaded, 16)
                sp.dma_start(ends[:, 1, n:n + 1], dst[n * ROW_E:n * ROW_E + 1].rearrange("(a q) -> a q", a=1)).then_inc(loaded, 16)
            sp.wait_ge(newseg_ready, 1)
            a = FULL_J * P * GE
            sp.dma_start(newseg_d[0:a].rearrange("(j p e) -> p j e", p=P, e=GE), newseg[:, 0:FULL_J, :]).then_inc(stored, 16)
            sp.dma_start(newseg_d[a:EPAD].rearrange("(p e) -> p e", e=GE), newseg[0:PADROWS, FULL_J, :]).then_inc(stored, 16)
            sp.dma_start(newseg_d[EPAD:EPAD + 1].rearrange("(a e) -> a e", a=1), tail[:, :]).then_inc(stored, 16)
            full = TSTEPS // P
            sp.wait_ge(turned_taken, len(jobs) - 4 + ST)
            sp.dma_start(dstrow_d[0:full * P, :].rearrange("(c p) e -> p c e", p=P),
                         dstrow[:, 0:full, :, :].rearrange("s c k p -> s c (k p)")).then_inc(stored, 16)
            sp.dma_start(dstrow_d[full * P:TSTEPS, :],
                         dstrow[0:TSTEPS - full * P, full, :, :].rearrange("s k p -> s (k p)")).then_inc(stored, 16)
            sp.wait_ge(stored, 80)

        @block.gpsimd
        def _(pool):
            pool.memset(dst_i[:, FULL_J, :], PADNODE).then_inc(pads_set, 1)
            pool.memset(src_i[:, FULL_J, :], 0).then_inc(pads_set, 1)
            pool.memset(typ_i[:, FULL_J, :], 0).then_inc(pads_set, 1)
            pool.memset(nrm_f[:, FULL_J, :], 0.0).then_inc(pads_set, 1)
            pool.memset(before[:, :], PADNODE).then_inc(pads_set, 1)
            pool.memset(ends[:, :, :], PADNODE).then_inc(pads_set, 1)
            pool.memset(t["ident"][:, :], 0.0).then_inc(consts, 1)
            pool.memset(minus[:, :], -1.0).then_inc(consts, 1)
            pool.memset(ones[:, :], 1.0).then_inc(consts, 1)
            pool.memset(t["eps"][:, :], EPS).then_inc(consts, 1)
            pool.memset(tail[:, :], -BIG).then_inc(consts, 1)
            pool.iota(iota_i[:, :], [[1, TSTEPS]], base=0, channel_multiplier=0).then_inc(consts, 1)
            pool.iota(iota_g[:, :], [[P, J]], base=0, channel_multiplier=1).then_inc(consts, 1)
            pool.wait_ge(consts, 1)
            pool.affine_select(out=t["ident"][:, :], in_=t["ident"][:, :], compare_op=ALU.not_equal, fill=1.0, base=0,
                               pattern=[[-1, P]], channel_multiplier=1).then_inc(consts, 1)

        @block.tensor
        def _(pe):
            pe.wait_ge(consts, 8)
            pe.wait_ge(cast, 4)
            pe.wait_ge(loaded, 16 * (LOADS - 2))
            pe.wait_ge(passed_ready, J)
            for half in range(2):
                for j in range(J):
                    rows = P if j < FULL_J else PADROWS
                    last = nc.tensor.matmul(count[half][:, 0:HS], ones[0:rows, :], passed[0:rows, j, half * HS:half * HS + HS],
                                            start=(j == 0), stop=(j == J - 1))
            last.then_inc(count_ready, 1)
            pe.wait_ge(pick_ready, 1)
            for n, (f, to, half, k) in enumerate(jobs):
                if n >= 4:
                    pe.wait_ge(turned_taken if n >= 8 else dst_taken, n - 7 if n >= 8 else n - 3)
                for i, (j, a, b) in enumerate(spans(half, BLOCKS - 1)):
                    rows = P if j < FULL_J else PADROWS
                    last = nc.tensor.matmul(turned[n % 4][:, a - half * HS:b - half * HS], f[0:rows, j, k::2], pick[0:rows, j, a:b],
                                            start=(i == 0), stop=(b == half * HS + HS), skip_group_check=True)
                last.then_inc(turned_ready, 1)
            pe.wait_ge(base_ready, 2)
            for st in range(ST):
                n = len(jobs) + st
                a, b = st * P, min((st + 1) * P, TSTEPS)
                pe.wait_ge(turned_taken, n - 7)
                for j in range(max(0, a - BLOCKS + 1) // P, min(J - 1, (b - 1) // P) + 1):
                    rows = P if j < FULL_J else PADROWS
                    nc.tensor.matmul(turned[n % 4][0:b - a, 0:GE], pick[0:rows, j, a:b], dst_f[0:rows, j, :],
                                     start=(j == max(0, a - BLOCKS + 1) // P), stop=False)
                nc.tensor.matmul(turned[n % 4][0:b - a, 0:GE], nbase[0:1, a:b], minus[:, :], start=False, stop=True).then_inc(turned_ready, 1)

        @block.scalar
        def _(act):
            for n, (f, to, half, k) in enumerate(jobs):
                if n < 4:
                    continue
                act.wait_ge(turned_ready, n + 1)
                view = to[:, :].rearrange("p (s k) -> p k s", k=2)[:, k, half * HS:half * HS + HS]
                nc.scalar.activation(view, turned[n % 4][:, 0:HS], ACT.Copy).then_inc(turned_taken, 1)
            for st in range(ST):
                n = len(jobs) + st
                rows = min(P, TSTEPS - st * P)
                act.wait_ge(turned_ready, n + 1)
                nc.scalar.activation(dstrow[0:rows, st, :, :], turned[n % 4][0:rows, 0:GE].rearrange("s (p k) -> s k p", k=2),
                                     ACT.Copy).then_inc(turned_taken, 1)

        @block.vector
        def _(dve):
            n = [0]

            def done(ins):
                n[0] += 1
                ins.then_inc(link, 1)
                dve.wait_ge(link, n[0])

            dve.wait_ge(consts, 8)
            dve.wait_ge(loaded, 16 * (LOADS - 2))
            nc.vector.tensor_copy(t["iota"][:, :], iota_i[:, 0:P])
            nc.vector.tensor_copy(t["node"][:, :], iota_g[:, 0:1])
            nc.vector.tensor_copy(dst_f[:, :, :], dst_i[:, :, :]).then_inc(cast, 1)
            nc.vector.tensor_copy(src_f[:, :, :], src_i[:, :, :]).then_inc(cast, 1)
            nc.vector.tensor_copy(beforef[:, :], before[:, :])
            nc.vector.tensor_copy(iota_gf[:, :], iota_g[:, :])
            nc.vector.tensor_copy(endsf[:, :, :], ends[:, :, :])
            nc.vector.tensor_copy(iota_s[:, :], iota_i[:, :]).then_inc(cast, 1)
            done(nc.vector.tensor_scalar(last_blk[:, :], dst_i[:, :, GE - 1], 7, None, ALU.arith_shift_right))
            nc.vector.scalar_tensor_tensor(out=rel_f[:, :, :], in0=typ_i[:, :, :], scalar=float(NPAD), in1=src_f[:, :, :],
                                           op0=ALU.mult, op1=ALU.add).then_inc(cast, 1)
            done(nc.vector.tensor_tensor(key[:, :], last_blk[:, :], iota_gf[:, :], ALU.add))
            for j in range(J):
                rows = P if j < FULL_J else PADROWS
                nc.vector.tensor_scalar(passed[0:rows, j, :], iota_s[0:rows, :], key[0:rows, j:j + 1], None,
                                        ALU.is_gt).then_inc(passed_ready, 1)
            done(nc.vector.tensor_scalar(step128[:, :], iota_s[:, :], float(P), None, ALU.mult))
            dve.wait_ge(count_ready, 1)
            for half in range(2):
                for j, a, b in spans(half, P):
                    last = nc.vector.tensor_scalar(pick[:, j, a:b], count[half][:, a - half * HS:b - half * HS], iota_gf[:, j:j + 1],
                                                   None, ALU.is_equal)
            last.then_inc(pick_ready, 1)
            for half in range(2):
                a, b = half * HS, half * HS + HS
                nc.vector.tensor_copy(grpf[:, a:b], count[half][0:1, 0:HS])
                nc.vector.scalar_tensor_tensor(out=blkf[:, a:b], in0=count[half][0:1, 0:HS], scalar=-1.0, in1=iota_s[0:1, a:b],
                                               op0=ALU.mult, op1=ALU.add)
                nc.vector.scalar_tensor_tensor(out=nbase[:, a:b], in0=count[half][:, 0:HS], scalar=-float(P),
                                                    in1=step128[:, a:b], op0=ALU.mult, op1=ALU.add).then_inc(base_ready, 1)
            dve.wait_ge(base_ready, 2)
            nc.vector.tensor_copy(t["block"][:, :], blkf[:, :])
            nc.vector.tensor_copy(t["group"][:, :], grpf[:, :])
            for m, (f, to, half, k) in enumerate(jobs[0:4]):
                dve.wait_ge(turned_ready, m + 1)
                a, b = half * HS, half * HS + HS
                view = to[:, :].rearrange("p (s k) -> p k s", k=2)[:, k, a:b]
                nc.vector.tensor_tensor(view, turned[m][:, 0:HS], nbase[:, a:b], ALU.subtract).then_inc(dst_taken, 1)
            nc.vector.tensor_tensor(same[:, :, 1:GE], dst_f[:, :, 1:GE], dst_f[:, :, 0:GE - 1], ALU.is_equal)
            done(nc.vector.tensor_tensor(same[:, :, 0:1], dst_f[:, :, 0:1], beforef[:, :].unsqueeze(2), ALU.is_equal))
            nc.vector.tensor_scalar(newseg[:, :, :], same[:, :, :], -1.0, BIG, ALU.add, ALU.mult).then_inc(newseg_ready, 1)
            for way in range(2):
                c = t["chain"][:, way, 0, :]
                done(nc.vector.memset(c, 0.0))
                if way == 0:
                    done(nc.vector.tensor_tensor(c[:, 1:ROWS], endsf[:, 0, 1:ROWS], endsf[:, 0, 0:ROWS - 1], ALU.is_equal))
                else:
                    done(nc.vector.tensor_tensor(c[:, 0:ROWS - 1], endsf[:, 1, 0:ROWS - 1], endsf[:, 1, 1:ROWS], ALU.is_equal))
                done(nc.vector.tensor_scalar(c, c, -1.0, BIG, ALU.add, ALU.mult))
                for h in range(1, H):
                    nc.vector.tensor_copy(t["chain"][:, way, h, :], c)


def blocks_loop(eng, body, last=BLOCKS):
    body(0, 0, 0)
    pairs = (last - 1) // 2
    with eng.Fori(0, pairs) as i:
        body(2 * i + 1, 1, i)
        body(2 * i + 2, 0, i + 1)
    if last > 2 * pairs + 1:
        body(last - 1, 1, pairs)


def node_projections(nc, t, q3, scores, x, wq, wk, wv, k_d, v_d):
    ctx, sb, ps, sem = phase(nc)
    B = 7
    BATCHES = BLOCKS // B
    assert BATCHES * B == BLOCKS
    SLOT = [0, 1, 2, 0, 1, 2, 1]
    TURN = [j % 2 for j in range(B)]
    BACK, TURN_BACK = ([next(d for d in range(1, B + 1) if ring[(j - d) % B] == ring[j]) for j in range(B)]
                       for ring in (SLOT, TURN))
    with ctx:
        w = sb("w_qkv", [P, 2, 3 * D])
        xin = sb("xin", [P, B, D])
        stats = sb("stats", [P, B, 6])
        mv = sb("mv", [P, B, 2])
        std = sb("std", [P, B, 1])
        rstd = sb("rstd", [P, B, 1])
        xn = sb("xn", [P, B, D])
        hT = sb("hT", [P, 3, 2, P])
        qr = sb("qr", [P, B, D])
        ko = sb("ko", [P, B, D])
        vo = sb("vo", [P, B, H, HD1])
        turned = [ps(f"xT{i}", [P, 512]) for i in range(2)]
        qq = [ps(f"qq{i}", [P, 512]) for i in range(3)]
        kv = [ps(f"kv{i}", [P, 512]) for i in range(3)]
        dve_go = sem("dve_go")
        w_in = sem("w_in")
        ones_set = sem("ones_set")
        x_in = sem("x_in")
        stats_ready = sem("stats_ready")
        mv_ready = sem("mv_ready")
        std_ready = sem("std_ready")
        rstd_ready = sem("rstd_ready")
        xn_ready = sem("xn_ready")
        turned_ready = sem("xT_ready")
        hT_ready = sem("hT_ready")
        proj_ready = sem("proj_ready")
        q0_ready = sem("q0_ready")
        qr_ready = sem("qr_ready")
        q1_ready = sem("q1_ready")
        kv_ready = sem("kv_ready")
        k_stored = sem("k_stored", B)
        v_stored = sem("v_stored", B)
        block = ctx.enter_context(nc.Block())
        X_LOADS = 2

        def batches(eng, iteration):
            iteration(0, True)
            with eng.Fori(1, BATCHES - 1) as i:
                iteration(i, True)
            iteration(BATCHES - 1, False)

        @block.sync
        def _(sp):
            def load(i):
                wait(sp, xn_ready, B * i)
                last = isinstance(i, int) and i == BATCHES - 1
                full = B - 1 if last else B
                rows = x[bass.ds(i * (B * P), full * P), :].rearrange("(j p) d -> p j d", p=P)
                sp.dma_start(xin[:, 0:3, :], rows[:, 0:3, :]).then_inc(x_in, 16)
                sp.dma_start(xin[:, 3:full, :], rows[:, 3:full, :]).then_inc(x_in, 16)
                if last:
                    sp.dma_start(xin[0:LAST_ROWS, B - 1, :], x[(BLOCKS - 1) * P:N, :]).then_inc(x_in, 16)

            load(0)
            for i, m in enumerate((wq, wk, wv)):
                sp.dma_start(w[:, :, i * D:(i + 1) * D], m.rearrange("(c p) n -> p c n", p=P)).then_inc(w_in, 16)
            load(1)

            def stores(i):
                for j in range(B):
                    n = B * i + j
                    sp.wait_ge(kv_ready, n + 1)
                    sp.dma_start(k_d[bass.ds(n * P, P), :], ko[:, j, :]).then_inc(k_stored[j], 16)

            stores(0)
            load(2)
            with sp.Fori(1, BATCHES - 3) as i:
                stores(i)
                load(i + 2)
            stores(BATCHES - 3)
            load(BATCHES - 1)
            stores(BATCHES - 2)
            stores(BATCHES - 1)
            for j in range(B):
                sp.wait_ge(k_stored[j], 16 * BATCHES)

        @block.gpsimd
        def _(pool):
            pool.memset(vo[:, :, :, HD:HD1], 1.0).then_inc(ones_set, 1)
            pool.wait_ge(ones_set, 1)
            pool.memset(scores[:, :, :], 0.0)

            def iteration(i, more):
                for j in range(B):
                    n = B * i + j
                    pool.wait_ge(kv_ready, n + 1)
                    pool.dma_start(v_d[bass.ds(n * P, P), :], vo[:, j, :, :].rearrange("p h c -> p (h c)")).then_inc(v_stored[j], 16)

            batches(pool, iteration)
            for j in range(B):
                pool.wait_ge(v_stored[j], 16 * BATCHES)

        @block.vector
        def _(dve):
            def moments(i, j):
                nc.vector.bn_stats(stats[:, j, :], xin[:, j, :]).then_inc(stats_ready, 1)

            def aggregate(i, js):
                hold(dve, stats_ready, B * i + js[-1] + 1, dve_go)
                for j in js:
                    nc.vector.bn_aggr(mv[:, j, :], stats[:, j, :]).then_inc(mv_ready, 1)

            def invert(i):
                dve.wait_ge(std_ready, i + 1)
                nc.vector.reciprocal(rstd[:, :, :], std[:, :, :]).then_inc(rstd_ready, 1)
                dve.wait_ge(rstd_ready, i + 1)

            def normalise(i, j):
                nc.vector.tensor_scalar(xn[:, j, :], xin[:, j, :], mv[:, j, 0:1], rstd[:, j, :],
                                        ALU.subtract, ALU.mult).then_inc(xn_ready, 1)

            def loaded(i):
                if isinstance(i, int) and i == BATCHES - 1:
                    hold(dve, x_in, 16 * (X_LOADS * BATCHES + 1), dve_go)
                else:
                    hold(dve, x_in, 16 * X_LOADS * (i + 1), dve_go)

            def q_part(part, n):
                return q3[:, bass.ds(n, 1), part, :].rearrange("p a d -> p (a d)")

            def split(i, j):
                n = B * i + j
                first = isinstance(i, int) and i == 0
                dve.wait_ge(q0_ready, n + 1)
                nc.vector.scalar_tensor_tensor(out=qr[:, j, :], in0=qq[SLOT[j]][:, 0:D], scalar=HD ** -0.5, in1=q_part(0, n),
                                               op0=ALU.mult, op1=ALU.subtract).then_inc(qr_ready, 1)
                if not (first and j < 1):
                    second(n - 1, (j - 1) % B)
                if not (first and j < 2):
                    third(n - 2, (j - 2) % B)

            def second(n, j):
                dve.wait_ge(qr_ready, n + 1)
                nc.vector.tensor_copy(q_part(1, n), qr[:, j, :]).then_inc(q1_ready, 1)

            def third(n, j):
                dve.wait_ge(q1_ready, n + 1)
                nc.vector.tensor_tensor(q_part(2, n), qr[:, j, :], q_part(1, n), ALU.subtract)

            def iteration(i, more):
                for j in range(B):
                    split(i, j)
                    if more:
                        if j == 1:
                            loaded(i + 1)
                            for m in (0, 1, 2):
                                moments(i + 1, m)
                        elif j == 2:
                            aggregate(i + 1, (0, 1, 2))
                            for m in (3, 4, 5, 6):
                                moments(i + 1, m)
                        elif j == 3:
                            aggregate(i + 1, (3, 4, 5, 6))
                        elif j == 5:
                            invert(i + 1)
                            for m in (0, 1, 2):
                                normalise(i + 1, m)
                        elif j == 6:
                            for m in (3, 4, 5, 6):
                                normalise(i + 1, m)

            loaded(0)
            for m in range(B):
                moments(0, m)
            aggregate(0, range(B))
            invert(0)
            for m in range(B):
                normalise(0, m)
            iteration(0, True)
            with dve.Fori(1, BATCHES - 2) as i:
                iteration(i, True)
            iteration(BATCHES - 2, True)
            iteration(BATCHES - 1, False)
            second(BLOCKS - 1, B - 1)
            third(BLOCKS - 2, B - 2)
            third(BLOCKS - 1, B - 1)

        @block.scalar
        def _(act):
            def root(i):
                act.wait_ge(mv_ready, B * (i + 1))
                nc.scalar.activation(std[:, :, :], mv[:, :, 1:2], ACT.Sqrt, bias=t["eps"][:, 0:1]).then_inc(std_ready, 1)

            def take_turned(n, j):
                act.wait_ge(turned_ready, n + 1)
                wait(act, proj_ready, n + 1 - BACK[j])
                nc.scalar.activation(hT[:, SLOT[j], :, :], turned[TURN[j]][:, 0:2 * P].rearrange("p (c n) -> p c n", c=2),
                                     ACT.Relu).then_inc(hT_ready, 1)

            def iteration(i, more):
                for j in range(B):
                    n = B * i + j
                    s = SLOT[j]
                    if j < B - 1 or more:
                        take_turned(n + 1, (j + 1) % B)
                    if j == 5 and more:
                        root(i + 1)
                    act.wait_ge(proj_ready, n + 1)
                    nc.scalar.activation(q3[:, bass.ds(n, 1), 0, :].rearrange("p a d -> p (a d)"), qq[s][:, 0:D], ACT.Copy,
                                         scale=HD ** -0.5).then_inc(q0_ready, 1)
                    if not (isinstance(i, int) and i == 0):
                        act.wait_ge(k_stored[j], 16 * i)
                        act.wait_ge(v_stored[j], 16 * i)
                    nc.scalar.activation(ko[:, j, :], kv[s][:, 0:D], ACT.Copy)
                    nc.scalar.activation(vo[:, j, :, 0:HD], kv[s][:, D:2 * D].rearrange("p (h c) -> p h c", h=H),
                                         ACT.Copy).then_inc(kv_ready, 1)

            act.wait_ge(ones_set, 1)
            root(0)
            take_turned(0, 0)
            batches(act, iteration)

        @block.tensor
        def _(pe):
            def turn(n, j):
                pe.wait_ge(xn_ready, n + 1)
                wait(pe, hT_ready, n + 1 - TURN_BACK[j])
                for c in range(2):
                    last = nc.tensor.transpose(turned[TURN[j]][:, c * P:(c + 1) * P], xn[:, j, c * P:(c + 1) * P], t["ident"][:, :])
                last.then_inc(turned_ready, 1)

            def iteration(i, more):
                for j in range(B):
                    n = B * i + j
                    s = SLOT[j]
                    if j < B - 1 or more:
                        turn(n + 1, (j + 1) % B)
                    pe.wait_ge(hT_ready, n + 1)
                    wait(pe, qr_ready, n + 1 - BACK[j])
                    wait(pe, kv_ready, n + 1 - BACK[j])
                    for c in range(2):
                        nc.tensor.matmul(qq[s][:, 0:D], hT[:, s, c, :], w[:, c, 0:D], start=(c == 0), stop=(c == 1))
                    for c in range(2):
                        last = nc.tensor.matmul(kv[s][:, :], hT[:, s, c, :], w[:, c, D:3 * D], start=(c == 0), stop=(c == 1))
                    last.then_inc(proj_ready, 1)

            pe.wait_ge(w_in, 48)
            turn(0, 0)
            batches(pe, iteration)


IN_RANGE = "counted on the chip: s - BLOCKS < group(s) <= s and below GROUPS, block(s) = s - group(s)"


def block_of(nc, eng, t, s):
    return nc.values_load(t["block"][0:1, bass.ds(s, 1)], engines=(eng.engine,), min_val=0, max_val=BLOCKS - 1,
                          skip_runtime_bounds_check_because=IN_RANGE)


def group_of(nc, eng, t, s):
    return nc.values_load(t["group"][0:1, bass.ds(s, 1)], engines=(eng.engine,), min_val=0, max_val=GROUPS - 1,
                          skip_runtime_bounds_check_because=IN_RANGE)


def edge_scores(nc, t, q3, scores, edge_attr, w1, b1, w2, b2, k_d, mlp_d, dstrow_d):
    ctx, sb, ps, sem = phase(nc)
    with ctx:
        w1s = sb("w1s", [P, D])
        w2s = sb("w2s", [P, 2, MW])
        b1s = sb("b1s", [P, 2])
        b2s = sb("b2s", [U * H, 1])
        raw = sb("ef_raw", [P, U, P])
        efT = sb("efT", [P, U, P])
        hid = sb("hid", [P, 2, U, P])
        dsts = sb("dsts", [P, U, 2 * P], BF16)
        pickT = sb("pickT", [P, U, 2 * P], BF16)
        idx = sb("idx", [P, U, 2], I32)
        rows = sb("k_rows", [P, U, 2, D])
        prod = sb("prod", [P, 2, H, HD])
        red = sb("red", [P, 2, H])
        mlp = sb("mlp", [U * H, P, 2])
        p_ef = ps("p_ef", [P, 512])
        p_hid = [ps(f"p_hid{i}", [P, 512]) for i in range(2)]
        p_mlp = ps("p_mlp", [P, 512])
        p_q = [ps(f"p_q{i}", [P, 512]) for i in range(U)]
        w_in = sem("w1_in")
        ef_in = sem("ef_in")
        ef_turned = sem("ef_turned")
        efT_ready = sem("efT_ready")
        hid_done = sem("hid_done", U)
        hid_ready = sem("hid_ready", U)
        mlp_done = sem("mlp_done")
        mlp_taken = sem("mlp_taken")
        mlp_stored = sem("mlp_stored")
        w2_cleared = sem("w2_cleared")
        dsts_in = sem("dsts_in", 2)
        pick_ready = sem("pickT_ready", U)
        q_done = sem("q_rows_done", U)
        idx_ready = sem("idx_ready", U)
        gathered = sem("gathered", U)
        prod_done = sem("prod_done", U)
        red_done = sem("red_done", U)
        pool_go = sem("pool_go")
        block = ctx.enter_context(nc.Block())
        chunks = edge_attr[0:FULL_GROUPS * GE, :].rearrange("(g p k) f -> p g (k f)", p=P, k=2)

        @block.sync
        def _(sp):
            for pair in range(2):
                rows = dstrow_d[2 * pair:2 * pair + 2, :].rearrange("(a s) e -> a (s e)", a=1)
                sp.dma_start(dsts[:, 2 * pair:2 * pair + 2, :].rearrange("p s e -> p (s e)"),
                             rows.to_broadcast([P, 4 * P])).then_inc(dsts_in[pair], 16)
            for k in range(2):
                sp.dma_start(w1s[k * FE:(k + 1) * FE, :], w1[:, :]).then_inc(w_in, 16)
            sp.wait_ge(w2_cleared, 1)
            sp.dma_start(w2s[:, :, MW0:MW0 + H], w2.rearrange("(c p) h -> p c h", p=P)).then_inc(w_in, 16)
            with nc.allow_non_contiguous_dma(reason="256 numbers"):
                sp.dma_start(b1s[:, :], b1.rearrange("(c p) -> p c", p=P)).then_inc(w_in, 16)
                for g in range(U):
                    sp.dma_start(b2s[g * H:(g + 1) * H, :], b2.rearrange("(h a) -> h a", a=1)).then_inc(w_in, 16)

            def load(c):
                wait(sp, ef_turned, c)
                sp.dma_start(raw[:, :, :], chunks[:, bass.ds(U * c, U), :]).then_inc(ef_in, 16)

            def store(c):
                sp.wait_ge(mlp_taken, c + 1)
                sp.dma_start(mlp_d[bass.ds(U * H * c, U * H), :], mlp[:, :, :].rearrange("r p k -> r (p k)")).then_inc(mlp_stored, 16)

            def load_dsts(i, pair):
                wait(sp, pick_ready[2 * pair + 1], i)
                rows = dstrow_d[bass.ds(U * i + 2 * pair, 2), :].rearrange("(a s) e -> a (s e)", a=1)
                sp.dma_start(dsts[:, 2 * pair:2 * pair + 2, :].rearrange("p s e -> p (s e)"),
                             rows.to_broadcast([P, 4 * P])).then_inc(dsts_in[pair], 16)

            for c in range(3):
                load(c)
            with sp.Fori(0, CHUNKS - 4) as c:
                load_dsts(c + 1, 0)
                store(c)
                load_dsts(c + 1, 1)
                load(c + 3)
            load_dsts(CHUNKS - 3, 0)
            store(CHUNKS - 4)
            load_dsts(CHUNKS - 3, 1)
            sp.wait_ge(ef_turned, CHUNKS - 1)
            g = U * (CHUNKS - 1)
            sp.dma_start(raw[:, 0:FULL_GROUPS - g, :], chunks[:, g:FULL_GROUPS, :]).then_inc(ef_in, 16)
            sp.dma_start(raw[0:TAIL // 2, FULL_GROUPS - g, :],
                         edge_attr[FULL_GROUPS * GE:E, :].rearrange("(p k) f -> p (k f)", k=2)).then_inc(ef_in, 16)
            for c in range(CHUNKS - 3, CHUNKS):
                load_dsts(c + 1, 0)
                store(c)
                load_dsts(c + 1, 1)
            with sp.Fori(CHUNKS, ITERS) as i:
                load_dsts(i + 1, 0)
                load_dsts(i + 1, 1)
            sp.wait_ge(mlp_stored, 16 * CHUNKS)

        @block.gpsimd
        def _(pool):
            pool.memset(w2s[:, :, :], 0.0).then_inc(w2_cleared, 1)

            def gather(i, u):
                wait(pool, prod_done[u], i)
                hold(pool, idx_ready[u], i + 1, pool_go)
                for k in range(2):
                    pool.indirect_dma_start(rows[:, u, k, :], None, k_d[:, :],
                                            bass.IndirectOffsetOnAxis(idx[:, u, k:k + 1], 0)).then_inc(gathered[u], 16)

            for u in range(U):
                gather(0, u)
            with pool.Fori(1, ITERS) as i:
                for u in range(U):
                    gather(i, u)

        @block.scalar
        def _(act):
            def take_ef():
                nc.scalar.activation(efT[:, :, :], p_ef[:, :].rearrange("p (g e) -> p g e", g=U), ACT.Copy).then_inc(efT_ready, 1)

            def take_hidden(i, u, n):
                act.wait_ge(hid_done[u], n + 1)
                nc.scalar.activation(hid[:, u % 2, :, :], p_hid[u % 2][:, :].rearrange("p (g e) -> p g e", g=U), ACT.Relu,
                                     bias=b1s[:, u % 2:u % 2 + 1]).then_inc(hid_ready[u], 1)

            def next_idx(i, u, n):
                wait(act, gathered[u], 32 * n)
                s = U * i + u
                nc.scalar.activation(idx[:, u, :], t["src"][:, bass.ds(2 * s, 2)], ACT.Copy).then_inc(idx_ready[u], 1)

            def take_mlp(c):
                act.wait_ge(mlp_done, c + 1)
                wait(act, mlp_stored, 16 * c)
                nc.scalar.activation(mlp[:, :, :].rearrange("r p k -> r k p"),
                                     p_mlp[0:U * H, 0:2 * P].rearrange("r (k p) -> r k p", k=2),
                                     ACT.Identity, bias=b2s[:, :]).then_inc(mlp_taken, 1)

            def iteration(i, hidden, mlp=True, features=True):
                for u in range(U):
                    if hidden:
                        take_hidden(i, u, i + 1)
                    if mlp and u == 0:
                        take_mlp(i)
                    if hidden:
                        if u == U - 1 and features:
                            act.wait_ge(ef_turned, i + 3)
                            take_ef()
                    next_idx(i + 1, u, i + 1)

            for u in range(U):
                next_idx(0, u, 0)
            act.wait_ge(w_in, WIN)
            act.wait_ge(ef_turned, 1)
            take_ef()
            for u in range(U):
                take_hidden(0, u, 0)
            act.wait_ge(ef_turned, 2)
            take_ef()
            iteration(0, True)
            with act.Fori(1, CHUNKS - 2) as i:
                iteration(i, True)
            iteration(CHUNKS - 2, True, features=False)
            iteration(CHUNKS - 1, False)
            with act.Fori(CHUNKS, ITERS) as i:
                iteration(i, False, mlp=False)

        @block.tensor
        def _(pe):
            def turn_ef(c):
                pe.wait_ge(ef_in, 16 * (c + 1) if not (isinstance(c, int) and c == CHUNKS - 1) else 16 * (CHUNKS + 1))
                for g in range(U):
                    last = nc.tensor.transpose(p_ef[:, g * P:(g + 1) * P], raw[:, g, :], t["ident"][:, :])
                last.then_inc(ef_turned, 1)

            def hidden(c, u):
                k, half = divmod(u, 2)
                if u == 0:
                    pe.wait_ge(efT_ready, c + 1)
                nc.tensor.matmul(p_hid[half][:, :], w1s[k * FE:(k + 1) * FE, half * P:(half + 1) * P],
                                 efT[k * FE:(k + 1) * FE, :, :], start=True, stop=True).then_inc(hid_done[u], 1)

            def mlp_out(c, u):
                k, half = divmod(u, 2)
                pe.wait_ge(hid_ready[u], c + 1)
                if u == 0:
                    wait(pe, mlp_taken, c)
                for g in range(U):
                    last = nc.tensor.matmul(p_mlp[0:U * H, k * P:(k + 1) * P], w2s[:, half, MW0 - g * H:MW0 + (U - g) * H],
                                            hid[:, half, g, :], start=(half == 0 and g == 0), stop=(half == 1 and g == U - 1))
                if u == U - 1:
                    last.then_inc(mlp_done, 1)

            def iteration(i, next_chunk, turn=True, drain=True):
                for u in range(U):
                    if next_chunk:
                        hidden(i + 1, u)
                        if u == U - 1 and turn:
                            turn_ef(i + 2)
                        if u:
                            mlp_out(i + 1, u - 1)
                    if u == 0 and drain:
                        mlp_out(i, U - 1)
                    b = block_of(nc, pe, t, U * i + u)
                    pe.wait_ge(pick_ready[u], i + 1)
                    for k in range(2):
                        for part in range(3):
                            last = nc.tensor.matmul(p_q[u][:, k * D:(k + 1) * D], pickT[:, u, k * P:(k + 1) * P],
                                                    q3[:, bass.ds(b, 1), part, :], start=(part == 0), stop=(part == 2))
                    last.then_inc(q_done[u], 1)

            pe.wait_ge(w_in, WIN)
            turn_ef(0)
            for u in range(U):
                hidden(0, u)
                if u:
                    mlp_out(0, u - 1)
            turn_ef(1)
            iteration(0, True)
            with pe.Fori(1, CHUNKS - 3) as i:
                iteration(i, True)
            iteration(CHUNKS - 3, True)
            iteration(CHUNKS - 2, True, turn=False)
            iteration(CHUNKS - 1, False)
            with pe.Fori(CHUNKS, ITERS) as i:
                iteration(i, False, drain=False)

        @block.vector
        def _(dve):
            def make_pick(u, n):
                if u % 2 == 0:
                    dve.wait_ge(dsts_in[u // 2], 16 * (n + 1))
                nc.vector.tensor_scalar(pickT[:, u, :], dsts[:, u, :], t["node"][:, 0:1], None,
                                        ALU.is_equal).then_inc(pick_ready[u], 1)

            def iteration(i):
                for u in range(U):
                    s = U * i + u
                    g = group_of(nc, dve, t, s)
                    dve.wait_ge(q_done[u], i + 1)
                    dve.wait_ge(gathered[u], 32 * (i + 1))
                    nc.vector.tensor_tensor(prod[:, :, :, :].rearrange("p k h c -> p (k h c)"), p_q[u][:, :],
                                            rows[:, u, :, :].rearrange("p k d -> p (k d)"), ALU.mult).then_inc(prod_done[u], 1)
                    make_pick((u + 3) % U, i + (u + 3) // U)
                    dve.wait_ge(prod_done[u], i + 1)
                    nc.vector.tensor_reduce(red[:, :, :].rearrange("p k h -> p (k h)"),
                                            prod[:, :, :, :].rearrange("p k h c -> p (k h) c"), AX.X, ALU.add).then_inc(red_done[u], 1)
                    dve.wait_ge(red_done[u], i + 1)
                    to = scores[:, bass.ds(2 * g, 2), :]
                    nc.vector.tensor_tensor(to, to, red[:, :, :], ALU.add)

            for s in range(3):
                make_pick(s, 0)
            iteration(0)
            with dve.Fori(1, ITERS) as i:
                iteration(i)


def softmax_numerators(nc, t, scores, newseg_d, mlp_d):
    ctx, sb, ps, sem = phase(nc)
    PIECES = 4
    PL = ROW_E // PIECES
    PAIRS = ROW_GROUPS // 2
    SPLITS = [2, 6]
    MLP_PIECES = [(0, 10), (10, 26), (26, ROW_GROUPS)]
    with ctx:
        sT = sb("sT", [P, ROW_GROUPS, P, 2])
        mx = sb("mx", [P, ROW_E])
        pen = sb("pen", [P, 2, PL], BF16)
        stage = sb("stage", [P, 2, 4, P])
        line = sb("line", [1, 4, P])
        carry = sb("carry", [P, 2])
        turned = [ps(f"sturn{i}", [P, 512]) for i in range(2)]
        small = ps("small", [P, 512])
        small2 = ps("small2", [P, 512])
        stage_ready = sem("stage_ready", 2)
        turned_ready = sem("sturned_ready", 2)
        turned_taken = sem("sturned_taken", 2)
        back_staged = sem("back_staged", 2)
        back_turned = sem("back_turned", 2)
        back_taken = sem("back_taken", 2)
        pen_in = sem("pen_in", 2)
        mlp_in = sem("mlp_in", 3)
        scanned = sem("scanned")
        line_ready = sem("line_ready")
        small_ready = sem("small_ready")
        link = sem("mlink")
        shifted = sem("shifted")
        block = ctx.enter_context(nc.Block())
        by_j = scores[:, :, :].rearrange("p (q j k) h -> p q j k h", q=ROWS, j=ROW_GROUPS)
        flat = sT[:, :, :, :].rearrange("r j p k -> r (j p k)")
        passes = [("f", range(PIECES)), ("f", range(PIECES)), ("b", range(PIECES - 1, -1, -1)), ("b", range(PIECES - 1, -1, -1))]
        plan = [(n, way, c) for n, (way, order) in enumerate(passes) for c in order]

        def pairs_loop(eng, body, start=0, stop=None):
            if start == 0:
                body(0, 0, 0)
            steps = (PAIRS - 1) // 2
            with eng.Fori(start, steps if stop is None else stop) as i:
                body(2 * i + 1, 1, i)
                body(2 * i + 2, 0, i + 1)
            if stop is None:
                body(PAIRS - 1, 1, steps)
                body(PAIRS, 0, steps + 1, w=ROW_GROUPS - 2 * PAIRS)

        @block.sync
        def _(sp):
            by_row = mlp_d.rearrange("(q j h) e -> q h j e", q=ROWS, h=H)
            for i, (a, b) in enumerate(MLP_PIECES):
                for q in range(ROWS):
                    sp.dma_start(sT[q * H:(q + 1) * H, a:b, :, :].rearrange("r j p k -> r j (p k)"),
                                 by_row[q:q + 1, :, a:b, :].rearrange("q h j e -> (q h) j e")).then_inc(mlp_in[i], 16)
            for m, (n, way, c) in enumerate(plan):
                if m >= 2:
                    sp.wait_ge(scanned, m - 1)
                past = 0 if way == "f" else 1
                rows = newseg_d[past:past + EPAD].rearrange("(q e) -> q e", q=ROWS)[:, c * PL:(c + 1) * PL]
                for h in range(H):
                    sp.dma_start(pen[h::H, m % 2, :], rows).then_inc(pen_in[m % 2], 16)

        @block.gpsimd
        def _(pool):
            for i in range(PIECES):
                c = plan[(len(passes) - 1) * PIECES + i][2]
                piece = flat[:, c * PL:(c + 1) * PL]
                pool.wait_ge(scanned, (len(passes) - 1) * PIECES + i + 1)
                pool.tensor_tensor(piece, piece, mx[:, c * PL:(c + 1) * PL], ALU.subtract).then_inc(shifted, 1)

        @block.scalar
        def _(act):
            def stage_in(b, s, n, w=2):
                wait(act, turned_ready[s], n)
                nc.scalar.activation(stage[:, s, 0:2 * w, :].rearrange("p c (q h) -> p c q h", h=H),
                                     by_j[:, :, bass.ds(2 * b, w), :, :].rearrange("p q j k h -> p (j k) q h"),
                                     ACT.Copy).then_inc(stage_ready[s], 1)

            pairs_loop(act, stage_in)

            def stage_back(b, s, n, w=2):
                wait(act, back_turned[s], n)
                nc.scalar.activation(stage[:, s, 0:2 * w, :].rearrange("r (j k) p -> r j k p", k=2),
                                     sT[:, bass.ds(2 * b, w), :, :].rearrange("r j p k -> r j k p"),
                                     ACT.Exp).then_inc(back_staged[s], 1)

            act.wait_ge(shifted, PIECES)
            pairs_loop(act, stage_back)

        @block.tensor
        def _(pe):
            def turn(b, s, n, w=2):
                pe.wait_ge(stage_ready[s], n + 1)
                wait(pe, turned_taken[s], n)
                for c in range(2 * w):
                    last = nc.tensor.transpose(turned[s][:, c * P:(c + 1) * P], stage[:, s, c, :], t["ident"][:, :])
                last.then_inc(turned_ready[s], 1)

            pairs_loop(pe, turn)
            for way in range(2):
                pe.wait_ge(line_ready, 3 * way + 1)
                nc.tensor.transpose(small[0:1, 0:P], carry[:, 0:1], t["ident"][:, :]).then_inc(small_ready, 1)
                pe.wait_ge(line_ready, 3 * way + 2)
                nc.tensor.transpose(small2[:, 0:1], line[:, 3, :], t["ident"][0:1, 0:1]).then_inc(small_ready, 1)

            def turn_back(b, s, n, w=2):
                pe.wait_ge(back_staged[s], n + 1)
                wait(pe, back_taken[s], n)
                for c in range(2 * w):
                    last = nc.tensor.transpose(turned[s][:, c * P:(c + 1) * P], stage[:, s, c, :], t["ident"][:, :])
                last.then_inc(back_turned[s], 1)

            pairs_loop(pe, turn_back)

        @block.vector
        def _(dve):
            def take(b, s, n, w=2):
                dve.wait_ge(turned_ready[s], n + 1)
                to = sT[:, bass.ds(2 * b, w), :, :].rearrange("r j p k -> r j k p")
                nc.vector.tensor_tensor(to, to, turned[s][:, 0:2 * w * P].rearrange("r (j k p) -> r j k p", k=2, p=P),
                                        ALU.add).then_inc(turned_taken[s], 1)

            for i in range(3):
                dve.wait_ge(mlp_in[i], 16 * ROWS)
                pairs_loop(dve, take, ([0] + SPLITS)[i], (SPLITS + [None])[i])
            dve.wait_ge(turned_taken[0], PAIRS // 2 + 1)
            dve.wait_ge(turned_taken[1], PAIRS // 2)
            cnt = [0]

            def done(ins):
                cnt[0] += 1
                ins.then_inc(link, 1)
                dve.wait_ge(link, cnt[0])

            for m, (n, way, c) in enumerate(plan):
                a, b = c * PL, (c + 1) * PL
                dve.wait_ge(pen_in[m % 2], 16 * H * (m // 2 + 1))
                if m:
                    dve.wait_ge(scanned, m)
                first = c == (0 if way == "f" else PIECES - 1)
                if way == "f":
                    init = (-BIG if n == 0 else carry[:, 1:2]) if first else mx[:, a - 1:a]
                    nc.vector.tensor_tensor_scan(mx[:, a:b], pen[:, m % 2, :], flat[:, a:b] if n == 0 else mx[:, a:b], init,
                                                 ALU.add, ALU.max).then_inc(scanned, 1)
                else:
                    init = (-BIG if n == 2 else carry[:, 1:2]) if first else mx[:, b:b + 1]
                    nc.vector.tensor_tensor_scan(mx[:, a:b][:, ::-1], pen[:, m % 2, :][:, ::-1], mx[:, a:b][:, ::-1], init,
                                                 ALU.add, ALU.max).then_inc(scanned, 1)
                if m % PIECES == PIECES - 1 and n in (0, 2):
                    w = 0 if n == 0 else 1
                    edge = mx[:, ROW_E - 1:ROW_E] if n == 0 else mx[:, 0:1]
                    dve.wait_ge(scanned, m + 1)
                    nc.vector.tensor_copy(carry[:, 0:1], edge).then_inc(line_ready, 1)
                    dve.wait_ge(small_ready, 2 * w + 1)
                    done(nc.vector.tensor_copy(line[:, 0, :].rearrange("a (h q) -> a h q", h=H),
                                               small[0:1, 0:P].rearrange("a (q h) -> a h q", h=H)))
                    pens = t["chain"][:, w, :, :].rearrange("a h q -> a (h q)")
                    step = 1 if n == 0 else -1
                    done(nc.vector.tensor_tensor_scan(line[:, 1, ::step], pens[:, ::step], line[:, 0, ::step], -BIG, ALU.add, ALU.max))
                    done(nc.vector.memset(line[:, 3, :], -BIG))
                    by_q = line[:, 3, :].rearrange("a (q h) -> a h q", h=H)
                    got = line[:, 1, :].rearrange("a (h q) -> a h q", h=H)
                    if n == 0:
                        nc.vector.tensor_copy(by_q[:, :, 1:ROWS], got[:, :, 0:ROWS - 1]).then_inc(line_ready, 1)
                    else:
                        nc.vector.tensor_copy(by_q[:, :, 0:ROWS - 1], got[:, :, 1:ROWS]).then_inc(line_ready, 1)
                    dve.wait_ge(small_ready, 2 * w + 2)
                    nc.vector.tensor_copy(carry[:, 1:2], small2[:, 0:1]).then_inc(line_ready, 1)
                    dve.wait_ge(line_ready, 3 * w + 3)

            def take_back(b, s, n, w=2):
                dve.wait_ge(back_turned[s], n + 1)
                nc.vector.tensor_copy(by_j[:, :, bass.ds(2 * b, w), :, :].rearrange("p q j k h -> p (j k) q h"),
                                      turned[s][:, 0:2 * w * P].rearrange("p (c q h) -> p c q h", c=2 * w, h=H)).then_inc(back_taken[s], 1)

            pairs_loop(dve, take_back)


def edge_sums(nc, t, name, table, width, index, acc, weigh, weigh_engine, extra=None):
    ctx, sb, ps, sem = phase(nc)
    with ctx:
        onehot = sb(name + "oh", [P, U, 2, P])
        idx = sb(name + "idx", [P, U, 2], I32)
        rows = sb(name + "rows", [P, U, 2, width])
        wrows = sb(name + "wrows", [P, U, 2, width])
        sums = [ps(f"{name}sums{i}", [P, 512]) for i in range(U)]
        onehot_ready = sem(name + "oh_ready", U)
        idx_ready = sem(name + "idx_ready", U)
        gathered = sem(name + "gathered", U)
        weighed = sem(name + "weighed", U)
        summed = sem(name + "summed", U)
        added = sem(name + "added", U)
        cleared = sem(name + "cleared")
        pool_go = sem(name + "pool_go")
        block = ctx.enter_context(nc.Block())

        def iterations(eng, body):
            body(0)
            with eng.Fori(1, ITERS) as i:
                body(i)

        @block.gpsimd
        def _(pool):
            def body(i):
                for u in range(U):
                    wait(pool, weighed[u], i)
                    hold(pool, idx_ready[u], i + 1, pool_go)
                    for k in range(2):
                        pool.indirect_dma_start(rows[:, u, k, :], None, table[:, :],
                                                bass.IndirectOffsetOnAxis(idx[:, u, k:k + 1], 0)).then_inc(gathered[u], 16)

            iterations(pool, body)

        def do_weigh(eng, i, u, s):
            eng.wait_ge(gathered[u], 32 * (i + 1))
            wait(eng, summed[u], i)
            weigh(wrows[:, u, :, :], rows[:, u, :, :], s).then_inc(weighed[u], 1)

        @block.scalar
        def _(act):
            def next_idx(i, u, n):
                wait(act, gathered[u], 32 * n)
                s = U * i + u
                nc.scalar.activation(idx[:, u, :], index[:, bass.ds(2 * s, 2)], ACT.Copy).then_inc(idx_ready[u], 1)

            def body(i):
                for u in range(U):
                    if weigh_engine == "scalar":
                        do_weigh(act, i, u, U * i + u)
                    next_idx(i + 1, u, i + 1)

            for u in range(U):
                next_idx(0, u, 0)
            iterations(act, body)

        @block.tensor
        def _(pe):
            def body(i):
                for u in range(U):
                    pe.wait_ge(onehot_ready[u], i + 1)
                    pe.wait_ge(weighed[u], i + 1)
                    wait(pe, added[u], i)
                    for k in range(2):
                        last = nc.tensor.matmul(sums[u][:, 0:width], onehot[:, u, k, :], wrows[:, u, k, :],
                                                start=(k == 0), stop=(k == 1))
                    last.then_inc(summed[u], 1)

            iterations(pe, body)

        @block.vector
        def _(dve):
            def prepare(s, u, i):
                wait(dve, summed[u], i)
                for k in range(2):
                    last = nc.vector.tensor_scalar(onehot[:, u, k, :], t["iota"][:, :], t["dst"][:, bass.ds(2 * s + k, 1)],
                                                   None, ALU.is_equal)
                last.then_inc(onehot_ready[u], 1)
                if weigh_engine == "vector":
                    do_weigh(dve, i, u, s)

            def add(s, u, i):
                b = block_of(nc, dve, t, s)
                dve.wait_ge(summed[u], i + 1)
                if u > 0:
                    dve.wait_ge(added[u - 1], i + 1)
                else:
                    wait(dve, added[U - 1], i)
                to = acc[:, bass.ds(b, 1), :]
                nc.vector.tensor_tensor(to, to, sums[u][:, 0:width].unsqueeze(1), ALU.add).then_inc(added[u], 1)

            nc.vector.memset(acc[:, :, :], 0.0).then_inc(cleared, 1)
            dve.wait_ge(cleared, 1)
            for u in range(U):
                prepare(u, u, 0)
                if u:
                    add(u - 1, u - 1, 0)
            with dve.Fori(1, ITERS) as i:
                for u in range(U):
                    prepare(U * i + u, u, i)
                    if u:
                        add(U * i + u - 1, u - 1, i)
                    else:
                        add(U * i - 1, U - 1, i - 1)
            add(STEPS - 1, U - 1, ITERS - 1)
            dve.wait_ge(added[U - 1], ITERS)


def weighted_sums(nc, t, scores, att, v_d):
    def weigh(out, rows, s):
        g = group_of(nc, nc.vector, t, s)
        return nc.vector.tensor_tensor(
            out.rearrange("p k (h c) -> p (k h) c", h=H), rows.rearrange("p k (h c) -> p (k h) c", h=H),
            scores[:, bass.ds(2 * g, 2), :].rearrange("p k h -> p (k h)").unsqueeze(2).to_broadcast([P, 2 * H, HD1]), ALU.mult)

    edge_sums(nc, t, "v_", v_d, H * HD1, t["src"], att[:, :, :, :].rearrange("p b h c -> p b (h c)"), weigh, "vector")


def messages(nc, t, att, x1, x, wo, bo, rel_w, gate_w, msg_d):
    ctx, sb, ps, sem = phase(nc)
    QUARTERS = 4
    with ctx:
        wos = sb("wos", [P, 2, D])
        bos = sb("bos", [P, D])
        wr = sb("wr", [P, 2, RELS, D])
        gw = sb("gw", [P, 2, RELS])
        xin = sb("x_res", [P, 2, D])
        den = sb("den", [P, H, 1])
        rden = sb("rden", [P, H, 1])
        o = sb("o", [P, H, HD])
        oT = sb("oT", [P, 2, P])
        stats = sb("stats1", [P, 6])
        mv = sb("mv1", [P, 2])
        std = sb("std1", [P, 1])
        rstd = sb("rstd1", [P, 1])
        xn = sb("xn1", [P, D])
        hT = sb("h1T", [P, 2, 2, P])
        gate = sb("gate", [P, 2, RELS])
        msg = sb("msg", [P, RELS, D])
        p_oT = ps("p_oT", [P, 512])
        p_o = ps("p_o", [P, 512])
        p_xT = ps("p_xT", [P, 512])
        p_g = ps("p_g", [P, 512])
        p_m = [ps(f"p_m{i}", [P, 512]) for i in range(4)]
        dve_go = sem("dve_go1")
        w_in = sem("wr_in")
        x_in = sem("xr_in", 2)
        xb_ready = sem("xb_ready", 2)
        den_link = sem("den_link")
        o_ready = sem("o_ready")
        oT_done = sem("oT_done")
        oT_ready = sem("oT_ready")
        wo_done = sem("wo_done")
        x1_ready = sem("x1_ready")
        ln_link = sem("ln_link")
        std_ready = sem("std1_ready")
        xn_ready = sem("xn1_ready")
        xT_done = sem("xT_done")
        hT_ready = sem("h1T_ready")
        gate_done = sem("gate_done")
        gate_ready = sem("gate_ready")
        msg_done = sem("msg_done", 4)
        msg_taken = sem("msg_taken", 4)
        msg_stored = sem("msg_stored", QUARTERS)
        block = ctx.enter_context(nc.Block())
        table = msg_d.rearrange("(r n) d -> n r d", r=RELS)

        def all_blocks(eng, front, back):
            front(0, 0, 0)
            back(0, 0, 0, True)
            with eng.Fori(0, (BLOCKS - 3) // 2) as i:
                back(2 * i + 1, 1, i, True)
                back(2 * i + 2, 0, i + 1, True)
            back(BLOCKS - 2, 1, (BLOCKS - 3) // 2, True)
            back(BLOCKS - 1, 0, (BLOCKS - 1) // 2, False)

        @block.sync
        def _(sp):
            sp.dma_start(wos[:, :, :], wo.rearrange("(c p) n -> p c n", p=P)).then_inc(w_in, 16)
            sp.dma_start(bos[:, :], bo.rearrange("(a n) -> a n", a=1).to_broadcast([P, D])).then_inc(w_in, 16)
            for c in range(2):
                sp.dma_start(wr[:, c, :, :], rel_w[:, c * P:(c + 1) * P, :].rearrange("r p n -> p r n")).then_inc(w_in, 16)
            with nc.allow_non_contiguous_dma(reason="4096 numbers"):
                for c in range(2):
                    sp.dma_start(gw[:, c, :], gate_w[:, c * P:(c + 1) * P, :].rearrange("r p a -> p (r a)")).then_inc(w_in, 16)

            def load(b, s, n, rows=P):
                wait(sp, x1_ready, b - 1)
                sp.dma_start(xin[0:rows, s, :], x[bass.ds(b * P, rows), :]).then_inc(x_in[s], 16)

            def store(b):
                for q in range(QUARTERS):
                    use = 2 * b + q // 2
                    sp.wait_ge(msg_taken[2 * (q % 2)], use + 1)
                    sp.wait_ge(msg_taken[2 * (q % 2) + 1], use + 1)
                    sp.dma_start(table[bass.ds(b * P, P), 4 * q:4 * q + 4, :], msg[:, 4 * q:4 * q + 4, :]).then_inc(msg_stored[q], 16)

            load(0, 0, 0)
            load(1, 1, 0)
            store(0)
            with sp.Fori(0, (BLOCKS - 3) // 2) as i:
                load(2 * i + 2, 0, i + 1)
                store(2 * i + 1)
                load(2 * i + 3, 1, i + 1)
                store(2 * i + 2)
            load(BLOCKS - 1, 0, BLOCKS // 2, LAST_ROWS)
            store(BLOCKS - 2)
            store(BLOCKS - 1)
            for q in range(QUARTERS):
                sp.wait_ge(msg_stored[q], 16 * BLOCKS)

        @block.gpsimd
        def _(pool):
            pool.wait_ge(w_in, 96)

            def add_bias(b, s, n):
                pool.wait_ge(x_in[s], 16 * (n + 1))
                nc.gpsimd.tensor_tensor(xin[:, s, :], xin[:, s, :], bos[:, :], ALU.add).then_inc(xb_ready[s], 1)

            blocks_loop(pool, add_bias)

        def front_of(pieces):
            def front(b, s, n):
                for piece in pieces:
                    piece(b, s, n)
            return front

        def next_of(b, s, n):
            return (b + 1, 1 - s, n if s == 0 else n + 1)

        @block.vector
        def _(dve):
            def normalise(b, s, n):
                a = att[:, bass.ds(b, 1), :, :].rearrange("p b h c -> p (b h) c")
                nc.vector.tensor_scalar(den[:, :, :], a[:, :, HD:HD1], 1.0e-30, None, ALU.max).then_inc(den_link, 1)
                dve.wait_ge(den_link, 2 * b + 1)
                nc.vector.reciprocal(rden[:, :, :], den[:, :, :]).then_inc(den_link, 1)
                dve.wait_ge(den_link, 2 * b + 2)
                nc.vector.tensor_tensor(o[:, :, :], a[:, :, 0:HD], rden[:, :, :].to_broadcast([P, H, HD]), ALU.mult).then_inc(o_ready, 1)

            def residual(b, s, n):
                to = x1[:, bass.ds(b, 1), :].rearrange("p b d -> p (b d)")
                dve.wait_ge(wo_done, b + 1)
                dve.wait_ge(xb_ready[s], n + 1)
                nc.vector.tensor_tensor(to, p_o[:, 0:D], xin[:, s, :], ALU.add).then_inc(x1_ready, 1)
                hold(dve, x1_ready, b + 1, dve_go)
                nc.vector.bn_stats(stats[:, :], to).then_inc(ln_link, 1)
                hold(dve, ln_link, 3 * b + 1, dve_go)
                nc.vector.bn_aggr(mv[:, :], stats[:, :]).then_inc(ln_link, 1)

            def layer_norm(b, s, n):
                to = x1[:, bass.ds(b, 1), :].rearrange("p b d -> p (b d)")
                dve.wait_ge(std_ready, b + 1)
                nc.vector.reciprocal(rstd[:, :], std[:, :]).then_inc(ln_link, 1)
                dve.wait_ge(ln_link, 3 * b + 3)
                nc.vector.tensor_scalar(xn[:, :], to, mv[:, 0:1], rstd[:, :], ALU.subtract, ALU.mult).then_inc(xn_ready, 1)

            def take(b, s, c):
                use = 2 * b + c // 4
                dve.wait_ge(msg_done[c % 4], use + 1)
                wait(dve, msg_stored[c // 2], 16 * b)
                for r in range(2):
                    last = nc.vector.tensor_scalar(msg[:, 2 * c + r, :], p_m[c % 4][:, r * D:(r + 1) * D],
                                                   gate[:, s, 2 * c + r:2 * c + r + 1], None, ALU.mult)
                last.then_inc(msg_taken[c % 4], 1)

            def back(b, s, n, more):
                if more:
                    normalise(*next_of(b, s, n))
                dve.wait_ge(gate_ready, b + 1)
                take(b, s, 1)
                if more:
                    residual(*next_of(b, s, n))
                take(b, s, 3)
                if more:
                    layer_norm(*next_of(b, s, n))
                take(b, s, 5)
                take(b, s, 7)

            all_blocks(dve, front_of([normalise, residual, layer_norm]), back)

        @block.scalar
        def _(act):
            def take_oT(b, s, n):
                act.wait_ge(oT_done, b + 1)
                nc.scalar.activation(oT[:, :, :], p_oT[:, 0:2 * P].rearrange("p (c n) -> p c n", c=2), ACT.Copy).then_inc(oT_ready, 1)

            def root(b, s, n):
                act.wait_ge(ln_link, 3 * b + 2)
                nc.scalar.activation(std[:, :], mv[:, 1:2], ACT.Sqrt, bias=t["eps"][:, 0:1]).then_inc(std_ready, 1)

            def take_hT(b, s, n):
                act.wait_ge(xT_done, b + 1)
                nc.scalar.activation(hT[:, s, :, :], p_xT[:, 0:2 * P].rearrange("p (c n) -> p c n", c=2), ACT.Relu).then_inc(hT_ready, 1)

            def gates(b, s, n):
                act.wait_ge(gate_done, b + 1)
                nc.scalar.activation(gate[:, s, :], p_g[:, 0:RELS], ACT.Sigmoid).then_inc(gate_ready, 1)

            def take(b, s, c):
                use = 2 * b + c // 4
                act.wait_ge(msg_done[c % 4], use + 1)
                wait(act, msg_stored[c // 2], 16 * b)
                for r in range(2):
                    last = nc.scalar.activation(msg[:, 2 * c + r, :], p_m[c % 4][:, r * D:(r + 1) * D], ACT.Copy,
                                                scale=gate[:, s, 2 * c + r:2 * c + r + 1])
                last.then_inc(msg_taken[c % 4], 1)

            def back(b, s, n, more):
                act.wait_ge(gate_ready, b + 1)
                if more:
                    take_oT(*next_of(b, s, n))
                take(b, s, 0)
                take(b, s, 2)
                if more:
                    root(*next_of(b, s, n))
                take(b, s, 4)
                if more:
                    take_hT(*next_of(b, s, n))
                take(b, s, 6)
                if more:
                    gates(*next_of(b, s, n))

            all_blocks(act, front_of([take_oT, root, take_hT, gates]), back)

        @block.tensor
        def _(pe):
            pe.wait_ge(w_in, 96)

            def turn_o(b, s, n):
                pe.wait_ge(o_ready, b + 1)
                flat = o[:, :, :].rearrange("p h c -> p (h c)")
                for c in range(2):
                    last = nc.tensor.transpose(p_oT[:, c * P:(c + 1) * P], flat[:, c * P:(c + 1) * P], t["ident"][:, :])
                last.then_inc(oT_done, 1)

            def project(b, s, n):
                pe.wait_ge(oT_ready, b + 1)
                for c in range(2):
                    last = nc.tensor.matmul(p_o[:, 0:D], oT[:, c, :], wos[:, c, :], start=(c == 0), stop=(c == 1))
                last.then_inc(wo_done, 1)

            def turn_x(b, s, n):
                pe.wait_ge(xn_ready, b + 1)
                for c in range(2):
                    last = nc.tensor.transpose(p_xT[:, c * P:(c + 1) * P], xn[:, c * P:(c + 1) * P], t["ident"][:, :])
                last.then_inc(xT_done, 1)

            def gates(b, s, n):
                pe.wait_ge(hT_ready, b + 1)
                for c in range(2):
                    last = nc.tensor.matmul(p_g[:, 0:RELS], hT[:, s, c, :], gw[:, c, :], start=(c == 0), stop=(c == 1))
                last.then_inc(gate_done, 1)

            def relations(b, s, c):
                use = 2 * b + c // 4
                wait(pe, msg_taken[c % 4], use)
                for half in range(2):
                    last = nc.tensor.matmul(p_m[c % 4][:, :], hT[:, s, half, :], wr[:, half, 2 * c:2 * c + 2, :],
                                            start=(half == 0), stop=(half == 1))
                last.then_inc(msg_done[c % 4], 1)

            def back(b, s, n, more):
                relations(b, s, 0)
                if more:
                    turn_o(*next_of(b, s, n))
                relations(b, s, 1)
                if more:
                    project(*next_of(b, s, n))
                relations(b, s, 2)
                relations(b, s, 3)
                relations(b, s, 4)
                if more:
                    turn_x(*next_of(b, s, n))
                relations(b, s, 5)
                relations(b, s, 6)
                if more:
                    gates(*next_of(b, s, n))
                relations(b, s, 7)

            all_blocks(pe, front_of([turn_o, project, turn_x, gates]), back)


def message_sums(nc, t, x1, msg_d, out):
    with nc.sbuf_tensor("agg", [P, BLOCKS, D], F32) as agg:
        def weigh(o, rows, s):
            for k in range(2):
                last = nc.scalar.activation(o[:, k, :], rows[:, k, :], ACT.Copy, scale=t["norm"][:, bass.ds(2 * s + k, 1)])
            return last

        edge_sums(nc, t, "m_", msg_d, D, t["rel"], agg[:, :, :], weigh, "scalar")

        ctx, sb, ps, sem = phase(nc)
        PARTS = 7
        W = BLOCKS // PARTS
        with ctx:
            out_ready = sem("out_ready")
            out_stored = sem("out_stored")
            block = ctx.enter_context(nc.Block())

            @block.vector
            def _(dve):
                for c in range(PARTS):
                    a = slice(c * W, (c + 1) * W)
                    nc.vector.scalar_tensor_tensor(out=agg[:, a, :], in0=agg[:, a, :], scalar=0.0, in1=x1[:, a, :],
                                                   op0=ALU.max, op1=ALU.add).then_inc(out_ready, 1)

            @block.sync
            def _(sp):
                whole = out[0:(BLOCKS - 1) * P, :].rearrange("(b p) d -> p b d", p=P)
                for c in range(PARTS):
                    a, b = c * W, min((c + 1) * W, BLOCKS - 1)
                    sp.wait_ge(out_ready, c + 1)
                    sp.dma_start(whole[:, a:b, :], agg[:, a:b, :]).then_inc(out_stored, 16)
                sp.dma_start(out[(BLOCKS - 1) * P:N, :], agg[0:LAST_ROWS, BLOCKS - 1, :]).then_inc(out_stored, 16)
                sp.wait_ge(out_stored, 16 * (PARTS + 1))


_INS = ['x', 'src', 'dst', 'edge_attr_64', 'edge_type_16', 'edge_weight1', 'L0_gnn_Wq', 'L0_gnn_Wk', 'L0_gnn_Wv',
        'L0_gnn_W1', 'L0_gnn_b1', 'L0_gnn_W2', 'L0_gnn_b2', 'L0_gnn_Wo', 'L0_gnn_bo', 'L1_gnn_weight', 'L1_gnn_gate_weight']


def kernel(**inputs):
    import numpy as _np
    import concourse.bacc as _bacc
    from concourse import mybir as _mybir
    from concourse.bass_utils import run_bass_kernel_spmd as _run

    nc = _bacc.Bacc("TRN2", target_bir_lowering=False, num_devices=1)
    arrays, args = {}, []
    for name in _INS:
        a = _np.ascontiguousarray(inputs[name])
        arrays[f"in_{name}_dram"] = a
        args.append(nc.dram_tensor(f"in_{name}_dram", a.shape, _mybir.dt.from_np(a.dtype), kind="ExternalInput").ap())
    args.append(nc.dram_tensor("out_0_dram", (N, D), F32, kind="ExternalOutput").ap())
    build(nc, *args)
    r = _run(nc, [arrays], core_ids=[0])
    return r.results[0]["out_0_dram"]
```
